# Optimizing a Trainium2 kernel written in Bass

```python
import numpy as np
import jax
import jax.numpy as jnp

def _softmax(x, axis=-1):
    return jax.nn.softmax(x, axis=axis)

def _gelu(x):
    return jax.nn.gelu(x, approximate=True)

def _silu(x):
    return jax.nn.silu(x)

def _sigmoid(x):
    return jax.nn.sigmoid(x)

def _layernorm(x, axis=-1, eps=1e-05):
    m = jnp.mean(x, axis=axis, keepdims=True)
    v = jnp.var(x, axis=axis, keepdims=True)
    return (x - m) / jnp.sqrt(v + eps)

def _scatter_add(tgt, idx, src, axis=0):
    return tgt.at[idx].add(src)

def _segment_sum(src, seg, n):
    return jax.ops.segment_sum(src, seg, n)
kernel_name = 'mk_flamingo_gated_d2_seqx_r4_2f59e6'

def setup_inputs(seed: int=0):
    np.random.seed(seed)
    _w = jnp.asarray

    def _rec_inputs():
        import jax
        import jax.numpy as jnp
        _rk = jax.random.key(seed)
        x = -0.0003929 + 0.9999 * jax.random.normal(jax.random.fold_in(_rk, 1), (8, 256, 1024), jnp.float32)
        _lenS = 256 - jax.random.randint(jax.random.fold_in(_rk, 7), (8,), 0, max(1, 256 // 4) + 1, jnp.int32)
        _lenS2 = 256 - jax.random.randint(jax.random.fold_in(_rk, 8), (8,), 0, max(1, 256 // 4) + 1, jnp.int32)
        _ctx_4096P = jax.random.normal(jax.random.fold_in(_rk, 11), (8, 16, 1024), jnp.float32)
        _ctx_4096c = jax.random.dirichlet(jax.random.fold_in(_rk, 511), 0.3 * jnp.ones((16,), jnp.float32), (8, 256))
        _ctx_4096t = jnp.einsum('bsk,bkd->bsd', _ctx_4096c, _ctx_4096P)
        _ctx_4096t = _ctx_4096t * jax.lax.rsqrt(jnp.mean(jnp.square(_ctx_4096t)) + 1e-12) * 0.953939
        ctx_4096 = 2.81802e-05 + 1.00001 * (_ctx_4096t + 0.3 * jax.random.normal(jax.random.fold_in(_rk, 611), (8, 256, 1024), jnp.float32))
        _g = jax.random.normal(jax.random.fold_in(_rk, 9001), (2, 2), jnp.float32)
        _g = jnp.sign(_g) * jnp.maximum(jnp.abs(_g), 1.0) + (_g == 0) * 1.0
        g_xattn = _g[0]
        g_ffn = _g[1]
        return (x, ctx_4096, g_xattn, g_ffn)
    x, ctx_4096, g_xattn, g_ffn = _rec_inputs()

    def _L0_xattn_setup():
        import jax, jax.numpy as jnp
        import numpy as np
        EMB_DIM = 128
        HEADS = 8
        key = jax.random.key(seed)
        kq, kk, kv = jax.random.split(key, 3)
        B, C, N = (8, EMB_DIM, 1024)
        q = jax.random.normal(kq, (B, C, N), dtype=jnp.float32)
        k = jax.random.normal(kk, (B, C, N), dtype=jnp.float32)
        v = jax.random.normal(kv, (B, C, N), dtype=jnp.float32)
        return {'q': q, 'k': k, 'v': v}
    _L0_xattn_all = _L0_xattn_setup()
    _L0_xattn_in = {k: v for k, v in _L0_xattn_all.items() if k in ()}
    del _L0_xattn_all

    def _L0_ffn_setup():
        import jax, jax.numpy as jnp
        import numpy as np
        B, S, DM, DFF, R = (4, 256, 1024, 2752, 16)
        BLOCK = 64
        NF4 = jnp.array([-1.0, -0.6961928009986877, -0.5250730514526367, -0.39491748809814453, -0.28444138169288635, -0.18477343022823334, -0.09105003625154495, 0.0, 0.07958029955625534, 0.16093020141124725, 0.2461123019456863, 0.33791524171829224, 0.44070982933044434, 0.5626170039176941, 0.7229568362236023, 1.0], dtype=jnp.float32)

        def dequant4(codes, absmax):
            o, i = codes.shape
            w = NF4[codes].reshape(o, i // BLOCK, BLOCK) * absmax[:, :, None]
            return w.reshape(o, i)
        key = jax.random.key(seed)
        ks = jax.random.split(key, 16)
        x1 = jax.random.normal(ks[0], (B, S, DM), jnp.float32)

        def qw(k1, k2, o, i):
            codes = jax.random.randint(k1, (o, i), 0, 16, dtype=jnp.int32)
            absmax = jax.random.uniform(k2, (o, i // BLOCK), jnp.float32) * 0.02
            return (codes, absmax)
        g_codes, g_absmax = qw(ks[1], ks[2], DFF, DM)
        u_codes, u_absmax = qw(ks[3], ks[4], DFF, DM)
        d_codes, d_absmax = qw(ks[5], ks[6], DM, DFF)
        sc = 0.02
        g_lora_a = jax.random.normal(ks[7], (DM, R), jnp.float32) * sc
        g_lora_b = jax.random.normal(ks[8], (R, DFF), jnp.float32) * sc
        u_lora_a = jax.random.normal(ks[9], (DM, R), jnp.float32) * sc
        u_lora_b = jax.random.normal(ks[10], (R, DFF), jnp.float32) * sc
        d_lora_a = jax.random.normal(ks[11], (DFF, R), jnp.float32) * sc
        d_lora_b = jax.random.normal(ks[12], (R, DM), jnp.float32) * sc
        return dict(x1=x1, g_codes=g_codes, g_absmax=g_absmax, g_lora_a=g_lora_a, g_lora_b=g_lora_b, u_codes=u_codes, u_absmax=u_absmax, u_lora_a=u_lora_a, u_lora_b=u_lora_b, d_codes=d_codes, d_absmax=d_absmax, d_lora_a=d_lora_a, d_lora_b=d_lora_b)
    _L0_ffn_all = _L0_ffn_setup()
    _L0_ffn_in = {k: v for k, v in _L0_ffn_all.items() if k in ('g_codes', 'g_absmax', 'g_lora_a', 'g_lora_b', 'u_codes', 'u_absmax', 'u_lora_a', 'u_lora_b', 'd_codes', 'd_absmax', 'd_lora_a', 'd_lora_b')}
    del _L0_ffn_all

    def _L1_xattn_setup():
        import jax, jax.numpy as jnp
        import numpy as np
        H = 8
        C = 2

        def _autocorrelation(Q, K, V):
            B, L, D = Q.shape
            d = D // H
            q = Q.reshape(B, L, H, d).transpose(0, 2, 1, 3)
            k = K.reshape(B, L, H, d).transpose(0, 2, 1, 3)
            v = V.reshape(B, L, H, d).transpose(0, 2, 1, 3)
            qf = jnp.fft.fft(q, axis=2)
            kf = jnp.fft.fft(k, axis=2)
            corr = jnp.fft.ifft(qf * jnp.conj(kf), axis=2).real
            topk = int(C * np.log(L))
            w, idx = jax.lax.top_k(corr.transpose(0, 1, 3, 2), topk)
            w = jax.nn.softmax(w, axis=-1)
            pos = jnp.arange(L)[:, None]
            out = jnp.zeros_like(v)
            for i in range(topk):
                g = jnp.minimum(idx[:, :, None, :, i] + pos, L - 1)
                out = out + w[:, :, None, :, i] * jnp.take_along_axis(v, g, axis=2)
            return out.transpose(0, 2, 1, 3).reshape(B, L, D)
        key = jax.random.key(seed)
        k1, k2, k3 = jax.random.split(key, 3)
        B, L, D = (16, 128, 1024)
        Q = jax.random.normal(k1, (B, L, D), dtype=jnp.float32)
        K = jax.random.normal(k2, (B, L, D), dtype=jnp.float32)
        V = jax.random.normal(k3, (B, L, D), dtype=jnp.float32)
        return {'Q': Q, 'K': K, 'V': V}
    _L1_xattn_all = _L1_xattn_setup()
    _L1_xattn_in = {k: v for k, v in _L1_xattn_all.items() if k in ()}
    del _L1_xattn_all

    def _L1_ffn_setup():
        import jax, jax.numpy as jnp
        import numpy as np
        B, S, DIN, DOUT, R = (2, 512, 1024, 1024, 32)
        key = jax.random.key(seed)
        k1, k2, k3, k4, k5 = jax.random.split(key, 5)
        std = 1.0 / np.sqrt(R)
        return {'x': jax.random.normal(k1, (B, S, DIN), dtype=jnp.float32), 'W': jax.random.normal(k2, (DOUT, DIN), dtype=jnp.float32) * 0.02, 'lora_A': jax.random.normal(k3, (R, DIN), dtype=jnp.float32) * std, 'lora_B': jax.random.normal(k4, (DOUT, R), dtype=jnp.float32) * 0.01, 'magnitude': jax.random.uniform(k5, (DOUT,), dtype=jnp.float32) + 0.5}
    _L1_ffn_all = _L1_ffn_setup()
    _L1_ffn_in = {k: v for k, v in _L1_ffn_all.items() if k in ('W', 'lora_A', 'lora_B', 'magnitude')}
    del _L1_ffn_all
    return {'x': x, 'ctx_4096': ctx_4096, 'g_xattn': g_xattn, 'g_ffn': g_ffn, 'L0_ffn_g_codes': _L0_ffn_in['g_codes'], 'L0_ffn_g_absmax': _L0_ffn_in['g_absmax'], 'L0_ffn_g_lora_a': _L0_ffn_in['g_lora_a'], 'L0_ffn_g_lora_b': _L0_ffn_in['g_lora_b'], 'L0_ffn_u_codes': _L0_ffn_in['u_codes'], 'L0_ffn_u_absmax': _L0_ffn_in['u_absmax'], 'L0_ffn_u_lora_a': _L0_ffn_in['u_lora_a'], 'L0_ffn_u_lora_b': _L0_ffn_in['u_lora_b'], 'L0_ffn_d_codes': _L0_ffn_in['d_codes'], 'L0_ffn_d_absmax': _L0_ffn_in['d_absmax'], 'L0_ffn_d_lora_a': _L0_ffn_in['d_lora_a'], 'L0_ffn_d_lora_b': _L0_ffn_in['d_lora_b'], 'L1_ffn_W': _L1_ffn_in['W'], 'L1_ffn_lora_A': _L1_ffn_in['lora_A'], 'L1_ffn_lora_B': _L1_ffn_in['lora_B'], 'L1_ffn_magnitude': _L1_ffn_in['magnitude']}

def reference(x, ctx_4096, g_xattn, g_ffn, L0_ffn_g_codes, L0_ffn_g_absmax, L0_ffn_g_lora_a, L0_ffn_g_lora_b, L0_ffn_u_codes, L0_ffn_u_absmax, L0_ffn_u_lora_a, L0_ffn_u_lora_b, L0_ffn_d_codes, L0_ffn_d_absmax, L0_ffn_d_lora_a, L0_ffn_d_lora_b, L1_ffn_W, L1_ffn_lora_A, L1_ffn_lora_B, L1_ffn_magnitude):
    import jax
    import jax.numpy as jnp

    def _L0_xattn_ref(q, k, v):
        import jax, jax.numpy as jnp
        import numpy as np
        EMB_DIM = 128
        HEADS = 8
        B, C, N = q.shape
        H = HEADS
        dh = C // H
        qh = q.transpose(0, 2, 1).reshape(B, N, H, dh)
        kh = k.transpose(0, 2, 1).reshape(B, N, H, dh)
        vh = v.transpose(0, 2, 1).reshape(B, N, H, dh)
        qh = jax.nn.softmax(qh, axis=3)
        kh = jax.nn.softmax(kh, axis=1)
        kvs = jnp.einsum('bnhd,bnhe->bhde', kh, vh)
        out = jnp.einsum('bnhd,bhde->bnhe', qh, kvs)
        return out.transpose(0, 2, 3, 1).reshape(B, C, N)

    def _L0_ffn_ref(x1, g_codes, g_absmax, g_lora_a, g_lora_b, u_codes, u_absmax, u_lora_a, u_lora_b, d_codes, d_absmax, d_lora_a, d_lora_b):
        import jax, jax.numpy as jnp
        import numpy as np
        B, S, DM, DFF, R = (4, 256, 1024, 2752, 16)
        BLOCK = 64
        NF4 = jnp.array([-1.0, -0.6961928009986877, -0.5250730514526367, -0.39491748809814453, -0.28444138169288635, -0.18477343022823334, -0.09105003625154495, 0.0, 0.07958029955625534, 0.16093020141124725, 0.2461123019456863, 0.33791524171829224, 0.44070982933044434, 0.5626170039176941, 0.7229568362236023, 1.0], dtype=jnp.float32)

        def dequant4(codes, absmax):
            o, i = codes.shape
            w = NF4[codes].reshape(o, i // BLOCK, BLOCK) * absmax[:, :, None]
            return w.reshape(o, i)
        Wg = dequant4(g_codes, g_absmax).T
        Wu = dequant4(u_codes, u_absmax).T
        Wd = dequant4(d_codes, d_absmax).T
        y1 = x1 @ Wg + x1 @ g_lora_a @ g_lora_b
        y2 = x1 @ Wu + x1 @ u_lora_a @ u_lora_b
        x3 = jax.nn.relu(y1) * y2
        y3 = x3 @ Wd + x3 @ d_lora_a @ d_lora_b
        return y3

    def _L1_xattn_ref(Q, K, V):
        import jax, jax.numpy as jnp
        import numpy as np
        H = 8
        C = 2

        def _autocorrelation(Q, K, V):
            B, L, D = Q.shape
            d = D // H
            q = Q.reshape(B, L, H, d).transpose(0, 2, 1, 3)
            k = K.reshape(B, L, H, d).transpose(0, 2, 1, 3)
            v = V.reshape(B, L, H, d).transpose(0, 2, 1, 3)
            qf = jnp.fft.fft(q, axis=2)
            kf = jnp.fft.fft(k, axis=2)
            corr = jnp.fft.ifft(qf * jnp.conj(kf), axis=2).real
            topk = int(C * np.log(L))
            w, idx = jax.lax.top_k(corr.transpose(0, 1, 3, 2), topk)
            w = jax.nn.softmax(w, axis=-1)
            pos = jnp.arange(L)[:, None]
            out = jnp.zeros_like(v)
            for i in range(topk):
                g = jnp.minimum(idx[:, :, None, :, i] + pos, L - 1)
                out = out + w[:, :, None, :, i] * jnp.take_along_axis(v, g, axis=2)
            return out.transpose(0, 2, 1, 3).reshape(B, L, D)
        return _autocorrelation(Q, K, V)

    def _L1_ffn_ref(x, W, lora_A, lora_B, magnitude):
        import jax, jax.numpy as jnp
        import numpy as np
        B, S, DIN, DOUT, R = (2, 512, 1024, 1024, 32)
        base = jnp.einsum('bsi,oi->bso', x, W)
        lora = jnp.einsum('bsr,or->bso', jnp.einsum('bsi,ri->bsr', x, lora_A), lora_B)
        eff_W = W + lora_B @ lora_A
        column_norm = jax.lax.stop_gradient(jnp.sqrt(jnp.sum(eff_W * eff_W, axis=1)))
        result = (base + lora) / column_norm[None, None, :]
        return result * magnitude[None, None, :]
    x = x + jnp.tanh(g_xattn[0]) * _L0_xattn_ref(_layernorm(x, axis=-1), ctx_4096, ctx_4096)
    x = x + jnp.tanh(g_ffn[0]) * _L0_ffn_ref(_layernorm(x, axis=-1), L0_ffn_g_codes, L0_ffn_g_absmax, L0_ffn_g_lora_a, L0_ffn_g_lora_b, L0_ffn_u_codes, L0_ffn_u_absmax, L0_ffn_u_lora_a, L0_ffn_u_lora_b, L0_ffn_d_codes, L0_ffn_d_absmax, L0_ffn_d_lora_a, L0_ffn_d_lora_b)
    x = x + jnp.tanh(g_xattn[1]) * _L1_xattn_ref(_layernorm(x, axis=-1), ctx_4096, ctx_4096)
    x = x + jnp.tanh(g_ffn[1]) * _L1_ffn_ref(_layernorm(x, axis=-1), L1_ffn_W, L1_ffn_lora_A, L1_ffn_lora_B, L1_ffn_magnitude)
    return x

_drawn_inputs = setup_inputs


def setup_inputs(seed=0):
    import zlib

    import numpy as np

    out = dict(_drawn_inputs(seed))
    spreads = {'g_ffn': (-1.0, 0.6)}
    factors = {'L0_ffn_g_absmax': 8.0,
     'L0_ffn_g_lora_a': 8.0,
     'L0_ffn_g_lora_b': 8.0,
     'L0_ffn_u_absmax': 8.0,
     'L0_ffn_u_lora_a': 8.0,
     'L0_ffn_u_lora_b': 8.0,
     'L0_ffn_d_absmax': 8.0,
     'L0_ffn_d_lora_a': 8.0,
     'L0_ffn_d_lora_b': 8.0,
     'L1_ffn_W': 2.999,
     'L1_ffn_lora_A': 6.048,
     'L1_ffn_lora_B': 5.907,
     'L1_ffn_magnitude': 8.0}
    for name, (base, spread) in spreads.items():
        noise = np.random.default_rng([zlib.crc32(name.encode()), seed]).standard_normal(out[name].shape)
        drawn = base * np.exp(spread * noise) if base else spread * noise
        out[name] = jnp.asarray(drawn.astype(out[name].dtype))
    for name, factor in factors.items():
        out[name] = (out[name] * factor).astype(out[name].dtype)
    return out
```

```python
from contextlib import ExitStack

import numpy as np

import concourse.bass as bass
from concourse import mybir

F32 = mybir.dt.float32
I32 = mybir.dt.int32
HALF = mybir.dt.bfloat16
FINE = mybir.dt.float16
ALU = mybir.AluOpType
ACT = mybir.ActivationFunctionType
AX = mybir.AxisListType

P = 128
B, L, D = 8, 256, 1024
TILES = B * L // P
KD = D // P
BANK = 512
EPS = 1e-5
DFF, R0 = 2752, 16
PAIR = 2 * P
PAIRS = -(-DFF // PAIR)
DFF_PAD = PAIRS * PAIR
QBLK = 64
HEADS0 = 8
ROWS0 = L // HEADS0
TOPK = int(2 * np.log(L))
R1 = 32
HALVES = 2
UNITS = 12
TB = B * L // BANK
BIG = 3.0e38
W_SCALE = 2.0 ** 12
LN_SCALE = 2.0 ** 6

NF4 = [-1.0, -0.6961928009986877, -0.5250730514526367, -0.39491748809814453, -0.28444138169288635,
       -0.18477343022823334, -0.09105003625154495, 0.0, 0.07958029955625534, 0.16093020141124725,
       0.2461123019456863, 0.33791524171829224, 0.44070982933044434, 0.5626170039176941,
       0.7229568362236023, 1.0]


def nf4_lines():
    out = []
    for j in (4, 5, 6, 7, 0, 1, 2, 3):
        s = NF4[2 * j + 1] - NF4[2 * j]
        o = NF4[2 * j] - 2 * j * s
        out.append((s, o) if j >= 4 else (-s, -o))
    return out


def pack_units():
    units = [(m, c, hf) for c in range(2) for m in (0, 1) for hf in range(2)]
    return units + [(2, c, hf) for c in range(2) for hf in range(2)]


FIRST = 1


def settler(passed):
    def settle(engine):
        engine.sem_inc(passed, 1)
    return settle


def phase_linear_attention(nc, io, res):
    settle = settler(res["passed"])
    X, xT_hi, xT_lo, ident, blk, tg, mhalf, gates = (
        res[k] for k in ("X", "xT_hi", "xT_lo", "ident", "blk", "tg", "mhalf", "gates"))
    x_d = io["x"].rearrange("b (h p) n -> b h p n", p=P)
    c_d = io["ctx"].rearrange("b (h p) n -> b h p n", p=P)
    with ExitStack() as ctx:
        def sb(name, shape, dt=F32):
            return [ctx.enter_context(nc.sbuf_tensor(f"{name}{h}", shape, dt)) for h in range(2)]

        def sem1(name):
            return ctx.enter_context(nc.semaphore(name))

        def sem(name):
            return [sem1(f"{name}{h}") for h in range(2)]

        c_in, eq, ek = sb("c_in", [P, D]), sb("eq", [P, D]), sb("ek", [P, D])
        ekT, cT, rS = sb("ekT", [P, D]), sb("cT", [P, D]), sb("rS", [P, D])
        kvm = sb("kvm", [P, P])
        st, mv, ve, rstd, nmr = sb("st", [P, 12]), sb("mv", [P, 2]), sb("ve", [P, 1]), sb("rstd", [P, 1]), sb("nmr", [P, 1])
        st2, mv2, ve2, rstd2, nmr2 = sb("st2", [P, 12]), sb("mv2", [P, 2]), sb("ve2", [P, 1]), sb("rstd2", [P, 1]), sb("nmr2", [P, 1])
        cm, ncm, ksum, rks = sb("cm", [P, 1]), sb("ncm", [P, 1]), sb("ksum", [P, 1]), sb("rks", [P, 1])
        xn = sb("xn", [P, D])
        psS = [ctx.enter_context(nc.psum_tensor(f"psS{h}", [P, D], F32)) for h in range(2)]
        psT = [ctx.enter_context(nc.psum_tensor(f"psT{h}", [P, D], F32)) for h in range(2)]

        const_in = ctx.enter_context(nc.semaphore("const_in"))
        gates_in = ctx.enter_context(nc.semaphore("gates_in"))
        mhalf_set = ctx.enter_context(nc.semaphore("mhalf_set"))
        tanh_done = ctx.enter_context(nc.semaphore("tanh_done"))
        x_in, ctx_in, rks_done, ekT_mm, kv_mm, out_mm, t1_done, xnT_mm, lo_done = (
            sem(n) for n in ("x_in", "ctx_in", "rks_done", "ekT_mm", "kv_mm", "out_mm", "t1_done", "xnT_mm", "lo_done"))
        stats_done, mv_done, ve_done, rstd_done, nmr_done = (sem1(n) for n in ("stats_done", "mv_done", "ve_done", "rstd_done", "nmr_done"))
        cmax_done, ncm_done, eq_done, ek_done, sums_done, rS_done = (sem1(n) for n in ("cmax_done", "ncm_done", "eq_done", "ek_done", "sums_done", "rS_done"))
        cT_mm, cT_done, ekT_done, kvm_done, x_done = (sem1(n) for n in ("cT_mm", "cT_done", "ekT_done", "kvm_done", "x_done"))
        stats2_done, mv2_done, ve2_done, rstd2_done, nmr2_done = (sem1(n) for n in ("stats2_done", "mv2_done", "ve2_done", "rstd2_done", "nmr2_done"))
        xn_done, hi_done = sem1("xn_done"), sem1("hi_done")

        with nc.Block() as block:
            @block.sync
            def _(sp):
                sp.dma_start(ident[:], io["ident"]).then_inc(const_in, 16)
                sp.dma_start(blk[:], io["blk"]).then_inc(const_in, 16)
                for n, g in enumerate(("g_xattn", "g_ffn")):
                    sp.dma_start(gates[:, 2 * n:2 * n + 2], io[g].partition_broadcast(P)).then_inc(gates_in, 16)
                with sp.Fori(0, B) as b:
                    for h in range(2):
                        sp.wait_ge(ekT_mm[h], b + FIRST)
                        sp.dma_start(X[:, b * 2 + h, :], x_d[b, h]).then_inc(x_in[h], 16)
                        sp.dma_start(c_in[h][:], c_d[b, h]).then_inc(ctx_in[h], 16)

            @block.gpsimd
            def _(pool):
                pool.memset(mhalf[:], -0.5).then_inc(mhalf_set, 1)
                pool.wait_ge(mhalf_set, 1)
                with pool.Fori(0, B) as b:
                    for mv_, ve_, rs_, mvd, ved, rsd in ((mv, ve, rstd, mv_done, ve_done, rstd_done),
                                                        (mv2, ve2, rstd2, mv2_done, ve2_done, rstd2_done)):
                        for h in range(2):
                            pool.wait_ge(mvd, 2 * b + h + 1)
                            settle(pool)
                            pool.tensor_scalar(ve_[h][:], mv_[h][:, 1:2], EPS, None, ALU.add).then_inc(ved, 1)
                            pool.wait_ge(ved, 2 * b + h + 1)
                            pool.tensor_tensor(rs_[h][:], ve_[h][:], mhalf[:], ALU.pow).then_inc(rsd, 1)

            @block.scalar
            def _(act):
                act.wait_ge(gates_in, 32)
                act.activation(tg[:], gates[:], ACT.Tanh).then_inc(tanh_done, 1)
                with act.Fori(0, B) as b:
                    for h in range(2):
                        act.wait_ge(nmr_done, 2 * b + h + 1)
                        act.wait_ge(out_mm[h], b + FIRST)
                        settle(act)
                        act.activation(eq[h][:], X[:, b * 2 + h, :], ACT.Exp, scale=rstd[h][:], bias=nmr[h][:]).then_inc(eq_done, 1)
                        act.wait_ge(ekT_mm[h], b + FIRST)
                        act.wait_ge(rks_done[h], b + FIRST)
                        act.wait_ge(ncm_done, 2 * b + h + 1)
                        act.activation(ek[h][:], c_in[h][:], ACT.Exp, bias=ncm[h][:], accum_out=ksum[h][:]).then_inc(ek_done, 1)
                    for h in range(2):
                        act.wait_ge(kv_mm[h], b + FIRST)
                        act.wait_ge(cT_mm, 2 * b + h + 1)
                        act.activation(cT[h][:], psT[h][:], ACT.Copy).then_inc(cT_done, 1)
                    for h in range(2):
                        act.wait_ge(xnT_mm[h], b + FIRST)
                        act.wait_ge(nmr2_done, 2 * b + h + 1)
                        settle(act)
                        act.activation(xn[h][:], X[:, b * 2 + h, :], ACT.Identity, scale=rstd2[h][:], bias=nmr2[h][:]).then_inc(xn_done, 1)
                    for h in range(2):
                        act.wait_ge(xnT_mm[h], b + 1 + FIRST)
                        settle(act)
                        act.activation(xT_hi[:, :, bass.ds(b * L + h * P, P)], psT[h][:].rearrange("p (k t) -> p k t", k=KD), ACT.Copy).then_inc(hi_done, 1)

            @block.tensor
            def _(pe):
                for used in (*ekT_mm, *out_mm, *kv_mm, *xnT_mm):
                    pe.sem_inc(used, FIRST)
                pe.wait_ge(const_in, 32)
                with pe.Fori(0, B) as b:
                    for h in range(2):
                        pe.wait_ge(lo_done[h], b + FIRST)
                        pe.wait_ge(ctx_in[h], b * 16 + 16)
                        for k in range(KD):
                            mm = pe.transpose(psT[h][:, k * P:(k + 1) * P], c_in[h][:, k * P:(k + 1) * P], ident[:])
                        mm.then_inc(cT_mm, 1)
                    for h in range(2):
                        pe.wait_ge(t1_done[h], b + FIRST)
                        pe.wait_ge(eq_done, 2 * b + h + 1)
                        for n in range(2):
                            mm = pe.matmul(psS[h][:, n * BANK:(n + 1) * BANK], blk[:], eq[h][:, n * BANK:(n + 1) * BANK], start=True, stop=True)
                        mm.then_inc(sums_done, 1)
                    for h in range(2):
                        pe.wait_ge(cT_done, 2 * b + h + 1)
                        pe.wait_ge(ek_done, 2 * b + h + 1)
                        for k in range(KD):
                            mm = pe.transpose(psT[h][:, k * P:(k + 1) * P], ek[h][:, k * P:(k + 1) * P], ident[:])
                        mm.then_inc(ekT_mm[h], 1)
                    for h in range(2):
                        pe.wait_ge(ekT_done, 2 * b + h + 1)
                        for k in range(KD):
                            mm = pe.matmul(psT[h][:, 0:P], ekT[h][:, k * P:(k + 1) * P], cT[h][:, k * P:(k + 1) * P], start=(k == 0), stop=(k == KD - 1))
                        mm.then_inc(kv_mm[h], 1)
                    for h in range(2):
                        pe.wait_ge(rS_done, 2 * b + h + 1)
                        pe.wait_ge(kvm_done, 2 * b + h + 1)
                        for n in range(2):
                            mm = pe.matmul(psS[h][:, n * BANK:(n + 1) * BANK], kvm[h][:], eq[h][:, n * BANK:(n + 1) * BANK], start=True, stop=True)
                        mm.then_inc(out_mm[h], 1)
                    for h in range(2):
                        pe.wait_ge(xn_done, 2 * b + h + 1)
                        for k in range(KD):
                            mm = pe.transpose(psT[h][:, k * P:(k + 1) * P], xn[h][:, k * P:(k + 1) * P], ident[:])
                        mm.then_inc(xnT_mm[h], 1)

            @block.vector
            def _(dve):
                for used in (*rks_done, *lo_done, *t1_done):
                    dve.sem_inc(used, FIRST)
                def stats(b, h, st_, mv_, sd, md):
                    settle(dve)
                    for n in range(2):
                        dve.bn_stats(st_[h][:, 6 * n:6 * n + 6], X[:, b * 2 + h, n * BANK:(n + 1) * BANK]).then_inc(sd, 1)
                    dve.wait_ge(sd, 4 * b + 2 * h + 2)
                    settle(dve)
                    dve.bn_aggr(mv_[h][:], st_[h][:]).then_inc(md, 1)

                def offset(b, h, mv_, rs_, nm_, rsd, nmd):
                    dve.wait_ge(rsd, 2 * b + h + 1)
                    dve.scalar_tensor_tensor(nm_[h][:], mv_[h][:, 0:1], -1.0, rs_[h][:], ALU.mult, ALU.mult).then_inc(nmd, 1)

                dve.wait_ge(tanh_done, 1)
                with dve.Fori(0, B) as b:
                    for h in range(2):
                        dve.wait_ge(x_in[h], b * 16 + 16)
                        stats(b, h, st, mv, stats_done, mv_done)
                        dve.wait_ge(ctx_in[h], b * 16 + 16)
                        dve.reduce_max(cm[h][:], c_in[h][:], AX.X).then_inc(cmax_done, 1)
                        dve.wait_ge(cmax_done, 2 * b + h + 1)
                        dve.tensor_scalar(ncm[h][:], cm[h][:], -1.0, None, ALU.mult).then_inc(ncm_done, 1)
                        offset(b, h, mv, rstd, nmr, rstd_done, nmr_done)
                    for h in range(2):
                        dve.wait_ge(ek_done, 2 * b + h + 1)
                        dve.reciprocal(rks[h][:], ksum[h][:]).then_inc(rks_done[h], 1)
                        dve.wait_ge(ekT_mm[h], b + 1 + FIRST)
                        dve.tensor_copy(ekT[h][:], psT[h][:]).then_inc(ekT_done, 1)
                    for h in range(2):
                        dve.wait_ge(sums_done, 2 * b + h + 1)
                        dve.reciprocal(rS[h][:], psS[h][:]).then_inc(rS_done, 1)
                        dve.wait_ge(rks_done[h], b + 1 + FIRST)
                        dve.wait_ge(kv_mm[h], b + 1 + FIRST)
                        dve.scalar_tensor_tensor(kvm[h][:], psT[h][:, 0:P], rks[h][:], blk[:], ALU.mult, ALU.mult).then_inc(kvm_done, 1)
                    for h in range(2):
                        dve.wait_ge(rS_done, 2 * b + h + 1)
                        dve.wait_ge(out_mm[h], b + 1 + FIRST)
                        dve.tensor_tensor(rS[h][:], psS[h][:], rS[h][:], ALU.mult).then_inc(t1_done[h], 1)
                        dve.wait_ge(t1_done[h], b + 1 + FIRST)
                        dve.scalar_tensor_tensor(X[:, b * 2 + h, :], rS[h][:], tg[:, 0:1], X[:, b * 2 + h, :], ALU.mult, ALU.add).then_inc(x_done, 1)
                        dve.wait_ge(x_done, 2 * b + h + 1)
                        stats(b, h, st2, mv2, stats2_done, mv2_done)
                        offset(b, h, mv2, rstd2, nmr2, rstd2_done, nmr2_done)
                    for h in range(2):
                        dve.wait_ge(hi_done, 2 * b + h + 1)
                        dve.tensor_tensor(xT_lo[:, :, bass.ds(b * L + h * P, P)], psT[h][:].rearrange("p (k t) -> p k t", k=KD),
                                          xT_hi[:, :, bass.ds(b * L + h * P, P)], ALU.subtract).then_inc(lo_done[h], 1)


def phase_nf4_ffn(nc, io, res):
    X, xT_hi, xT_lo, tg = (res[k] for k in ("X", "xT_hi", "xT_lo", "tg"))
    units = pack_units()
    lines_of = nf4_lines()
    NL = len(lines_of)
    OPS = 7
    RING = 3
    with ExitStack() as ctx:
        def sb(name, shape, dt=F32):
            return ctx.enter_context(nc.sbuf_tensor(name, shape, dt))

        def sem(name):
            return ctx.enter_context(nc.semaphore(name))

        codes = [sb(f"codes{s}", [P, BANK], I32) for s in range(RING)]
        absm = [sb(f"absm{s}", [P, BANK]) for s in range(RING)]
        line_all = sb("lines", [P, NL, BANK])
        line = [line_all[:, j, :] for j in range(NL)]
        wt = [sb(f"wt{s}", [P, BANK]) for s in range(2)]
        gu_hi = [sb(f"gu_hi{c}", [P, 2, KD, P], HALF) for c in range(2)]
        gu_lo = [sb(f"gu_lo{c}", [P, 2, KD, P], HALF) for c in range(2)]
        dn_hi = [sb(f"dn_hi{c}", [P, D], HALF) for c in range(2)]
        dn_lo = [sb(f"dn_lo{c}", [P, D], HALF) for c in range(2)]
        hid_hi = [sb(f"hid_hi{c}", [P, B * L], HALF) for c in range(2)]
        hid_lo = [sb(f"hid_lo{c}", [P, B * L], HALF) for c in range(2)]
        rel = [sb(f"rel{s}", [P, BANK]) for s in range(2)]
        LROWS = 96
        lora_a = sb("lora_a", [LROWS, 3, D], HALF)
        lora_bf = sb("lora_bf", [LROWS, 3, PAIR])
        lora_b = sb("lora_b", [LROWS, 3, PAIR], HALF)
        la_f = line_all[0:LROWS, 0:6, :].rearrange("p (m t) n -> p m (t n)", m=3)

        ps_lora = [ctx.enter_context(nc.psum_tensor(f"ps_lora{s}", [P, BANK], F32)) for s in range(2)]
        ps_ring = [ctx.enter_context(nc.psum_tensor(f"ps_ring{s}", [P, BANK], F32)) for s in range(6)]

        codes_in = [sem(f"codes_in{s}") for s in range(RING)]
        absm_in = [sem(f"absm_in{s}") for s in range(RING)]
        la_in, la_hi, la_done = sem("la_in"), sem("la_hi"), sem("la_done")
        lb_in, lb_hi, lb_done = sem("lb_in"), sem("lb_hi"), sem("lb_done")
        line_done, line_used = sem("line_done"), sem("line_used")
        scaled, wt_done, whi_done, wlo_done = sem("scaled"), sem("wt_done"), sem("whi_done"), sem("wlo_done")
        lora_mm = sem("lora_mm")
        up_mm, rel_done, mul_done, hidhi_done, hidlo_done = (sem(n) for n in ("up_mm", "rel_done", "mul_done", "hidhi_done", "hidlo_done"))
        down_mm, acc_done = sem("down_mm"), sem("acc_done")

        def dest(u, part):
            m, c, hf = units[u]
            if m == 2:
                return (dn_hi if part == 0 else dn_lo)[c][:, hf * BANK:(hf + 1) * BANK]
            kk = KD // 2
            return (gu_hi if part == 0 else gu_lo)[c][:, m, hf * kk:(hf + 1) * kk, :].rearrange("p k f -> p (k f)")

        def unit_no(j, u):
            return j * UNITS + u

        with nc.Block() as block:
            @block.sync
            def _(sp):
                sp.dma_start(la_f, io["lora_a"]).then_inc(la_in, 16)

                def load(j, u, first=False):
                    g = unit_no(j, u)
                    s = u % RING
                    if not first:
                        sp.wait_ge(scaled, g - RING + 1)
                    sp.dma_start(codes[s][:], io["codes"][j, u]).then_inc(codes_in[s], 16)
                    for half in range(2):
                        sp.dma_start(absm[s][half * QBLK:(half + 1) * QBLK, :],
                                     io["absmax"][j, u, half].partition_broadcast(QBLK)).then_inc(absm_in[s], 16)

                def load_lora(j, first=False):
                    if not first:
                        sp.wait_ge(lora_mm, j * UNITS)
                    sp.dma_start(lora_bf[:], io["lora_b"][j]).then_inc(lb_in, 16)

                load_lora(0, first=True)
                for u in range(UNITS):
                    load(0, u, first=u < RING)
                with sp.Fori(1, PAIRS) as j:
                    load_lora(j)
                    for u in range(UNITS):
                        load(j, u)

            @block.scalar
            def _(act):
                def lora_parts(j):
                    act.wait_ge(lb_in, j * 16 + 16)
                    act.activation(lora_b[:], lora_bf[:], ACT.Copy).then_inc(lb_hi, 1)

                def lines(j, u, first=False):
                    g = unit_no(j, u)
                    act.wait_ge(codes_in[u % RING], (j * (UNITS // RING) + u // RING) * 16 + 16)
                    for k, (slope, off) in enumerate(lines_of):
                        if not first:
                            act.wait_ge(line_used, (g - 1) * OPS + (OPS if k in (0, 4) else k if k < 4 else k - 1))
                        act.activation(
                            line[k], codes[u % RING][:], ACT.Copy, bias=off, scale=slope).then_inc(line_done, 1)

                def w_hi(j, u):
                    g = unit_no(j, u)
                    act.wait_ge(wt_done, g + 1)
                    act.activation(dest(u, 0), wt[u % 2][:], ACT.Copy).then_inc(whi_done, 1)

                def relu(j, c, t):
                    n = j * 2 * TB + c * TB + t
                    act.wait_ge(up_mm, n + 1)
                    act.activation(rel[t % 2][:], ps_ring[2 * (t % 2)][:], ACT.Relu).then_inc(rel_done, 1)

                def h_hi(j, c, t):
                    n = j * 2 * TB + c * TB + t
                    act.wait_ge(mul_done, n + 1)
                    act.activation(hid_hi[c][:, t * BANK:(t + 1) * BANK], rel[t % 2][:], ACT.Copy).then_inc(hidhi_done, 1)

                act.wait_ge(la_in, 16)
                act.activation(lora_a[:], la_f, ACT.Copy).then_inc(la_hi, 1)
                act.wait_ge(la_done, 1)
                lora_parts(0)
                for u in range(8):
                    lines(0, u, first=u == 0)
                    if u:
                        w_hi(0, u - 1)

                def pair(j, more):
                    for c in range(2):
                        for t in range(TB):
                            if c == 1 and t == 0 and more:
                                lora_parts(j + 1)
                            relu(j, c, t)
                            h_hi(j, c, t)
                            if c == 0:
                                w_hi(j, 7 + t)
                                lines(j, 8 + t)
                            elif t == 0:
                                w_hi(j, 11)
                                if more:
                                    lines(j + 1, 0)
                            elif more:
                                w_hi(j + 1, t - 1)
                                lines(j + 1, t)
                    if more:
                        for s in range(4):
                            w_hi(j + 1, 3 + s)
                            lines(j + 1, 4 + s)

                with act.Fori(0, PAIRS - 1) as j:
                    pair(j, True)
                pair(PAIRS - 1, False)

            @block.vector
            def _(dve):
                dve.sem_inc(acc_done, FIRST)

                def lora_parts(j):
                    dve.wait_ge(lb_hi, j + 1)
                    dve.tensor_tensor(lora_b[64:96], lora_bf[64:96], lora_b[64:96], ALU.subtract).then_inc(lb_done, 1)

                def weights(j, u):
                    g = unit_no(j, u)
                    n = 0

                    def used():
                        return g * OPS + n
                    for base in (0, 4):
                        for k in range(1, 4):
                            dve.wait_ge(line_done, g * NL + base + k + 1)
                            if k > 1:
                                dve.wait_ge(line_used, used())
                            if k == 1:
                                ins = dve.scalar_tensor_tensor(line[base], line[base], 0.0, line[base + 1], ALU.max, ALU.max)
                            else:
                                ins = dve.tensor_tensor(line[base], line[base], line[base + k], ALU.max)
                            ins.then_inc(line_used, 1)
                            n += 1
                    dve.wait_ge(line_used, used())
                    dve.wait_ge(wlo_done, g - 1) if not (isinstance(g, int) and g < 2) else None
                    dve.tensor_tensor(wt[u % 2][:], line[0], line[4], ALU.subtract).then_inc(line_used, 1)
                    n += 1
                    dve.wait_ge(line_used, used())
                    c = j * (UNITS // RING) + u // RING
                    dve.wait_ge(absm_in[u % RING], c * 32 + 32)
                    dve.tensor_tensor(wt[u % 2][:], wt[u % 2][:], absm[u % RING][:], ALU.mult).then_inc(scaled, 1)
                    dve.wait_ge(scaled, g + 1)
                    dve.wait_ge(lora_mm, g + 1)
                    dve.tensor_tensor(wt[u % 2][:], wt[u % 2][:], ps_lora[u % 2][:], ALU.add).then_inc(wt_done, 1)

                def w_lo(j, u):
                    g = unit_no(j, u)
                    dve.wait_ge(whi_done, g + 1)
                    dve.tensor_tensor(dest(u, 1), wt[u % 2][:], dest(u, 0), ALU.subtract).then_inc(wlo_done, 1)

                def mul(j, c, t):
                    n = j * 2 * TB + c * TB + t
                    dve.wait_ge(rel_done, n + 1)
                    dve.tensor_tensor(rel[t % 2][:], rel[t % 2][:], ps_ring[2 * (t % 2) + 1][:], ALU.mult).then_inc(mul_done, 1)

                def h_lo(j, c, t):
                    n = j * 2 * TB + c * TB + t
                    dve.wait_ge(hidhi_done, n + 1)
                    dve.tensor_tensor(hid_lo[c][:, t * BANK:(t + 1) * BANK], rel[t % 2][:], hid_hi[c][:, t * BANK:(t + 1) * BANK],
                                      ALU.subtract).then_inc(hidlo_done, 1)

                def accumulate(j, n):
                    i, hf = n // HALVES, n % HALVES
                    dve.wait_ge(down_mm, j * 2 * TILES + n + 1)
                    dst = X[:, i, hf * BANK:(hf + 1) * BANK]
                    dve.scalar_tensor_tensor(dst, ps_ring[n % 6][:], tg[:, 2:3], dst, ALU.mult, ALU.add).then_inc(acc_done, 1)

                dve.wait_ge(la_hi, 1)
                dve.tensor_tensor(lora_a[32:64], la_f[32:64], lora_a[32:64], ALU.subtract).then_inc(la_done, 1)
                lora_parts(0)
                for u in range(8):
                    weights(0, u)
                    if u:
                        w_lo(0, u - 1)

                def pair(j, more):
                    for c in range(2):
                        for t in range(TB):
                            if c == 1 and t == 0 and more:
                                lora_parts(j + 1)
                            mul(j, c, t)
                            h_lo(j, c, t)
                            if c == 0:
                                w_lo(j, 7 + t)
                                weights(j, 8 + t)
                            elif t == 0:
                                w_lo(j, 11)
                                if more:
                                    weights(j + 1, 0)
                            elif more:
                                w_lo(j + 1, t - 1)
                                weights(j + 1, t)
                    for s in range(4):
                        for n in range(8 * s, 8 * s + 8):
                            if n == 0:
                                dve.wait_ge(acc_done, j * 2 * TILES + FIRST)
                            accumulate(j, n)
                        if more:
                            w_lo(j + 1, 3 + s)
                            weights(j + 1, 4 + s)

                with dve.Fori(0, PAIRS - 1) as j:
                    pair(j, True)
                pair(PAIRS - 1, False)

            @block.tensor
            def _(pe):
                def lora(j, u):
                    g = unit_no(j, u)
                    m, c, hf = units[u]
                    if u == 0:
                        pe.wait_ge(lb_done, j + 1)
                    if not (isinstance(g, int) and g < 2):
                        pe.wait_ge(wt_done, g - 1)
                    o = ps_lora[u % 2]
                    if m == 2:
                        mm = pe.matmul(o[:], lora_b[:, m, c * P:(c + 1) * P], lora_a[:, m, hf * BANK:(hf + 1) * BANK], start=True, stop=True)
                    else:
                        for k in range(KD // 2):
                            kk = hf * (KD // 2) + k
                            mm = pe.matmul(o[:, k * P:(k + 1) * P], lora_a[:, m, kk * P:(kk + 1) * P], lora_b[:, m, c * P:(c + 1) * P], start=True, stop=True)
                    mm.then_inc(lora_mm, 1)

                def up(j, c, t):
                    n = j * 2 * TB + c * TB + t
                    if t == 0:
                        pe.wait_ge(wlo_done, j * UNITS + 4 * c + 4)
                        if c == 0:
                            pe.wait_ge(acc_done, j * 2 * TILES + FIRST)
                    if c > 0 or t >= 2:
                        pe.wait_ge(mul_done, n - 1)
                    ts = slice(t * BANK, (t + 1) * BANK)
                    for m in range(2):
                        o = ps_ring[2 * (t % 2) + m]
                        q = 0
                        for k in range(KD):
                            for w, xx in ((gu_hi, xT_hi), (gu_hi, xT_lo), (gu_lo, xT_hi)):
                                mm = pe.matmul(o[:], w[c][:, m, k, :], xx[:, k, ts], start=(q == 0), stop=(q == 3 * KD - 1))
                                q += 1
                    mm.then_inc(up_mm, 1)

                def down(j, n):
                    i, hf = n // HALVES, n % HALVES
                    if n == 0:
                        pe.wait_ge(wlo_done, j * UNITS + UNITS)
                        pe.wait_ge(hidlo_done, j * 2 * TB + 2 * TB)
                    if n >= 6:
                        pe.wait_ge(acc_done, j * 2 * TILES + n - 5 + FIRST)
                    q = 0
                    for c in range(2):
                        for hh, w in ((hid_hi, dn_hi), (hid_hi, dn_lo), (hid_lo, dn_hi)):
                            mm = pe.matmul(ps_ring[n % 6][:], hh[c][:, i * P:(i + 1) * P], w[c][:, hf * BANK:(hf + 1) * BANK],
                                           start=(q == 0), stop=(q == 5))
                            q += 1
                    mm.then_inc(down_mm, 1)

                pe.wait_ge(la_done, 1)
                for u in range(8):
                    lora(0, u)

                def pair(j, more):
                    for c in range(2):
                        for t in range(TB):
                            if c == 0:
                                lora(j, 8 + t)
                            up(j, c, t)
                            if c == 1 and more:
                                lora(j + 1, t)
                    for n in range(2 * TILES):
                        if more and n % 8 == 0:
                            lora(j + 1, 4 + n // 8)
                        down(j, n)

                with pe.Fori(0, PAIRS - 1) as j:
                    pair(j, True)
                pair(PAIRS - 1, False)


def spectra():
    t, f = np.arange(L)[:, None], np.arange(P)[None, :]
    even, odd = 2 * np.pi * t * f / L, 2 * np.pi * t * (f + 0.5) / L
    nyquist = np.where(t % 2 == 0, 1.0, -1.0)
    im = -np.sin(even)
    im[:, :1] = nyquist
    odd_re, odd_im = np.cos(odd), -np.sin(odd)
    last = (t == L - 1)
    fwd = np.stack([np.stack([np.cos(even), im]), np.stack([odd_re, odd_im]),
                    np.stack([odd_re - last * odd_re.sum(0), odd_im - last * odd_im.sum(0)])])
    weight = np.where(f == 0, 1.0, 2.0) / L
    re_inv = np.cos(even) * weight
    im_inv = re_inv.copy()
    im_inv[:, :1] = nyquist / L
    inv = np.stack([re_inv, im_inv, -np.sin(even) * weight, odd_re * 2 / L, odd_im * 2 / L])
    return (fwd.reshape(3, 2, 2, P, P).transpose(3, 2, 0, 1, 4).astype(np.float32),
            inv.transpose(2, 0, 1).astype(np.float32))


def phase_autocorrelation(nc, io, res):
    settle = settler(res["passed"])
    X, ident, tg, mhalf = (res[k] for k in ("X", "ident", "tg", "mhalf"))
    CB = BANK
    CH = CB // P
    U = 4
    N = B * 2
    c_d = io["ctx"].rearrange("b (t p) n -> b p t n", p=P)
    with ExitStack() as ctx:
        def sb(name, shape, dt=F32):
            return ctx.enter_context(nc.sbuf_tensor(name, shape, dt))

        def sem(name):
            return ctx.enter_context(nc.semaphore("a_" + name))

        fwd, inv, last = sb("fwd", [P, 2, 3, 2, P]), sb("inv", [P, 5, L]), sb("last", [P, P])
        half_gate = sb("half_gate", [P, 1])
        c_in = [sb(f"a_ctx{s}", [P, 2, D]) for s in range(2)]
        q = [sb(f"a_q{s}", [P, 2, D]) for s in range(2)]
        k_re, k_im, o_re, o_im = ([sb(f"{n}{s}", [P, CB]) for s in range(2)] for n in ("k_re", "k_im", "o_re", "o_im"))
        t_rr, t_ii, t_ir, t_ri = (sb(n, [P, CB]) for n in ("t_rr", "t_ii", "t_ir", "t_ri"))
        e_rr, e_ii, e_ri, e_ir = (sb(n, [P, CB]) for n in ("e_rr", "e_ii", "e_ri", "e_ir"))
        n_rr, n_ii, n_ri, n_ir = (sb(n, [P, CB]) for n in ("n_rr", "n_ii", "n_ri", "n_ir"))
        top8, next3 = sb("top8", [P, CH, 8]), sb("next3", [P, CH, 8])
        nmax, wsum, rws = sb("nmax", [P, CH]), sb("wsum", [P, CH]), sb("rws", [P, CH])
        cut, cut2, ex, wn = (sb(n, [P, CH, L]) for n in ("cut", "cut2", "ex", "wn"))
        wT = sb("wT", [P, 2, CB])
        st, mv, ve, rstd, nmr = sb("a_st", [P, 2, 12]), sb("a_mv", [P, 2, 2]), sb("a_ve", [P, 2]), sb("a_rstd", [P, 2]), sb("a_nmr", [P, 2])

        ps = [ctx.enter_context(nc.psum_tensor(f"a_ps{s}", [P, 2 * BANK], F32)) for s in range(4)]
        re, im = slice(0, CB), slice(CB, 2 * CB)

        const_in, gate_done = sem("const_in"), sem("gate_done")
        ctx_in = [sem(f"ctx_in{s}") for s in range(2)]
        stats_done, mv_done, ve_done, rstd_done, nmr_done, q_done = (sem(n) for n in ("stats_done", "mv_done", "ve_done", "rstd_done", "nmr_done", "q_done"))
        k_mm, u_mm, q_mm, k_done, u_done = (sem(n) for n in ("k_mm", "u_mm", "q_mm", "k_done", "u_done"))
        prod_done, prod_diff, corr_mm = sem("prod_done"), sem("prod_diff"), sem("corr_mm")
        top_done, cut_done, nmax_done, next_done, fill_done, cut2_done = (sem(n) for n in ("top_done", "cut_done", "nmax_done", "next_done", "fill_done", "cut2_done"))
        ex_done, w_done, rws_done, wn_done = (sem(n) for n in ("ex_done", "w_done", "rws_done", "wn_done"))
        wT_mm, wT_done, ws_mm, wprod_done, wprod_comb, out_mm, x_done = (sem(n) for n in ("wT_mm", "wT_done", "ws_mm", "wprod_done", "wprod_comb", "out_mm", "x_done"))

        with nc.Block() as block:
            @block.sync
            def _(sp):
                sp.dma_start(fwd[:], io["fwd"]).then_inc(const_in, 16)
                sp.dma_start(inv[:], io["inv"]).then_inc(const_in, 16)
                sp.dma_start(last[:], io["last"]).then_inc(const_in, 16)
                for s in range(2):
                    sp.dma_start(c_in[s][:], c_d[s]).then_inc(ctx_in[s], 16)
                with sp.Fori(1, B // 2) as m:
                    for s in range(2):
                        sp.wait_ge(out_mm, 4 * m - 2 + 2 * s + FIRST)
                        sp.dma_start(c_in[s][:], c_d[2 * m + s]).then_inc(ctx_in[s], 16)

            @block.gpsimd
            def _(pool):
                def rstd_of(batch):
                    pool.wait_ge(mv_done, 2 * batch + 2)
                    settle(pool)
                    pool.tensor_scalar(ve[:], mv[:, :, 1], EPS, None, ALU.add).then_inc(ve_done, 1)
                    pool.wait_ge(ve_done, batch + 1)
                    pool.tensor_tensor(rstd[:], ve[:], mhalf[:].to_broadcast([P, 2]), ALU.pow).then_inc(rstd_done, 1)

                def corr_diff(n):
                    pool.wait_ge(prod_done, 4 * n + 4)
                    pool.tensor_tensor(t_ir[:], t_ir[:], t_ri[:], ALU.subtract).then_inc(prod_diff, 1)

                def out_comb(n):
                    for k, (a, b_, op) in enumerate(((e_ri, e_ir, ALU.subtract), (n_rr, n_ii, ALU.add), (n_ri, n_ir, ALU.subtract))):
                        pool.wait_ge(wprod_done, 8 * n + (4, 6, 8)[k] + FIRST)
                        pool.tensor_tensor(a[:], a[:], b_[:], op).then_inc(wprod_comb, 1)

                rstd_of(0)
                corr_diff(0)

                def units(m, more):
                    for r in range(U):
                        n = U * m + r
                        if r % 2 == 0 and (more or r == 0):
                            rstd_of(2 * m + r // 2 + 1)
                        if more or r < U - 1:
                            corr_diff(n + 1)
                        out_comb(n)

                with pool.Fori(0, N // U - 1) as m:
                    units(m, True)
                units(N // U - 1, False)

            @block.scalar
            def _(act):
                def q_norm(batch, s):
                    act.wait_ge(nmr_done, batch + 1)
                    settle(act)
                    for t in range(2):
                        act.activation(q[s][:, t, :], X[:, 2 * batch + t, :], ACT.Identity, scale=rstd[:, t:t + 1], bias=nmr[:, t:t + 1]).then_inc(q_done, 1)

                def spectra_out(n, par):
                    for mm, done, pair, dst in ((k_mm, k_done, 1, (k_re, k_im)), (u_mm, u_done, 2, (o_re, o_im))):
                        act.wait_ge(mm, n + 1)
                        for half, d in zip((re, im), dst):
                            act.activation(d[par][:], ps[pair][:, half], ACT.Copy).then_inc(done, 1)

                def weights(n):
                    act.wait_ge(nmax_done, n + 1)
                    for c in range(CH):
                        act.activation(ex[:, c, :], ps[3][:, c * L:(c + 1) * L], ACT.Exp, bias=nmax[:, c:c + 1]).then_inc(ex_done, 1)
                    act.wait_ge(rws_done, n + 1)
                    for c in range(CH):
                        act.activation(wn[:, c, :], cut2[:, c, :], ACT.Copy, scale=rws[:, c:c + 1]).then_inc(wn_done, 1)

                def weights_T(n):
                    act.wait_ge(wT_mm, n + 1)
                    act.activation(wT[:].rearrange("p h c -> p (h c)"), ps[3][:], ACT.Copy).then_inc(wT_done, 1)

                q_norm(0, 0)
                spectra_out(0, 0)
                weights(0)

                def units(m, more):
                    for r in range(U):
                        n = U * m + r
                        nxt = more or r < U - 1
                        if r % 2 == 0 and (more or r == 0):
                            q_norm(2 * m + r // 2 + 1, (r // 2 + 1) % 2)
                        if nxt:
                            spectra_out(n + 1, (r + 1) % 2)
                        weights_T(n)
                        if nxt:
                            weights(n + 1)

                with act.Fori(0, N // U - 1) as m:
                    units(m, True)
                units(N // U - 1, False)

            @block.tensor
            def _(pe):
                pe.sem_inc(out_mm, FIRST)

                def dft(pair, half, kind, src, start=True):
                    for t in range(2):
                        mm = pe.matmul(ps[pair][:, half], fwd[:, t, kind, 0 if half is re else 1, :], src(t), start=(t == 0), stop=(t == 1))
                    return mm

                def spectra_in(n, batch, r, first=False):
                    s, cb = (r // 2) % 2, r % 2
                    cs = slice(cb * CB, (cb + 1) * CB)
                    if cb == 0:
                        pe.wait_ge(ctx_in[s], 16 * (batch // 2 + 1) if isinstance(batch, int) else 16 * first)
                    if not (isinstance(n, int) and n == 0):
                        pe.wait_ge(k_done, 2 * n)
                        pe.wait_ge(u_done, 2 * n)
                        pe.wait_ge(wprod_done, 8 * n - 8 + FIRST)
                    for half in (re, im):
                        mm = dft(1, half, 0, lambda t: c_in[s][:, t, cs])
                    mm.then_inc(k_mm, 1)
                    for half in (re, im):
                        mm = dft(2, half, 2, lambda t: c_in[s][:, t, cs])
                    mm.then_inc(u_mm, 1)
                    if cb == 0:
                        pe.wait_ge(q_done, 2 * batch + 2)
                    if not (isinstance(n, int) and n < 2):
                        pe.wait_ge(x_done, 2 * n - 2 + FIRST)
                    for half in (re, im):
                        mm = dft(0, half, 0, lambda t: q[s][:, t, cs])
                    mm.then_inc(q_mm, 1)

                def corr(n):
                    pe.wait_ge(prod_diff, n + 1)
                    pe.wait_ge(prod_done, 4 * n + 4)
                    if not (isinstance(n, int) and n == 0):
                        pe.wait_ge(wT_done, n)
                    for c in range(CH):
                        for k, src in enumerate((t_rr, t_ii, t_ir)):
                            mm = pe.matmul(ps[3][:, c * L:(c + 1) * L], src[:, c * P:(c + 1) * P], inv[:, k, :], start=(k == 0), stop=(k == 2))
                    mm.then_inc(corr_mm, 1)

                def weight_spectra(n):
                    pe.wait_ge(wn_done, CH * n + CH)
                    for h in range(2):
                        for c in range(CH):
                            mm = pe.transpose(ps[3][:, h * CB + c * P:h * CB + (c + 1) * P], wn[:, c, h * P:(h + 1) * P], ident[:])
                    mm.then_inc(wT_mm, 1)
                    pe.wait_ge(wT_done, n + 1)
                    return

                def weight_dfts(n, nxt):
                    pe.wait_ge(k_done, 2 * n + (4 if nxt else 2))
                    for half in (re, im):
                        dft(1, half, 0, lambda t: wT[:, t, :])
                    pe.wait_ge(u_done, 2 * n + (4 if nxt else 2))
                    for half in (re, im):
                        mm = dft(2, half, 1, lambda t: wT[:, t, :])
                    mm.then_inc(ws_mm, 1)

                def output(n, r, nxt):
                    s, cb = (r // 2) % 2, r % 2
                    pe.wait_ge(wprod_comb, 3 * n + 3)
                    pe.wait_ge(wprod_done, 8 * n + 8 + FIRST)
                    pe.wait_ge(prod_done, 4 * n + (8 if nxt else 4))
                    for t in range(2):
                        ts = slice(t * P, (t + 1) * P)
                        o = ps[0][:, t * CB:(t + 1) * CB]
                        pe.matmul(o, last[:], c_in[s][:, 1, cb * CB:(cb + 1) * CB], start=True, stop=False)
                        for k, src in enumerate((e_rr, e_ii, e_ri, n_rr, n_ri)):
                            mm = pe.matmul(o, inv[:, k, ts], src[:], start=False, stop=(k == 4))
                    mm.then_inc(out_mm, 1)

                pe.wait_ge(const_in, 48)
                spectra_in(0, 0, 0)
                corr(0)

                def units(m, more):
                    for r in range(U):
                        n = U * m + r
                        nxt = more or r < U - 1
                        if nxt:
                            r1 = (r + 1) % U
                            batch = 2 * m + (r + 1) // 2
                            spectra_in(n + 1, batch, r1, first=(m + 1 if r < U - 1 else m + 2))
                        weight_spectra(n)
                        weight_dfts(n, nxt)
                        if nxt:
                            corr(n + 1)
                        output(n, r, nxt)

                with pe.Fori(0, N // U - 1) as m:
                    units(m, True)
                units(N // U - 1, False)

            @block.vector
            def _(dve):
                for used in (wprod_done, x_done):
                    dve.sem_inc(used, FIRST)
                def stats(batch):
                    for t in range(2):
                        if not (isinstance(batch, int) and batch == 0):
                            dve.wait_ge(nmr_done, batch)
                        settle(dve)
                        for h in range(2):
                            dve.bn_stats(st[:, t, 6 * h:6 * h + 6], X[:, 2 * batch + t, h * BANK:(h + 1) * BANK]).then_inc(stats_done, 1)
                    for t in range(2):
                        dve.wait_ge(stats_done, 4 * batch + 2 * t + 2)
                        if t == 0 and not (isinstance(batch, int) and batch == 0):
                            dve.wait_ge(q_done, 2 * batch)
                        settle(dve)
                        dve.bn_aggr(mv[:, t, :], st[:, t, :]).then_inc(mv_done, 1)

                def offset(batch):
                    dve.wait_ge(rstd_done, batch + 1)
                    dve.wait_ge(mv_done, 2 * batch + 2)
                    dve.scalar_tensor_tensor(nmr[:], mv[:, :, 0], -1.0, rstd[:], ALU.mult, ALU.mult).then_inc(nmr_done, 1)

                def products(n, par):
                    dve.wait_ge(q_mm, n + 1)
                    dve.wait_ge(k_done, 2 * n + 2)
                    if not (isinstance(n, int) and n == 0):
                        dve.wait_ge(corr_mm, n)
                    for dst, a, b_ in ((t_rr, re, k_re), (t_ii, im, k_im), (t_ir, im, k_re), (t_ri, re, k_im)):
                        dve.tensor_tensor(dst[:], ps[0][:, a], b_[par][:], ALU.mult).then_inc(prod_done, 1)

                def select(n):
                    dve.wait_ge(corr_mm, n + 1)
                    settle(dve)
                    row = [ps[3][:, c * L:(c + 1) * L] for c in range(CH)]
                    for c in range(CH):
                        dve.max(top8[:, c, :], row[c]).then_inc(top_done, 1)
                    for c in range(CH):
                        dve.wait_ge(top_done, CH * n + c + 1)
                        if c == 0:
                            dve.wait_ge(next_done, CH * n)
                        settle(dve)
                        dve.match_replace(cut[:, c, :], top8[:, c, :], row[c], -BIG).then_inc(cut_done, 1)
                    dve.wait_ge(top_done, CH * n + CH)
                    dve.tensor_scalar(nmax[:], top8[:, :, 0], -1.0, None, ALU.mult).then_inc(nmax_done, 1)
                    for c in range(CH):
                        dve.wait_ge(cut_done, CH * n + c + 1)
                        settle(dve)
                        dve.max(next3[:, c, :], cut[:, c, :]).then_inc(next_done, 1)
                    dve.wait_ge(next_done, CH * n + CH)
                    dve.memset(next3[:, :, TOPK - 8:8], -BIG).then_inc(fill_done, 1)
                    dve.wait_ge(fill_done, n + 1)
                    dve.wait_ge(wn_done, CH * n)
                    settle(dve)
                    for c in range(CH):
                        dve.match_replace(cut2[:, c, :], next3[:, c, :], cut[:, c, :], -BIG).then_inc(cut2_done, 1)
                    for c in range(CH):
                        dve.wait_ge(cut2_done, CH * n + c + 1)
                        dve.wait_ge(ex_done, CH * n + c + 1)
                        dve.scalar_tensor_tensor(cut2[:, c, :], cut2[:, c, :], -0.5 * BIG, ex[:, c, :], ALU.is_le, ALU.mult,
                                                 accum_out=wsum[:, c:c + 1]).then_inc(w_done, 1)
                    dve.wait_ge(w_done, CH * n + CH)
                    dve.reciprocal(rws[:], wsum[:]).then_inc(rws_done, 1)

                def weight_products(n, par):
                    dve.wait_ge(ws_mm, n + 1)
                    if not (isinstance(n, int) and n == 0):
                        dve.wait_ge(out_mm, n + FIRST)
                    for dst, pair, a, b_ in ((e_rr, 1, re, k_re), (e_ii, 1, im, k_im), (e_ri, 1, re, k_im), (e_ir, 1, im, k_re),
                                             (n_rr, 2, re, o_re), (n_ii, 2, im, o_im), (n_ri, 2, re, o_im), (n_ir, 2, im, o_re)):
                        dve.tensor_tensor(dst[:], ps[pair][:, a], b_[par][:], ALU.mult).then_inc(wprod_done, 1)

                def add(n, m, r):
                    cb = r % 2
                    dve.wait_ge(out_mm, n + 1 + FIRST)
                    for t in range(2):
                        dst = X[:, U * m + 2 * (r // 2) + t, cb * CB:(cb + 1) * CB]
                        dve.scalar_tensor_tensor(dst, ps[0][:, t * CB:(t + 1) * CB], half_gate[:], dst, ALU.mult, ALU.add).then_inc(x_done, 1)

                dve.tensor_scalar(half_gate[:], tg[:, 1:2], 0.5, None, ALU.mult).then_inc(gate_done, 1)
                stats(0)
                offset(0)
                products(0, 0)
                select(0)
                dve.wait_ge(gate_done, 1)

                def units(m, more):
                    for r in range(U):
                        n = U * m + r
                        nxt = more or r < U - 1
                        if r % 2 == 0 and (more or r == 0):
                            stats(2 * m + r // 2 + 1)
                            offset(2 * m + r // 2 + 1)
                        if nxt:
                            products(n + 1, (r + 1) % 2)
                        weight_products(n, r % 2)
                        if nxt:
                            select(n + 1)
                        add(n, m, r)

                with dve.Fori(0, N // U - 1) as m:
                    units(m, True)
                units(N // U - 1, False)


def phase_dora_linear(nc, io, res):
    settle = settler(res["passed"])
    X, ident, tg, mhalf = (res[k] for k in ("X", "ident", "tg", "mhalf"))
    out_d = io["out"].rearrange("b (h p) n -> b h p n", p=P)
    with ExitStack() as ctx:
        def sb(name, shape, dt=F32):
            return ctx.enter_context(nc.sbuf_tensor("d_" + name, shape, dt))

        def sb2(name, shape, dt=F32):
            return [sb(f"{name}{h}", shape, dt) for h in range(2)]

        def sem(name):
            return ctx.enter_context(nc.semaphore("d_" + name))

        def sem2(name):
            return [sem(f"{name}{h}") for h in range(2)]

        E, sq = sb("E", [P, KD, D]), sb2("sq", [P, D])
        w_hi, w_lo = sb("w_hi", [P, KD, D], FINE), sb("w_lo", [P, KD, D], FINE)
        la, lb, ones = sb("la", [P, D]), sb("lb", [P, D]), sb("ones", [P, 1])
        mag, norm2, rnorm, gain = sb("mag", [P, KD]), sb("norm2", [P, KD]), sb("rnorm", [P, KD]), sb("gain", [P, KD])
        rnorm_row, gain_row = sb("rnorm_row", [P, D]), sb("gain_row", [P, D])
        st, mv, ve, rstd, nmr = sb2("st", [P, 12]), sb2("mv", [P, 2]), sb2("ve", [P, 1]), sb2("rstd", [P, 1]), sb2("nmr", [P, 1])
        xn, x_hi, x_lo, prod = sb2("xn", [P, D]), sb2("x_hi", [P, D], FINE), sb2("x_lo", [P, D], FINE), sb2("prod", [P, D])
        psT = [ctx.enter_context(nc.psum_tensor(f"d_psT{h}", [P, D], F32)) for h in range(2)]
        psO = [ctx.enter_context(nc.psum_tensor(f"d_psO{h}", [P, D], F32)) for h in range(2)]

        small_in, ones_set = sem("small_in"), sem("ones_set")
        w_in = [sem(f"w_in{k}") for k in range(KD // 2)]
        lora_mm, E_done, sq_done, norm_mm, norm_done, rnorm_done = (sem(n) for n in ("lora_mm", "E_done", "sq_done", "norm_mm", "norm_done", "rnorm_done"))
        gain_done, row_mm, row_done, scaled, whi_done, wlo_done = (sem(n) for n in ("gain_done", "row_mm", "row_done", "scaled", "whi_done", "wlo_done"))
        stats_done, mv_done, ve_done, rstd_done, nmr_done, xn_done, hi_done = (
            sem(n) for n in ("stats_done", "mv_done", "ve_done", "rstd_done", "nmr_done", "xn_done", "hi_done"))
        T_mm, lo_done, out_mm, prod_done, x_done = (sem2(n) for n in ("T_mm", "lo_done", "out_mm", "prod_done", "x_done"))

        with nc.Block() as block:
            @block.sync
            def _(sp):
                for dst, name in ((la, "lora1_a"), (lb, "lora1_b"), (mag, "mag")):
                    sp.dma_start(dst[:], io[name]).then_inc(small_in, 16)
                for k in range(0, KD, 2):
                    sp.dma_start(E[:, k:k + 2, :], io["w1"][:, k:k + 2, :]).then_inc(w_in[k // 2], 16)
                with sp.Fori(0, B) as b:
                    for h in range(2):
                        sp.wait_ge(x_done[h], 2 * b + 2)
                        sp.dma_start(out_d[b, h], X[:, 2 * b + h, :]).then_inc(res["stored"], 16)
                sp.wait_ge(res["stored"], 16 * TILES)

            @block.gpsimd
            def _(pool):
                pool.memset(ones[:], 1.0).then_inc(ones_set, 1)
                pool.wait_ge(norm_done, 1)
                pool.tensor_tensor(rnorm[:], norm2[:], mhalf[:].to_broadcast([P, KD]), ALU.pow).then_inc(rnorm_done, 1)
                with pool.Fori(0, B) as b:
                    for h in range(2):
                        pool.wait_ge(mv_done, 2 * b + h + 1)
                        settle(pool)
                        pool.tensor_scalar(ve[h][:], mv[h][:, 1:2], EPS, None, ALU.add).then_inc(ve_done, 1)
                        pool.wait_ge(ve_done, 2 * b + h + 1)
                        pool.tensor_tensor(rstd[h][:], ve[h][:], mhalf[:], ALU.pow).then_inc(rstd_done, 1)

            @block.scalar
            def _(act):
                for k in range(KD):
                    act.wait_ge(E_done, 2 * k + 2)
                    if k >= 2:
                        act.wait_ge(norm_mm, k - 1)
                    act.activation(sq[k % 2][:], E[:, k, :], ACT.Square).then_inc(sq_done, 1)
                for k in range(KD):
                    act.wait_ge(scaled, k + 1)
                    act.activation(w_hi[:, k, :], E[:, k, :], ACT.Copy).then_inc(whi_done, 1)
                with act.Fori(0, B) as b:
                    for h in range(2):
                        act.wait_ge(T_mm[h], b + FIRST)
                        act.wait_ge(nmr_done, 2 * b + h + 1)
                        settle(act)
                        act.activation(xn[h][:], X[:, 2 * b + h, :], ACT.Identity, scale=rstd[h][:], bias=nmr[h][:]).then_inc(xn_done, 1)
                        act.wait_ge(out_mm[h], 2 * b + FIRST)
                        act.wait_ge(T_mm[h], b + 1 + FIRST)
                        act.activation(x_hi[h][:], psT[h][:], ACT.Copy, scale=LN_SCALE).then_inc(hi_done, 1)

            @block.tensor
            def _(pe):
                for used in (*T_mm, *out_mm):
                    pe.sem_inc(used, FIRST)
                pe.wait_ge(small_in, 48)
                for k in range(KD):
                    if k >= 2:
                        pe.wait_ge(E_done, 2 * k - 2)
                    for n in range(2):
                        mm = pe.matmul(psT[k % 2][:, n * BANK:(n + 1) * BANK], la[:, k * P:(k + 1) * P], lb[:, n * BANK:(n + 1) * BANK], start=True, stop=True)
                        mm.then_inc(lora_mm, 1)
                pe.wait_ge(ones_set, 1)
                for k in range(KD):
                    pe.wait_ge(sq_done, k + 1)
                    for o in range(KD):
                        mm = pe.matmul(psO[0][:, o:o + 1], sq[k % 2][:, o * P:(o + 1) * P], ones[:], start=(k == 0 and o == 0),
                                       stop=(k == KD - 1), skip_group_check=True)
                    mm.then_inc(norm_mm, 1)
                for dst, src, ready, need in ((0, rnorm, rnorm_done, 1), (1, gain, gain_done, 1)):
                    pe.wait_ge(ready, need)
                    for o in range(KD):
                        mm = pe.matmul(psT[dst][:, o * P:(o + 1) * P], src[:, o:o + 1].to_broadcast([P, P]), ident[:], start=True, stop=True)
                    mm.then_inc(row_mm, 1)

                def turn(b, h):
                    pe.wait_ge(xn_done, 2 * b + h + 1)
                    if isinstance(b, int) and b == 0:
                        pe.wait_ge(row_done, 2)
                    else:
                        pe.wait_ge(lo_done[h], b + FIRST)
                    for k in range(KD):
                        mm = pe.transpose(psT[h][:, k * P:(k + 1) * P], xn[h][:, k * P:(k + 1) * P], ident[:])
                    mm.then_inc(T_mm[h], 1)

                def linear(b, h):
                    pe.wait_ge(lo_done[h], b + 1 + FIRST)
                    pe.wait_ge(prod_done[h], 2 * b + FIRST)
                    for n in range(2):
                        cols = slice(n * BANK, (n + 1) * BANK)
                        q = 0
                        for k in range(KD):
                            ks = slice(k * P, (k + 1) * P)
                            for a, w in ((x_hi, w_hi), (x_hi, w_lo), (x_lo, w_hi)):
                                mm = pe.matmul(psO[h][:, cols], a[h][:, ks], w[:, k, cols], start=(q == 0), stop=(q == 3 * KD - 1))
                                q += 1
                        mm.then_inc(out_mm[h], 1)

                turn(0, 0)
                pe.wait_ge(wlo_done, KD)

                def batch(b, more):
                    turn(b, 1)
                    linear(b, 0)
                    if more:
                        turn(b + 1, 0)
                    linear(b, 1)

                with pe.Fori(0, B - 1) as b:
                    batch(b, True)
                batch(B - 1, False)

            @block.vector
            def _(dve):
                for used in (*lo_done, *prod_done):
                    dve.sem_inc(used, FIRST)
                for k in range(KD):
                    dve.wait_ge(w_in[k // 2], 16)
                    for n in range(2):
                        cols = slice(n * BANK, (n + 1) * BANK)
                        dve.wait_ge(lora_mm, 2 * k + n + 1)
                        dve.tensor_tensor(E[:, k, cols], E[:, k, cols], psT[k % 2][:, cols], ALU.add).then_inc(E_done, 1)
                dve.tensor_scalar(gain[:], mag[:], tg[:, 3:4], 1.0 / (W_SCALE * LN_SCALE), ALU.mult, ALU.mult).then_inc(gain_done, 1)
                dve.wait_ge(norm_mm, KD)
                dve.tensor_copy(norm2[:], psO[0][:, 0:KD]).then_inc(norm_done, 1)
                dve.wait_ge(row_mm, 2)
                dve.tensor_copy(rnorm_row[:], psT[0][:]).then_inc(row_done, 1)
                dve.tensor_copy(gain_row[:], psT[1][:]).then_inc(row_done, 1)
                dve.wait_ge(row_done, 2)
                for k in range(KD):
                    dve.scalar_tensor_tensor(E[:, k, :], E[:, k, :], W_SCALE, rnorm_row[:], ALU.mult, ALU.mult).then_inc(scaled, 1)
                for k in range(KD):
                    dve.wait_ge(whi_done, k + 1)
                    dve.tensor_tensor(w_lo[:, k, :], E[:, k, :], w_hi[:, k, :], ALU.subtract).then_inc(wlo_done, 1)

                def normed(b, h):
                    settle(dve)
                    for n in range(2):
                        dve.bn_stats(st[h][:, 6 * n:6 * n + 6], X[:, 2 * b + h, n * BANK:(n + 1) * BANK]).then_inc(stats_done, 1)
                    dve.wait_ge(stats_done, 4 * b + 2 * h + 2)
                    settle(dve)
                    dve.bn_aggr(mv[h][:], st[h][:]).then_inc(mv_done, 1)
                    dve.wait_ge(rstd_done, 2 * b + h + 1)
                    dve.scalar_tensor_tensor(nmr[h][:], mv[h][:, 0:1], -1.0, rstd[h][:], ALU.mult, ALU.mult).then_inc(nmr_done, 1)
                    dve.wait_ge(hi_done, 2 * b + h + 1)
                    dve.scalar_tensor_tensor(x_lo[h][:], psT[h][:], LN_SCALE, x_hi[h][:], ALU.mult, ALU.subtract).then_inc(lo_done[h], 1)

                def add(b, h):
                    for n in range(2):
                        cols = slice(n * BANK, (n + 1) * BANK)
                        dve.wait_ge(out_mm[h], 2 * b + n + 1 + FIRST)
                        dve.tensor_tensor(prod[h][:, cols], psO[h][:, cols], gain_row[:, cols], ALU.mult).then_inc(prod_done[h], 1)
                    for n in range(2):
                        cols = slice(n * BANK, (n + 1) * BANK)
                        dve.wait_ge(prod_done[h], 2 * b + n + 1 + FIRST)
                        dve.tensor_tensor(X[:, 2 * b + h, cols], X[:, 2 * b + h, cols], prod[h][:, cols], ALU.add).then_inc(x_done[h], 1)

                def batch(b, more):
                    normed(b, 1)
                    add(b, 0)
                    if more:
                        normed(b + 1, 0)
                    add(b, 1)

                normed(0, 0)
                with dve.Fori(0, B - 1) as b:
                    batch(b, True)
                batch(B - 1, False)


def build(nc, io):
    with ExitStack() as ctx:
        def sb(name, shape, dt=F32):
            return ctx.enter_context(nc.sbuf_tensor(name, shape, dt))
        res = {"X": sb("X", [P, TILES, D]), "ident": sb("ident", [P, P]), "blk": sb("blk", [P, P]),
               "tg": sb("tg", [P, 4]), "gates": sb("gates", [P, 4]), "mhalf": sb("mhalf", [P, 1])}
        res["passed"] = ctx.enter_context(nc.semaphore("passed"))
        res["stored"] = ctx.enter_context(nc.semaphore("stored"))
        with ExitStack() as inner:
            res["xT_hi"] = inner.enter_context(nc.sbuf_tensor("xT_hi", [P, KD, B * L], HALF))
            res["xT_lo"] = inner.enter_context(nc.sbuf_tensor("xT_lo", [P, KD, B * L], HALF))
            phase_linear_attention(nc, io, res)
            phase_nf4_ffn(nc, io, res)
        phase_autocorrelation(nc, io, res)
        phase_dora_linear(nc, io, res)


def layouts(inputs):
    a = {k: np.asarray(v) for k, v in inputs.items()}
    padf = DFF_PAD - DFF
    kk = KD // 2
    units = pack_units()
    codes = np.zeros((PAIRS, UNITS, P, BANK), np.int32)
    absmax = np.zeros((PAIRS, UNITS, 2, BANK), np.float32)
    gate_up = []
    for m in ("g", "u"):
        c = np.pad(a[f"L0_ffn_{m}_codes"], ((0, padf), (0, 0)))
        s = np.pad(a[f"L0_ffn_{m}_absmax"], ((0, padf), (0, 0)))
        gate_up.append((c.reshape(PAIRS, 2, P, 2, kk, P), s.reshape(PAIRS, 2, P, 2, kk, 2)))
    dc = np.pad(a["L0_ffn_d_codes"], ((0, 0), (0, padf))).reshape(2, BANK, PAIRS, 2, P)
    ds = np.pad(a["L0_ffn_d_absmax"], ((0, 0), (0, padf // QBLK))).reshape(2, BANK, PAIRS, 2, 2)
    for u, (m, c, hf) in enumerate(units):
        if m < 2:
            cc, ss = gate_up[m]
            codes[:, u] = cc[:, c, :, hf].transpose(0, 3, 2, 1).reshape(PAIRS, P, BANK)
            absmax[:, u] = ss[:, c, :, hf].transpose(0, 3, 2, 1).reshape(PAIRS, 2, BANK)
        else:
            codes[:, u] = dc[hf, :, :, c].transpose(1, 2, 0)
            absmax[:, u] = ds[hf, :, :, c].transpose(1, 2, 0)
    lora_a = np.zeros((96, 3, D), np.float32)
    lora_b = np.zeros((PAIRS, 96, 3, PAIR), np.float32)
    for m, name in enumerate(("g", "u", "d")):
        la, lb = a[f"L0_ffn_{name}_lora_a"], a[f"L0_ffn_{name}_lora_b"]
        wide, long = (la.T, lb) if m < 2 else (lb, la.T)
        long = np.pad(long, ((0, 0), (0, padf))).reshape(R0, PAIRS, PAIR).transpose(1, 0, 2)
        for g in range(3):
            lora_a[32 * g:32 * g + R0, m] = wide
            lora_b[:, 32 * g:32 * g + R0, m] = long
    fwd, inv = spectra()
    last = np.zeros((P, P), np.float32)
    last[P - 1] = 1.0
    lora1_a, lora1_b = np.zeros((P, D), np.float32), np.zeros((P, D), np.float32)
    lora1_a[:R1], lora1_b[:R1] = a["L1_ffn_lora_A"], a["L1_ffn_lora_B"].T
    arrays = {
        "lora1_a": lora1_a, "lora1_b": lora1_b, "mag": a["L1_ffn_magnitude"].reshape(KD, P).T,
        "w1": a["L1_ffn_W"].T.reshape(KD, P, D).transpose(1, 0, 2),
        "fwd": fwd, "inv": inv, "last": last,
        "x": a["x"], "ctx": a["ctx_4096"], "g_xattn": a["g_xattn"], "g_ffn": a["g_ffn"],
        "ident": np.eye(P, dtype=np.float32), "blk": np.kron(np.eye(P // ROWS0), np.ones((ROWS0, ROWS0))).astype(np.float32),
        "codes": codes, "absmax": absmax, "lora_a": lora_a, "lora_b": lora_b,
    }
    return {k: np.ascontiguousarray(v) for k, v in arrays.items()}


def kernel(**inputs):
    import concourse.bacc as bacc
    from concourse.bass_utils import run_bass_kernel_spmd

    nc = bacc.Bacc("TRN2", target_bir_lowering=False, num_devices=1, dynamic_dma_scratch_size=2048)
    arrays, io = {}, {}
    for name, arr in layouts(inputs).items():
        arrays[f"in_{name}"] = arr
        io[name] = nc.dram_tensor(f"in_{name}", arr.shape, mybir.dt.from_np(arr.dtype), kind="ExternalInput").ap()
    io["out"] = nc.dram_tensor("out_0", (B, L, D), F32, kind="ExternalOutput").ap()
    build(nc, io)
    r = run_bass_kernel_spmd(nc, [arrays], core_ids=[0])
    return r.results[0]["out_0"]
```

```python
from contextlib import ExitStack

import numpy as np

import concourse.bass as bass
from concourse import mybir

F32 = mybir.dt.float32
I32 = mybir.dt.int32
HALF = mybir.dt.float16
ALU = mybir.AluOpType
ACT = mybir.ActivationFunctionType
AX = mybir.AxisListType

P = 128
B, L, D = 8, 256, 1024
TILES = B * L // P
KD = D // P
BANK = 512
EPS = 1e-5
DFF, R0 = 2752, 16
PAIR = 2 * P
PAIRS = -(-DFF // PAIR)
DFF_PAD = PAIRS * PAIR
QBLK = 64
HEADS0 = 8
ROWS0 = L // HEADS0
TOPK = int(2 * np.log(L))
R1 = 32
HALVES = 2
UNITS = 12
TB = B * L // BANK
BIG = 3.0e38
W_SCALE = 2.0 ** 12
LN_SCALE = 2.0 ** 6
WMAX, ABMAX, HMAX = 2.0 ** 13, 2.0 ** 13, 2.0 ** 15

NF4 = [-1.0, -0.6961928009986877, -0.5250730514526367, -0.39491748809814453, -0.28444138169288635,
       -0.18477343022823334, -0.09105003625154495, 0.0, 0.07958029955625534, 0.16093020141124725,
       0.2461123019456863, 0.33791524171829224, 0.44070982933044434, 0.5626170039176941,
       0.7229568362236023, 1.0]


def nf4_lines():
    out = []
    for j in (4, 5, 6, 7, 0, 1, 2, 3):
        s = NF4[2 * j + 1] - NF4[2 * j]
        o = NF4[2 * j] - 2 * j * s
        out.append((s, o) if j >= 4 else (-s, -o))
    return out


def pack_units():
    units = [(m, c, hf) for c in range(2) for m in (0, 1) for hf in range(2)]
    return units + [(2, c, hf) for c in range(2) for hf in range(2)]


FIRST = 1


def settler(passed):
    def settle(engine):
        engine.sem_inc(passed, 1)
    return settle


def phase_prepare(nc, io, res):
    X, ident, blk, tg, mhalf, gates, x_in = (res[k] for k in ("X", "ident", "blk", "tg", "mhalf", "gates", "x_in"))
    x_d = io["x"].rearrange("b (h p) n -> b h p n", p=P)
    NQ, NA, NB = io["bound_q"].shape[-1], KD, DFF_PAD // P
    TINY = 1e-30
    with ExitStack() as ctx:
        def sb(name, shape, dt=F32):
            return ctx.enter_context(nc.sbuf_tensor("p_" + name, shape, dt))

        def sem(name):
            return ctx.enter_context(nc.semaphore("p_" + name))

        q, a, b = sb("q", [P, 3, NQ]), sb("a", [P, 3, NA, R0]), sb("b", [P, 3, NB, R0])
        a_rows, b_cols = sb("a_rows", [P, 3, NA]), sb("b_cols", [P, 3, NB])
        own, every, norms = sb("own", [P, 12]), sb("every", [P, 12]), sb("norms", [P, 12])
        top, diag, ones, half = sb("top", [9, 1]), sb("diag", [9, 9]), sb("ones", [P, P]), sb("half", [P, 1])
        M, N, rM, rN, ab, rab, abp, ratio, nn = (sb(n, [P, k]) for n, k in (
            ("M", 3), ("N", 3), ("rM", 3), ("rN", 3), ("ab", 2), ("rab", 2), ("abp", 1), ("ratio", 3), ("nn", 1)))
        ps_top = ctx.enter_context(nc.psum_tensor("ps_top", [9, P], F32))
        ps_all = ctx.enter_context(nc.psum_tensor("ps_all", [P, 12], F32))
        bound_in, const_in, gates_in, const_set = sem("bound_in"), sem("const_in"), sem("gates_in"), sem("const_set")
        squared, step, top_mm, all_mm, norms_done, tanh_done = (sem(n) for n in ("squared", "step", "top_mm", "all_mm", "norms_done", "tanh_done"))
        OWN, DIAG, EVERY = 6, 8, 9

        with nc.Block() as block:
            @block.sync
            def _(sp):
                for dst, name in ((q, "bound_q"), (a, "bound_a"), (b, "bound_b")):
                    sp.dma_start(dst[:], io[name]).then_inc(bound_in, 16)
                sp.dma_start(ident[:], io["ident"]).then_inc(const_in, 16)
                sp.dma_start(blk[:], io["blk"]).then_inc(const_in, 16)
                for n, g in enumerate(("g_xattn", "g_ffn")):
                    sp.dma_start(gates[:, 2 * n:2 * n + 2], io[g].partition_broadcast(P)).then_inc(gates_in, 16)
                for h in range(2):
                    sp.dma_start(X[:, h, :], x_d[0, h]).then_inc(x_in[h], 16)

            @block.gpsimd
            def _(pool):
                pool.memset(mhalf[:], -0.5).then_inc(const_set, 1)
                pool.memset(half[:], 0.5).then_inc(const_set, 1)
                pool.memset(ones[:], 1.0).then_inc(const_set, 1)
                pool.wait_ge(const_set, 3)
                pool.wait_ge(step, EVERY)
                pool.tensor_tensor(norms[:], every[:], half[:].to_broadcast([P, 12]), ALU.pow).then_inc(norms_done, 1)

            @block.scalar
            def _(act):
                act.wait_ge(bound_in, 48)
                for t in (q, a, b):
                    act.activation(t[:], t[:], ACT.Square).then_inc(squared, 1)
                act.wait_ge(gates_in, 32)
                act.activation(tg[:], gates[:], ACT.Tanh).then_inc(tanh_done, 1)

            @block.tensor
            def _(pe):
                pe.wait_ge(const_in, 32)
                pe.wait_ge(step, OWN)
                pe.matmul(ps_top[:], own[:, 0:9], ident[:], start=True, stop=True).then_inc(top_mm, 1)
                pe.wait_ge(const_set, 3)
                pe.matmul(ps_all[:, 9:12], ones[:], own[:, 9:12], start=True, stop=True)
                pe.wait_ge(step, DIAG)
                pe.matmul(ps_all[:, 0:9], ones[0:9, :], diag[:], start=True, stop=True).then_inc(all_mm, 1)

            @block.vector
            def _(dve):
                dve.wait_ge(squared, 3)
                dve.reduce_max(own[:, 0:3], q[:], AX.X).then_inc(step, 1)
                dve.reduce_sum(a_rows[:], a[:], AX.X).then_inc(step, 1)
                dve.reduce_sum(b_cols[:], b[:], AX.X).then_inc(step, 1)
                dve.wait_ge(step, 3)
                dve.reduce_max(own[:, 3:6], a_rows[:], AX.X).then_inc(step, 1)
                dve.reduce_max(own[:, 6:9], b_cols[:], AX.X).then_inc(step, 1)
                dve.reduce_sum(own[:, 9:12], a_rows[:], AX.X).then_inc(step, 1)
                dve.wait_ge(top_mm, 1)
                dve.reduce_max(top[:], ps_top[:], AX.X).then_inc(step, 1)
                dve.wait_ge(step, 7)
                dve.tensor_scalar(diag[:], ident[0:9, 0:9], top[:], None, ALU.mult).then_inc(step, 1)
                dve.wait_ge(all_mm, 1)
                dve.tensor_copy(every[:], ps_all[:]).then_inc(step, 1)
                dve.wait_ge(norms_done, 1)
                max_q, max_a, max_b, norm_a = (norms[:, 3 * k:3 * k + 3] for k in range(4))
                dve.tensor_tensor(M[:], max_a, max_b, ALU.mult).then_inc(step, 1)
                dve.tensor_tensor(N[:], norm_a, max_b, ALU.mult).then_inc(step, 1)
                dve.reduce_max(ab[:], norms[:, 3:9].rearrange("p (s m) -> p s m", s=2), AX.X).then_inc(step, 1)
                dve.wait_ge(step, 12)
                dve.scalar_tensor_tensor(M[:], max_q, TINY, M[:], ALU.max, ALU.add).then_inc(step, 1)
                dve.tensor_scalar(ratio[:], max_q, D ** 0.5, TINY, ALU.mult, ALU.max).then_inc(step, 1)
                dve.tensor_scalar(ab[:], ab[:], TINY, None, ALU.max).then_inc(step, 1)
                dve.wait_ge(step, 15)
                dve.tensor_tensor(N[:], ratio[:], N[:], ALU.add).then_inc(step, 1)
                dve.reciprocal(rM[:], M[:]).then_inc(step, 1)
                dve.reciprocal(rab[:], ab[:]).then_inc(step, 1)
                dve.tensor_tensor(abp[:], ab[:, 0:1], ab[:, 1:2], ALU.mult).then_inc(step, 1)
                dve.wait_ge(step, 19)
                dve.reciprocal(rN[:], N[:]).then_inc(step, 1)
                dve.tensor_tensor(nn[:], N[:, 0:1], N[:, 1:2], ALU.mult).then_inc(step, 1)
                dve.tensor_scalar(res["w_scale"][:], rM[:], WMAX, None, ALU.mult).then_inc(step, 1)
                dve.tensor_scalar(res["ab_scale"][:], rab[:], ABMAX, None, ALU.mult).then_inc(step, 1)
                dve.wait_ge(step, 23)
                dve.tensor_scalar(res["lora_gain"][:], res["w_scale"][:], abp[:], ABMAX ** -2, ALU.mult, ALU.mult).then_inc(step, 1)
                dve.tensor_tensor(ratio[:], M[:], rN[:], ALU.mult).then_inc(step, 1)
                dve.scalar_tensor_tensor(nn[:], M[:, 2:3], D / (WMAX * HMAX), nn[:], ALU.mult, ALU.mult).then_inc(step, 1)
                dve.wait_ge(step, 26)
                dve.scalar_tensor_tensor(res["hid_gain"][:], ratio[:, 0:1], HMAX / (D * WMAX ** 2 * LN_SCALE ** 2), ratio[:, 1:2], ALU.mult, ALU.mult).then_inc(step, 1)
                dve.wait_ge(tanh_done, 1)
                dve.tensor_tensor(res["ffn_gain"][:], nn[:], tg[:, 2:3], ALU.mult).then_inc(step, 1)
                dve.wait_ge(step, 28)


def exists(i):
    return not isinstance(i, int) or 0 <= i < TILES


def after(engine, semaphore, count):
    if not isinstance(count, int) or count > 0:
        engine.wait_ge(semaphore, count)


def phase_linear_attention(nc, io, res):
    settle = settler(res["passed"])
    X, xT_hi, xT_lo, ident, blk, tg, mhalf, x_in = (res[k] for k in ("X", "xT_hi", "xT_lo", "ident", "blk", "tg", "mhalf", "x_in"))
    x_d = io["x"].rearrange("b (h p) n -> b h p n", p=P)
    c_d = io["ctx"].rearrange("b (h p) n -> b h p n", p=P)
    with ExitStack() as ctx:
        def sb(name, shape, dt=F32):
            return [ctx.enter_context(nc.sbuf_tensor(f"{name}{h}", shape, dt)) for h in range(2)]

        def sem(name):
            return ctx.enter_context(nc.semaphore(name))

        c_in, cT, eq, ek, ekT, xn = (sb(n, [P, D]) for n in ("c_in", "cT", "eq", "ek", "ekT", "xn"))
        kvm, rS = sb("kvm", [P, P]), sb("rS", [P, D // ROWS0])
        rSx = ctx.enter_context(nc.sbuf_tensor("rSx", [P, D], F32))
        st, mv, ve, rstd, nmr = sb("st", [P, 12]), sb("mv", [P, 2]), sb("ve", [P, 1]), sb("rstd", [P, 1]), sb("nmr", [P, 1])
        st2, mv2, ve2, rstd2, nmr2 = sb("st2", [P, 12]), sb("mv2", [P, 2]), sb("ve2", [P, 1]), sb("rstd2", [P, 1]), sb("nmr2", [P, 1])
        cm, ncm, ksum, rks = sb("cm", [P, 1]), sb("ncm", [P, 1]), sb("ksum", [P, 1]), sb("rks", [P, 1])
        psE, psB, psO, psX = (ctx.enter_context(nc.psum_tensor(n, [P, D], F32)) for n in ("psE", "psB", "psO", "psX"))

        ctx_in, cT_in = ([sem(f"{n}{h}") for h in range(2)] for n in ("ctx_in", "cT_in"))
        stats_done, mv_done, ve_done, rstd_done, nmr_done = (sem(n) for n in ("stats_done", "mv_done", "ve_done", "rstd_done", "nmr_done"))
        cmax_done, ncm_done, eq_done, ek_done, rks_done = (sem(n) for n in ("cmax_done", "ncm_done", "eq_done", "ek_done", "rks_done"))
        ekT_mm, ekT_done, kv_mm, kvm_done = (sem(n) for n in ("ekT_mm", "ekT_done", "kv_mm", "kvm_done"))
        sums_mm, rS_done, rSx_done, rS_mm, eqn_done, out_mm, x_done = (sem(n) for n in ("sums_mm", "rS_done", "rSx_done", "rS_mm", "eqn_done", "out_mm", "x_done"))
        stats2_done, mv2_done, ve2_done, rstd2_done, nmr2_done = (sem(n) for n in ("stats2_done", "mv2_done", "ve2_done", "rstd2_done", "nmr2_done"))
        xn_done, xT_mm, hi_done, lo_done = (sem(n) for n in ("xn_done", "xT_mm", "hi_done", "lo_done"))

        def run(engine, step):
            for i in range(4):
                step(i, i % 2)
            with engine.Fori(2, B - 1) as b:
                for h in range(2):
                    step(b * 2 + h, h)
            for i in range(TILES - 2, TILES + 3):
                step(i, i % 2)

        with nc.Block() as block:
            @block.sync
            def _(sp):
                def load(b, h):
                    sp.dma_start(c_in[h][:], c_d[b, h]).then_inc(ctx_in[h], 16)

                def load_T(b, h):
                    sp.dma_start(cT[h][:], io["ctxT"][b, h]).then_inc(cT_in[h], 16)

                for h in range(2):
                    load(0, h)
                    load_T(0, h)
                with sp.Fori(1, B) as b:
                    for h in range(2):
                        sp.wait_ge(ek_done, b * 2 + h - 1)
                        sp.dma_start(X[:, b * 2 + h, :], x_d[b, h]).then_inc(x_in[h], 16)
                        load(b, h)
                        sp.wait_ge(kv_mm, b * 2 + h - 1)
                        load_T(b, h)

            @block.gpsimd
            def _(pool):
                def rsqrt(i, h, mv_, ve_, rs_, mvd, ved, rsd):
                    pool.wait_ge(mvd, i + 1)
                    settle(pool)
                    pool.tensor_scalar(ve_[h][:], mv_[h][:, 1:2], EPS, None, ALU.add).then_inc(ved, 1)
                    pool.wait_ge(ved, i + 1)
                    pool.tensor_tensor(rs_[h][:], ve_[h][:], mhalf[:], ALU.pow).then_inc(rsd, 1)

                def step(i, h):
                    if exists(i + 1):
                        rsqrt(i + 1, 1 - h, mv, ve, rstd, mv_done, ve_done, rstd_done)
                    if exists(i - 1):
                        rsqrt(i - 1, 1 - h, mv2, ve2, rstd2, mv2_done, ve2_done, rstd2_done)

                rsqrt(0, 0, mv, ve, rstd, mv_done, ve_done, rstd_done)
                run(pool, step)

            @block.scalar
            def _(act):
                def exponentials(i, h):
                    act.wait_ge(nmr_done, i + 1)
                    after(act, out_mm, i - 1)
                    settle(act)
                    act.activation(eq[h][:], X[:, i, :], ACT.Exp, scale=rstd[h][:], bias=nmr[h][:]).then_inc(eq_done, 1)
                    after(act, ekT_mm, i - 1)
                    after(act, rks_done, i - 1)
                    act.wait_ge(ncm_done, i + 1)
                    act.activation(ek[h][:], c_in[h][:], ACT.Exp, bias=ncm[h][:], accum_out=ksum[h][:]).then_inc(ek_done, 1)

                def step(i, h):
                    if exists(i):
                        after(act, kv_mm, i - 1)
                        act.wait_ge(ekT_mm, i + 1)
                        act.activation(ekT[h][:], psE[:], ACT.Copy).then_inc(ekT_done, 1)
                        after(act, rS_mm, i)
                        act.wait_ge(rS_done, i + 1)
                        act.activation(rSx[:].rearrange("p (n r) -> p n r", r=ROWS0), rS[h][:].unsqueeze(2).to_broadcast([P, D // ROWS0, ROWS0]),
                                       ACT.Copy).then_inc(rSx_done, 1)
                    if exists(i + 1):
                        exponentials(i + 1, 1 - h)
                    if exists(i - 1):
                        after(act, xT_mm, i - 2)
                        act.wait_ge(nmr2_done, i)
                        settle(act)
                        act.activation(xn[1 - h][:], X[:, i - 1, :], ACT.Identity, scale=rstd2[1 - h][:], bias=nmr2[1 - h][:]).then_inc(xn_done, 1)
                    if exists(i - 2):
                        act.wait_ge(xT_mm, i - 1)
                        settle(act)
                        act.activation(xT_hi[:, :, bass.ds((i - 2) * P, P)], psX[:].rearrange("p (k t) -> p k t", k=KD),
                                       ACT.Copy, scale=LN_SCALE).then_inc(hi_done, 1)

                exponentials(0, 0)
                run(act, step)

            @block.tensor
            def _(pe):
                def step(i, h):
                    if exists(i):
                        after(pe, kvm_done, i)
                        pe.wait_ge(ek_done, i + 1)
                        for k in range(KD):
                            mm = pe.transpose(psE[:, k * P:(k + 1) * P], ek[h][:, k * P:(k + 1) * P], ident[:])
                        mm.then_inc(ekT_mm, 1)
                        after(pe, eqn_done, i)
                        pe.wait_ge(eq_done, i + 1)
                        for k in range(KD):
                            mm = pe.matmul(psB[:, k * P:(k + 1) * P], eq[h][:, k * P:(k + 1) * P], blk[:], start=True, stop=True)
                        mm.then_inc(sums_mm, 1)
                    if exists(i - 1):
                        pe.wait_ge(eqn_done, i)
                        pe.wait_ge(kvm_done, i)
                        after(pe, x_done, i - 1)
                        for n in range(2):
                            mm = pe.matmul(psO[:, n * BANK:(n + 1) * BANK], kvm[1 - h][:], eq[1 - h][:, n * BANK:(n + 1) * BANK], start=True, stop=True)
                        mm.then_inc(out_mm, 1)
                    if exists(i):
                        pe.wait_ge(ekT_done, i + 1)
                        pe.wait_ge(cT_in[h], (i // 2) * 16 + 16 if isinstance(i, int) else (i - h) * 8 + 16)
                        for k in range(KD):
                            mm = pe.matmul(psE[:, 0:P], ekT[h][:, k * P:(k + 1) * P], cT[h][:, k * P:(k + 1) * P], start=(k == 0), stop=(k == KD - 1))
                        mm.then_inc(kv_mm, 1)
                        pe.wait_ge(rSx_done, i + 1)
                        for k in range(KD):
                            mm = pe.matmul(psB[:, k * P:(k + 1) * P], rSx[:, k * P:(k + 1) * P], ident[:], start=True, stop=True)
                        mm.then_inc(rS_mm, 1)
                    if exists(i - 2):
                        pe.wait_ge(xn_done, i - 1)
                        after(pe, lo_done, i - 2)
                        for k in range(KD):
                            mm = pe.transpose(psX[:, k * P:(k + 1) * P], xn[h][:, k * P:(k + 1) * P], ident[:])
                        mm.then_inc(xT_mm, 1)

                run(pe, step)

            @block.vector
            def _(dve):
                def stats(i, h, st_, mv_, sd, md):
                    settle(dve)
                    for n in range(2):
                        dve.bn_stats(st_[h][:, 6 * n:6 * n + 6], X[:, i, n * BANK:(n + 1) * BANK]).then_inc(sd, 1)
                    dve.wait_ge(sd, i * 2 + 2)
                    settle(dve)
                    dve.bn_aggr(mv_[h][:], st_[h][:]).then_inc(md, 1)

                def offset(i, h, mv_, rs_, nm_, rsd, nmd):
                    dve.wait_ge(rsd, i + 1)
                    dve.scalar_tensor_tensor(nm_[h][:], mv_[h][:, 0:1], -1.0, rs_[h][:], ALU.mult, ALU.mult).then_inc(nmd, 1)

                def prepare(i, h):
                    loads = (i // 2) * 16 + 16 if isinstance(i, int) else (i - h) * 8 + 16
                    dve.wait_ge(x_in[h], loads)
                    stats(i, h, st, mv, stats_done, mv_done)
                    dve.wait_ge(ctx_in[h], loads)
                    dve.reduce_max(cm[h][:], c_in[h][:], AX.X).then_inc(cmax_done, 1)
                    offset(i, h, mv, rstd, nmr, rstd_done, nmr_done)
                    dve.wait_ge(cmax_done, i + 1)
                    dve.tensor_scalar(ncm[h][:], cm[h][:], -1.0, None, ALU.mult).then_inc(ncm_done, 1)

                def step(i, h):
                    if exists(i - 3):
                        dve.wait_ge(hi_done, i - 2)
                        cols = bass.ds((i - 3) * P, P)
                        dve.scalar_tensor_tensor(xT_lo[:, :, cols], psX[:].rearrange("p (k t) -> p k t", k=KD), LN_SCALE,
                                                 xT_hi[:, :, cols], ALU.mult, ALU.subtract).then_inc(lo_done, 1)
                    if exists(i + 1):
                        prepare(i + 1, 1 - h)
                    if exists(i):
                        dve.wait_ge(ek_done, i + 1)
                        dve.reciprocal(rks[h][:], ksum[h][:]).then_inc(rks_done, 1)
                        dve.wait_ge(sums_mm, i + 1)
                        dve.reciprocal(rS[h][:], psB[:, 0:D:ROWS0]).then_inc(rS_done, 1)
                    if exists(i - 1):
                        dve.wait_ge(out_mm, i)
                        dve.scalar_tensor_tensor(X[:, i - 1, :], psO[:], tg[:, 0:1], X[:, i - 1, :], ALU.mult, ALU.add).then_inc(x_done, 1)
                        dve.wait_ge(x_done, i)
                        stats(i - 1, 1 - h, st2, mv2, stats2_done, mv2_done)
                    if exists(i):
                        dve.wait_ge(rks_done, i + 1)
                        dve.wait_ge(kv_mm, i + 1)
                        dve.scalar_tensor_tensor(kvm[h][:], psE[:, 0:P], rks[h][:], blk[:], ALU.mult, ALU.mult).then_inc(kvm_done, 1)
                    if exists(i - 1):
                        offset(i - 1, 1 - h, mv2, rstd2, nmr2, rstd2_done, nmr2_done)
                    if exists(i):
                        dve.wait_ge(rS_mm, i + 1)
                        dve.tensor_tensor(eq[h][:], psB[:], eq[h][:], ALU.mult).then_inc(eqn_done, 1)

                prepare(0, 0)
                run(dve, step)


def phase_nf4_ffn(nc, io, res):
    X, xT_hi, xT_lo = (res[k] for k in ("X", "xT_hi", "xT_lo"))
    w_scale, ab_scale, lora_gain, hid_gain, ffn_gain = (res[k] for k in ("w_scale", "ab_scale", "lora_gain", "hid_gain", "ffn_gain"))
    units = pack_units()
    lines_of = nf4_lines()
    NL = len(lines_of)
    OPS = 7
    RING = 3
    ACC_FIRST = 8
    with ExitStack() as ctx:
        def sb(name, shape, dt=F32):
            return ctx.enter_context(nc.sbuf_tensor(name, shape, dt))

        def sem(name):
            return ctx.enter_context(nc.semaphore(name))

        codes = [sb(f"codes{s}", [P, BANK], I32) for s in range(RING)]
        absm = [sb(f"absm{s}", [P, BANK]) for s in range(RING)]
        line_all = sb("lines", [P, NL, BANK])
        line = [line_all[:, j, :] for j in range(NL)]
        wt = [sb(f"wt{s}", [P, BANK]) for s in range(2)]
        gu_hi = [sb(f"gu_hi{c}", [P, 2, KD, P], HALF) for c in range(2)]
        gu_lo = [sb(f"gu_lo{c}", [P, 2, KD, P], HALF) for c in range(2)]
        dn_hi = [sb(f"dn_hi{c}", [P, D], HALF) for c in range(2)]
        dn_lo = [sb(f"dn_lo{c}", [P, D], HALF) for c in range(2)]
        hid_hi = [sb(f"hid_hi{c}", [P, B * L], HALF) for c in range(2)]
        hid_lo = [sb(f"hid_lo{c}", [P, B * L], HALF) for c in range(2)]
        rel = [sb(f"rel{s}", [P, BANK]) for s in range(2)]
        LROWS = 96
        lora_a = sb("lora_a", [LROWS, 3, D], HALF)
        lora_bf = sb("lora_bf", [LROWS, 3, PAIR])
        lora_b = sb("lora_b", [LROWS, 3, PAIR], HALF)
        la_f = line_all[0:LROWS, 0:6, :].rearrange("p (m t) n -> p m (t n)", m=3)

        ps_lora = [ctx.enter_context(nc.psum_tensor(f"ps_lora{s}", [P, BANK], F32)) for s in range(2)]
        ps_ring = [ctx.enter_context(nc.psum_tensor(f"ps_ring{s}", [P, BANK], F32)) for s in range(6)]

        codes_in = [sem(f"codes_in{s}") for s in range(RING)]
        absm_in = [sem(f"absm_in{s}") for s in range(RING)]
        la_in, la_hi, la_done = sem("la_in"), sem("la_hi"), sem("la_done")
        lb_in, lb_hi, lb_done = sem("lb_in"), sem("lb_hi"), sem("lb_done")
        line_done, line_used = sem("line_done"), sem("line_used")
        scaled, wt_done, whi_done, wlo_done = sem("scaled"), sem("wt_done"), sem("whi_done"), sem("wlo_done")
        lora_mm = sem("lora_mm")
        up_mm, rel_done, mul_done, hidhi_done, hidlo_done = (sem(n) for n in ("up_mm", "rel_done", "mul_done", "hidhi_done", "hidlo_done"))
        down_mm, acc_done = sem("down_mm"), sem("acc_done")

        def dest(u, part):
            m, c, hf = units[u]
            if m == 2:
                return (dn_hi if part == 0 else dn_lo)[c][:, hf * BANK:(hf + 1) * BANK]
            kk = KD // 2
            return (gu_hi if part == 0 else gu_lo)[c][:, m, hf * kk:(hf + 1) * kk, :].rearrange("p k f -> p (k f)")

        AHEAD = 5
        UNIT_B = (10, 11, 0, 1)

        def unit_of_B(j, t):
            return j + (UNIT_B[t] < AHEAD), UNIT_B[t]

        def unit_no(j, u):
            return j * UNITS + u

        with nc.Block() as block:
            @block.sync
            def _(sp):
                sp.dma_start(la_f, io["lora_a"]).then_inc(la_in, 16)

                def load(j, u, first=False):
                    g = unit_no(j, u)
                    s = u % RING
                    if not first:
                        sp.wait_ge(scaled, g - RING + 1)
                    sp.dma_start(codes[s][:], io["codes"][j, u]).then_inc(codes_in[s], 16)
                    for half in range(2):
                        sp.dma_start(absm[s][half * QBLK:(half + 1) * QBLK, :],
                                     io["absmax"][j, u, half].partition_broadcast(QBLK)).then_inc(absm_in[s], 16)

                def load_lora(j, first=False):
                    if not first:
                        sp.wait_ge(lora_mm, j * UNITS)
                    sp.dma_start(lora_bf[:], io["lora_b"][j]).then_inc(lb_in, 16)

                load_lora(0, first=True)
                for u in range(UNITS):
                    load(0, u, first=u < RING)
                with sp.Fori(1, PAIRS) as j:
                    load_lora(j)
                    for u in range(UNITS):
                        load(j, u)

            @block.scalar
            def _(act):
                def lora_parts(j):
                    act.wait_ge(lb_in, j * 16 + 16)
                    act.activation(lora_b[:], lora_bf[:], ACT.Copy, scale=ab_scale[0:LROWS, 1:2]).then_inc(lb_hi, 1)

                def lines(j, u, first=False):
                    g = unit_no(j, u)
                    act.wait_ge(codes_in[u % RING], (j * (UNITS // RING) + u // RING) * 16 + 16)
                    for k, (slope, off) in enumerate(lines_of):
                        if not first:
                            act.wait_ge(line_used, (g - 1) * OPS + (OPS if k in (0, 4) else k if k < 4 else k - 1))
                        act.activation(
                            line[k], codes[u % RING][:], ACT.Copy, bias=off, scale=slope).then_inc(line_done, 1)

                def w_hi(j, u):
                    g = unit_no(j, u)
                    act.wait_ge(wt_done, g + 1)
                    act.activation(dest(u, 0), wt[u % 2][:], ACT.Copy).then_inc(whi_done, 1)

                def relu(j, c, t):
                    n = j * 2 * TB + c * TB + t
                    act.wait_ge(up_mm, n + 1)
                    act.activation(rel[t % 2][:], ps_ring[2 + 2 * (t % 2)][:], ACT.Relu).then_inc(rel_done, 1)

                def h_hi(j, c, t):
                    n = j * 2 * TB + c * TB + t
                    act.wait_ge(mul_done, n + 1)
                    act.activation(hid_hi[c][:, t * BANK:(t + 1) * BANK], rel[t % 2][:], ACT.Copy).then_inc(hidhi_done, 1)

                act.wait_ge(la_in, 16)
                act.activation(lora_a[:], la_f, ACT.Copy, scale=ab_scale[0:LROWS, 0:1]).then_inc(la_hi, 1)
                act.wait_ge(la_done, 1)
                lora_parts(0)
                for u in range(AHEAD):
                    lines(0, u, first=u == 0)
                    if u:
                        w_hi(0, u - 1)

                def unit(j, u):
                    lines(j, u)
                    w_hi(j - (u == 0), (u - 1) % UNITS)

                def pair(j, more):
                    unit(j, AHEAD)
                    for t in range(TB):
                        relu(j, 0, t)
                        unit(j, AHEAD + 1 + t)
                        h_hi(j, 0, t)
                    for t in range(TB):
                        if t == 2 and more:
                            lora_parts(j + 1)
                        relu(j, 1, t)
                        if t < 2 or more:
                            unit(*unit_of_B(j, t))
                        elif t == 2:
                            w_hi(j, UNITS - 1)
                        h_hi(j, 1, t)
                    if more:
                        for u in range(2, AHEAD):
                            unit(j + 1, u)

                with act.Fori(0, PAIRS - 1) as j:
                    pair(j, True)
                pair(PAIRS - 1, False)

            @block.gpsimd
            def _(pool):
                def w_lo(j, u):
                    pool.wait_ge(whi_done, unit_no(j, u) + 1)
                    pool.tensor_tensor(dest(u, 1), wt[u % 2][:], dest(u, 0), ALU.subtract).then_inc(wlo_done, 1)

                def pair(j, more):
                    for u in range(AHEAD, UNITS):
                        w_lo(j, u)
                    if more:
                        for u in range(AHEAD):
                            w_lo(j + 1, u)

                for u in range(AHEAD):
                    w_lo(0, u)
                with pool.Fori(0, PAIRS - 1) as j:
                    pair(j, True)
                pair(PAIRS - 1, False)

            @block.vector
            def _(dve):
                dve.sem_inc(acc_done, ACC_FIRST)

                def lora_parts(j):
                    dve.wait_ge(lb_hi, j + 1)
                    dve.scalar_tensor_tensor(lora_b[64:96], lora_bf[64:96], ab_scale[64:96, 1:2], lora_b[64:96], ALU.mult, ALU.subtract).then_inc(lb_done, 1)

                def combine(j, u, sign):
                    g = unit_no(j, u)
                    base, n = 4 * sign, g * OPS + 3 * sign
                    for k in range(1, 4):
                        dve.wait_ge(line_done, g * NL + base + k + 1)
                        if k == 1:
                            dve.scalar_tensor_tensor(line[base], line[base], 0.0, line[base + 1], ALU.max, ALU.max).then_inc(line_used, 1)
                        else:
                            dve.wait_ge(line_used, n + k - 1)
                            dve.tensor_tensor(line[base], line[base], line[base + k], ALU.max).then_inc(line_used, 1)

                def finish(j, u):
                    g = unit_no(j, u)
                    m = units[u][0]
                    dve.wait_ge(line_used, g * OPS + 6)
                    if not (isinstance(g, int) and g < 2):
                        dve.wait_ge(wlo_done, g - 1)
                    dve.tensor_tensor(wt[u % 2][:], line[0], line[4], ALU.subtract).then_inc(line_used, 1)
                    dve.wait_ge(line_used, g * OPS + OPS)
                    dve.wait_ge(absm_in[u % RING], (j * (UNITS // RING) + u // RING) * 32 + 32)
                    dve.scalar_tensor_tensor(wt[u % 2][:], wt[u % 2][:], w_scale[:, m:m + 1], absm[u % RING][:], ALU.mult, ALU.mult).then_inc(scaled, 1)
                    dve.wait_ge(scaled, g + 1)
                    dve.wait_ge(lora_mm, g + 1)
                    dve.scalar_tensor_tensor(wt[u % 2][:], ps_lora[u % 2][:], lora_gain[:, m:m + 1], wt[u % 2][:], ALU.mult, ALU.add).then_inc(wt_done, 1)

                def weights(j, u):
                    combine(j, u, 0)
                    combine(j, u, 1)
                    finish(j, u)

                def mul(j, c, t):
                    n = j * 2 * TB + c * TB + t
                    dve.wait_ge(rel_done, n + 1)
                    dve.scalar_tensor_tensor(rel[t % 2][:], ps_ring[3 + 2 * (t % 2)][:], hid_gain[:], rel[t % 2][:], ALU.mult, ALU.mult).then_inc(mul_done, 1)

                def h_lo(j, c, t):
                    n = j * 2 * TB + c * TB + t
                    dve.wait_ge(hidhi_done, n + 1)
                    dve.tensor_tensor(hid_lo[c][:, t * BANK:(t + 1) * BANK], rel[t % 2][:], hid_hi[c][:, t * BANK:(t + 1) * BANK],
                                      ALU.subtract).then_inc(hidlo_done, 1)

                def accumulate(j, n):
                    i, hf = n // HALVES, n % HALVES
                    dve.wait_ge(down_mm, j * 2 * TILES + n + 1)
                    dst = X[:, i, hf * BANK:(hf + 1) * BANK]
                    dve.scalar_tensor_tensor(dst, ps_ring[n % 6][:], ffn_gain[:], dst, ALU.mult, ALU.add).then_inc(acc_done, 1)

                dve.wait_ge(la_hi, 1)
                dve.scalar_tensor_tensor(lora_a[32:64], la_f[32:64], ab_scale[32:64, 0:1], lora_a[32:64], ALU.mult, ALU.subtract).then_inc(la_done, 1)
                lora_parts(0)
                for u in range(AHEAD):
                    weights(0, u)

                def outputs(j, first, count):
                    for n in range(first, first + count):
                        accumulate(j, n)

                def pair(j, more):
                    weights(j, AHEAD)
                    for t in range(TB):
                        mul(j, 0, t)
                        weights(j, AHEAD + 1 + t)
                        h_lo(j, 0, t)
                    for t in range(TB):
                        if t == 2 and more:
                            lora_parts(j + 1)
                        mul(j, 1, t)
                        if t < 2 or more:
                            weights(*unit_of_B(j, t))
                        h_lo(j, 1, t)
                    dve.wait_ge(acc_done, j * 2 * TILES + ACC_FIRST)
                    for s in range(4):
                        if more and s + 2 < AHEAD:
                            outputs(j, 8 * s, 3)
                            combine(j + 1, 2 + s, 0)
                            outputs(j, 8 * s + 3, 3)
                            combine(j + 1, 2 + s, 1)
                            outputs(j, 8 * s + 6, 2)
                            finish(j + 1, 2 + s)
                        else:
                            outputs(j, 8 * s, 8)

                with dve.Fori(0, PAIRS - 1) as j:
                    pair(j, True)
                pair(PAIRS - 1, False)

            @block.tensor
            def _(pe):
                def lora(j, u):
                    g = unit_no(j, u)
                    m, c, hf = units[u]
                    if u == 0:
                        pe.wait_ge(lb_done, j + 1)
                    if not (isinstance(g, int) and g < 2):
                        pe.wait_ge(wt_done, g - 1)
                    o = ps_lora[u % 2]
                    if m == 2:
                        mm = pe.matmul(o[:], lora_b[:, m, c * P:(c + 1) * P], lora_a[:, m, hf * BANK:(hf + 1) * BANK], start=True, stop=True)
                    else:
                        for k in range(KD // 2):
                            kk = hf * (KD // 2) + k
                            mm = pe.matmul(o[:, k * P:(k + 1) * P], lora_a[:, m, kk * P:(kk + 1) * P], lora_b[:, m, c * P:(c + 1) * P], start=True, stop=True)
                    mm.then_inc(lora_mm, 1)

                def up(j, c, t):
                    n = j * 2 * TB + c * TB + t
                    if t == 0:
                        pe.wait_ge(wlo_done, j * UNITS + 4 * c + 4)
                    if c == 0 and t < 2:
                        pe.wait_ge(acc_done, j * 2 * TILES - 4 + 2 * t + ACC_FIRST)
                    else:
                        pe.wait_ge(mul_done, n - 1)
                    ts = slice(t * BANK, (t + 1) * BANK)
                    for m in range(2):
                        o = ps_ring[2 + 2 * (t % 2) + m]
                        q = 0
                        for k in range(KD):
                            for w, xx in ((gu_hi, xT_hi), (gu_hi, xT_lo), (gu_lo, xT_hi)):
                                mm = pe.matmul(o[:], w[c][:, m, k, :], xx[:, k, ts], start=(q == 0), stop=(q == 3 * KD - 1))
                                q += 1
                    mm.then_inc(up_mm, 1)

                def down(j, n):
                    i, hf = n // HALVES, n % HALVES
                    if n == 0:
                        pe.wait_ge(wlo_done, j * UNITS + UNITS)
                    if n % (2 * TILES // TB) == 0:
                        pe.wait_ge(hidlo_done, j * 2 * TB + TB + n // (2 * TILES // TB) + 1)
                    if n < 2:
                        pe.wait_ge(acc_done, j * 2 * TILES - 2 + n + 1 + ACC_FIRST)
                    elif n < 6:
                        pe.wait_ge(mul_done, j * 2 * TB + 2 * TB - 2 + n // 2)
                    else:
                        pe.wait_ge(acc_done, j * 2 * TILES + n - 5 + ACC_FIRST)
                    q = 0
                    for c in range(2):
                        for hh, w in ((hid_hi, dn_hi), (hid_hi, dn_lo), (hid_lo, dn_hi)):
                            mm = pe.matmul(ps_ring[n % 6][:], hh[c][:, i * P:(i + 1) * P], w[c][:, hf * BANK:(hf + 1) * BANK],
                                           start=(q == 0), stop=(q == 5))
                            q += 1
                    mm.then_inc(down_mm, 1)

                pe.wait_ge(la_done, 1)
                for u in range(AHEAD):
                    lora(0, u)

                def pair(j, more):
                    lora(j, AHEAD)
                    for t in range(TB):
                        up(j, 0, t)
                        lora(j, AHEAD + 1 + t)
                    for t in range(TB):
                        up(j, 1, t)
                        if t < 2 or more:
                            lora(*unit_of_B(j, t))
                    for n in range(2 * TILES):
                        down(j, n)
                        if more and n % 8 == 7 and 2 + n // 8 < AHEAD:
                            lora(j + 1, 2 + n // 8)

                with pe.Fori(0, PAIRS - 1) as j:
                    pair(j, True)
                pair(PAIRS - 1, False)


def spectra():
    t, f = np.arange(L)[:, None], np.arange(P)[None, :]
    even, odd = 2 * np.pi * t * f / L, 2 * np.pi * t * (f + 0.5) / L
    nyquist = np.where(t % 2 == 0, 1.0, -1.0)
    im = -np.sin(even)
    im[:, :1] = nyquist
    odd_re, odd_im = np.cos(odd), -np.sin(odd)
    last = (t == L - 1)
    fwd = np.stack([np.stack([np.cos(even), im]), np.stack([odd_re, odd_im]),
                    np.stack([odd_re - last * odd_re.sum(0), odd_im - last * odd_im.sum(0)]),
                    np.stack([np.cos(even) + L * last * (f == 0), im])])
    weight = np.where(f == 0, 1.0, 2.0) / L
    im_inv = -np.sin(even) * weight
    im_inv[:, :1] = (nyquist - 1.0) / L
    inv = np.stack([np.cos(even) * weight, im_inv, odd_re * 2 / L, odd_im * 2 / L])
    return (fwd.reshape(4, 2, 2, P, P).transpose(3, 2, 0, 1, 4).astype(np.float32),
            inv.transpose(2, 0, 1).astype(np.float32))


def phase_autocorrelation(nc, io, res):
    settle = settler(res["passed"])
    X, ident, tg, mhalf = (res[k] for k in ("X", "ident", "tg", "mhalf"))
    CB = BANK
    CH = CB // P
    U = 4
    N = B * 2
    c_d = io["ctx"].rearrange("b (t p) n -> b p t n", p=P)
    with ExitStack() as ctx:
        def sb(name, shape, dt=F32):
            return ctx.enter_context(nc.sbuf_tensor(name, shape, dt))

        def sem(name):
            return ctx.enter_context(nc.semaphore("a_" + name))

        fwd, inv = sb("fwd", [P, 2, 4, 2, P]), sb("inv", [P, 4, L])
        half_gate = sb("half_gate", [P, 1])
        c_in = [sb(f"a_ctx{s}", [P, 2, D]) for s in range(2)]
        q = [sb(f"a_q{s}", [P, 2, D]) for s in range(2)]
        k_re, k_im, o_re, o_im = ([sb(f"{n}{s}", [P, CB]) for s in range(2)] for n in ("k_re", "k_im", "o_re", "o_im"))
        t_rr, t_ii, t_ir, t_ri = (sb(n, [P, CB]) for n in ("t_rr", "t_ii", "t_ir", "t_ri"))
        e_rr, e_ii, e_ri, e_ir = (sb(n, [P, CB]) for n in ("e_rr", "e_ii", "e_ri", "e_ir"))
        n_rr, n_ii, n_ri, n_ir = (sb(n, [P, CB]) for n in ("n_rr", "n_ii", "n_ri", "n_ir"))
        top8, next3 = sb("top8", [P, CH, 8]), sb("next3", [P, CH, 8])
        nmax, wsum, rws = sb("nmax", [P, CH]), sb("wsum", [P, CH]), sb("rws", [P, CH])
        cut, cut2, ex, wn = (sb(n, [P, CH, L]) for n in ("cut", "cut2", "ex", "wn"))
        wT = sb("wT", [P, 2, CB])
        st, mv, ve, rstd, nmr = sb("a_st", [P, 2, 12]), sb("a_mv", [P, 2, 2]), sb("a_ve", [P, 2]), sb("a_rstd", [P, 2]), sb("a_nmr", [P, 2])

        ps = [ctx.enter_context(nc.psum_tensor(f"a_ps{s}", [P, 2 * BANK], F32)) for s in range(4)]
        re, im = slice(0, CB), slice(CB, 2 * CB)

        const_in, gate_done = sem("const_in"), sem("gate_done")
        ctx_in = [sem(f"ctx_in{s}") for s in range(2)]
        stats_done, mv_done, ve_done, rstd_done, nmr_done, q_done = (sem(n) for n in ("stats_done", "mv_done", "ve_done", "rstd_done", "nmr_done", "q_done"))
        k_mm, u_mm, q_mm, k_done, u_done = (sem(n) for n in ("k_mm", "u_mm", "q_mm", "k_done", "u_done"))
        prod_done, prod_comb, prod_row, corr_mm = (sem(n) for n in ("prod_done", "prod_comb", "prod_row", "corr_mm"))
        top_done, cut_done, nmax_done, next_done, fill_done, cut2_done = (sem(n) for n in ("top_done", "cut_done", "nmax_done", "next_done", "fill_done", "cut2_done"))
        ex_done, w_done, rws_done, wn_done = (sem(n) for n in ("ex_done", "w_done", "rws_done", "wn_done"))
        wT_mm, wT_done, ws_mm, wprod_done, wprod_comb, out_mm, x_done = (sem(n) for n in ("wT_mm", "wT_done", "ws_mm", "wprod_done", "wprod_comb", "out_mm", "x_done"))
        wprod_row = sem("wprod_row")

        with nc.Block() as block:
            @block.sync
            def _(sp):
                sp.dma_start(fwd[:], io["fwd"]).then_inc(const_in, 16)
                sp.dma_start(inv[:], io["inv"]).then_inc(const_in, 16)
                for s in range(2):
                    sp.dma_start(c_in[s][:], c_d[s]).then_inc(ctx_in[s], 16)
                sp.dma_start(res["w1"][:], io["w1"]).then_inc(res["w1_in"], 16)
                with sp.Fori(1, B // 2) as m:
                    for s in range(2):
                        sp.wait_ge(out_mm, 4 * m - 2 + 2 * s + FIRST)
                        sp.dma_start(c_in[s][:], c_d[2 * m + s]).then_inc(ctx_in[s], 16)

            @block.gpsimd
            def _(pool):
                def rstd_of(batch):
                    pool.wait_ge(mv_done, 2 * batch + 2)
                    settle(pool)
                    pool.tensor_scalar(ve[:], mv[:, :, 1], EPS, None, ALU.add).then_inc(ve_done, 1)
                    pool.wait_ge(ve_done, batch + 1)
                    pool.tensor_tensor(rstd[:], ve[:], mhalf[:].to_broadcast([P, 2]), ALU.pow).then_inc(rstd_done, 1)

                def corr_comb(n):
                    for k, (a, b_, op) in enumerate(((t_rr, t_ii, ALU.add), (t_ir, t_ri, ALU.subtract))):
                        pool.wait_ge(prod_done, 4 * n + 2 * k + 2)
                        pool.tensor_tensor(a[:], a[:], b_[:], op).then_inc(prod_comb, 1)

                def out_comb(n):
                    for k, (a, b_, op) in enumerate(((e_rr, e_ii, ALU.add), (e_ri, e_ir, ALU.subtract), (n_rr, n_ii, ALU.add), (n_ri, n_ir, ALU.subtract))):
                        pool.wait_ge(wprod_done, 8 * n + 2 * k + 2 + FIRST)
                        pool.tensor_tensor(a[:], a[:], b_[:], op).then_inc(wprod_comb, 1)

                rstd_of(0)
                corr_comb(0)

                def units(m, more):
                    for r in range(U):
                        n = U * m + r
                        if r % 2 == 0 and (more or r == 0):
                            rstd_of(2 * m + r // 2 + 1)
                        if more or r < U - 1:
                            corr_comb(n + 1)
                        out_comb(n)

                with pool.Fori(0, N // U - 1) as m:
                    units(m, True)
                units(N // U - 1, False)

            @block.scalar
            def _(act):
                def q_norm(batch, s):
                    act.wait_ge(nmr_done, batch + 1)
                    settle(act)
                    for t in range(2):
                        act.activation(q[s][:, t, :], X[:, 2 * batch + t, :], ACT.Identity, scale=rstd[:, t:t + 1], bias=nmr[:, t:t + 1]).then_inc(q_done, 1)

                def spectra_out(n, par):
                    for mm, done, pair, dst in ((k_mm, k_done, 1, (k_re, k_im)), (u_mm, u_done, 2, (o_re, o_im))):
                        act.wait_ge(mm, n + 1)
                        for half, d in zip((re, im), dst):
                            act.activation(d[par][:], ps[pair][:, half], ACT.Copy).then_inc(done, 1)

                def weights(n):
                    act.wait_ge(nmax_done, n + 1)
                    for c in range(CH):
                        act.activation(ex[:, c, :], ps[3][:, c * L:(c + 1) * L], ACT.Exp, bias=nmax[:, c:c + 1]).then_inc(ex_done, 1)
                    act.wait_ge(rws_done, n + 1)
                    for c in range(CH):
                        act.activation(wn[:, c, :], cut2[:, c, :], ACT.Copy, scale=rws[:, c:c + 1]).then_inc(wn_done, 1)

                def weights_T(n):
                    act.wait_ge(wT_mm, n + 1)
                    act.activation(wT[:].rearrange("p h c -> p (h c)"), ps[3][:], ACT.Copy).then_inc(wT_done, 1)

                def corr_row(n):
                    act.wait_ge(prod_comb, 2 * n + 2)
                    act.activation(t_ir[0:1, :], t_ii[0:1, :], ACT.Copy).then_inc(prod_row, 1)

                def out_row(n):
                    act.wait_ge(wprod_comb, 4 * n + 2)
                    act.activation(e_ri[0:1, :], e_ii[0:1, :], ACT.Copy).then_inc(wprod_row, 1)

                q_norm(0, 0)
                spectra_out(0, 0)
                corr_row(0)
                weights(0)

                def units(m, more):
                    for r in range(U):
                        n = U * m + r
                        nxt = more or r < U - 1
                        if r % 2 == 0 and (more or r == 0):
                            q_norm(2 * m + r // 2 + 1, (r // 2 + 1) % 2)
                        if nxt:
                            spectra_out(n + 1, (r + 1) % 2)
                        weights_T(n)
                        if nxt:
                            corr_row(n + 1)
                        out_row(n)
                        if nxt:
                            weights(n + 1)

                with act.Fori(0, N // U - 1) as m:
                    units(m, True)
                units(N // U - 1, False)

            @block.tensor
            def _(pe):
                pe.sem_inc(out_mm, FIRST)

                def dft(pair, half, kind, src, start=True):
                    for t in range(2):
                        mm = pe.matmul(ps[pair][:, half], fwd[:, t, kind, 0 if half is re else 1, :], src(t), start=(t == 0), stop=(t == 1))
                    return mm

                def spectra_in(n, batch, r, first=False):
                    s, cb = (r // 2) % 2, r % 2
                    cs = slice(cb * CB, (cb + 1) * CB)
                    if cb == 0:
                        pe.wait_ge(ctx_in[s], 16 * (batch // 2 + 1) if isinstance(batch, int) else 16 * first)
                    if not (isinstance(n, int) and n == 0):
                        pe.wait_ge(k_done, 2 * n)
                        pe.wait_ge(u_done, 2 * n)
                        pe.wait_ge(wprod_done, 8 * n - 8 + FIRST)
                    for half in (re, im):
                        mm = dft(1, half, 3, lambda t: c_in[s][:, t, cs])
                    mm.then_inc(k_mm, 1)
                    for half in (re, im):
                        mm = dft(2, half, 2, lambda t: c_in[s][:, t, cs])
                    mm.then_inc(u_mm, 1)

                def q_spectrum(n, batch, r):
                    s, cb = (r // 2) % 2, r % 2
                    cs = slice(cb * CB, (cb + 1) * CB)
                    if cb == 0:
                        pe.wait_ge(q_done, 2 * batch + 2)
                    if not (isinstance(n, int) and n < 2):
                        pe.wait_ge(x_done, 2 * n - 2 + FIRST)
                    for half in (re, im):
                        mm = dft(0, half, 0, lambda t: q[s][:, t, cs])
                    mm.then_inc(q_mm, 1)

                def corr(n):
                    pe.wait_ge(prod_comb, 2 * n + 2)
                    pe.wait_ge(prod_row, n + 1)
                    if not (isinstance(n, int) and n == 0):
                        pe.wait_ge(wT_done, n)
                    for c in range(CH):
                        for k, src in enumerate((t_rr, t_ir)):
                            mm = pe.matmul(ps[3][:, c * L:(c + 1) * L], src[:, c * P:(c + 1) * P], inv[:, k, :], start=(k == 0), stop=(k == 1))
                    mm.then_inc(corr_mm, 1)

                def weight_turn(n):
                    pe.wait_ge(wn_done, CH * n + CH)
                    for h in range(2):
                        for c in range(CH):
                            mm = pe.transpose(ps[3][:, h * CB + c * P:h * CB + (c + 1) * P], wn[:, c, h * P:(h + 1) * P], ident[:])
                    mm.then_inc(wT_mm, 1)

                def weight_dfts(n, nxt):
                    pe.wait_ge(wT_done, n + 1)
                    pe.wait_ge(k_done, 2 * n + (4 if nxt else 2))
                    for half in (re, im):
                        dft(1, half, 0, lambda t: wT[:, t, :])
                    pe.wait_ge(u_done, 2 * n + (4 if nxt else 2))
                    for half in (re, im):
                        mm = dft(2, half, 1, lambda t: wT[:, t, :])
                    mm.then_inc(ws_mm, 1)

                def output(n, nxt):
                    pe.wait_ge(prod_done, 4 * n + (8 if nxt else 4))
                    pe.wait_ge(wprod_row, n + 1)
                    for first in (0, 2):
                        pe.wait_ge(wprod_comb, 4 * n + first + 2)
                        for t in range(2):
                            for k in (first, first + 1):
                                mm = pe.matmul(ps[0][:, t * CB:(t + 1) * CB], inv[:, k, t * P:(t + 1) * P], (e_rr, e_ri, n_rr, n_ri)[k][:],
                                               start=(k == 0), stop=(k == 3))
                    mm.then_inc(out_mm, 1)

                pe.wait_ge(const_in, 32)
                spectra_in(0, 0, 0)
                q_spectrum(0, 0, 0)
                corr(0)

                def units(m, more):
                    for r in range(U):
                        n = U * m + r
                        nxt = more or r < U - 1
                        if nxt:
                            r1 = (r + 1) % U
                            batch = 2 * m + (r + 1) // 2
                            spectra_in(n + 1, batch, r1, first=(m + 1 if r < U - 1 else m + 2))
                        weight_turn(n)
                        if nxt:
                            q_spectrum(n + 1, batch, r1)
                        weight_dfts(n, nxt)
                        if nxt:
                            corr(n + 1)
                        output(n, nxt)

                with pe.Fori(0, N // U - 1) as m:
                    units(m, True)
                units(N // U - 1, False)

            @block.vector
            def _(dve):
                for used in (wprod_done, x_done):
                    dve.sem_inc(used, FIRST)
                def stats(batch):
                    for t in range(2):
                        if not (isinstance(batch, int) and batch == 0):
                            dve.wait_ge(nmr_done, batch)
                        settle(dve)
                        for h in range(2):
                            dve.bn_stats(st[:, t, 6 * h:6 * h + 6], X[:, 2 * batch + t, h * BANK:(h + 1) * BANK]).then_inc(stats_done, 1)
                    for t in range(2):
                        dve.wait_ge(stats_done, 4 * batch + 2 * t + 2)
                        if t == 0 and not (isinstance(batch, int) and batch == 0):
                            dve.wait_ge(q_done, 2 * batch)
                        settle(dve)
                        dve.bn_aggr(mv[:, t, :], st[:, t, :]).then_inc(mv_done, 1)

                def offset(batch):
                    dve.wait_ge(rstd_done, batch + 1)
                    dve.wait_ge(mv_done, 2 * batch + 2)
                    dve.scalar_tensor_tensor(nmr[:], mv[:, :, 0], -1.0, rstd[:], ALU.mult, ALU.mult).then_inc(nmr_done, 1)

                def products(n, par):
                    dve.wait_ge(q_mm, n + 1)
                    dve.wait_ge(k_done, 2 * n + 2)
                    if not (isinstance(n, int) and n == 0):
                        dve.wait_ge(corr_mm, n)
                    for dst, a, b_ in ((t_rr, re, k_re), (t_ii, im, k_im), (t_ir, im, k_re), (t_ri, re, k_im)):
                        dve.tensor_tensor(dst[:], ps[0][:, a], b_[par][:], ALU.mult).then_inc(prod_done, 1)

                def select(n):
                    dve.wait_ge(corr_mm, n + 1)
                    settle(dve)
                    row = [ps[3][:, c * L:(c + 1) * L] for c in range(CH)]
                    for c in range(CH):
                        dve.max(top8[:, c, :], row[c]).then_inc(top_done, 1)
                    for c in range(CH):
                        dve.wait_ge(top_done, CH * n + c + 1)
                        if c == 0:
                            dve.wait_ge(next_done, CH * n)
                        settle(dve)
                        dve.match_replace(cut[:, c, :], top8[:, c, :], row[c], -BIG).then_inc(cut_done, 1)
                    dve.wait_ge(top_done, CH * n + CH)
                    dve.tensor_scalar(nmax[:], top8[:, :, 0], -1.0, None, ALU.mult).then_inc(nmax_done, 1)
                    for c in range(CH):
                        dve.wait_ge(cut_done, CH * n + c + 1)
                        settle(dve)
                        dve.max(next3[:, c, :], cut[:, c, :]).then_inc(next_done, 1)
                    dve.wait_ge(next_done, CH * n + CH)
                    dve.memset(next3[:, :, TOPK - 8:8], -BIG).then_inc(fill_done, 1)
                    dve.wait_ge(fill_done, n + 1)
                    dve.wait_ge(wn_done, CH * n)
                    settle(dve)
                    for c in range(CH):
                        dve.match_replace(cut2[:, c, :], next3[:, c, :], cut[:, c, :], -BIG).then_inc(cut2_done, 1)
                    for c in range(CH):
                        dve.wait_ge(cut2_done, CH * n + c + 1)
                        dve.wait_ge(ex_done, CH * n + c + 1)
                        dve.scalar_tensor_tensor(cut2[:, c, :], cut2[:, c, :], -0.5 * BIG, ex[:, c, :], ALU.is_le, ALU.mult,
                                                 accum_out=wsum[:, c:c + 1]).then_inc(w_done, 1)
                    dve.wait_ge(w_done, CH * n + CH)
                    dve.reciprocal(rws[:], wsum[:]).then_inc(rws_done, 1)

                def weight_products(n, par):
                    dve.wait_ge(ws_mm, n + 1)
                    if not (isinstance(n, int) and n == 0):
                        dve.wait_ge(out_mm, n + FIRST)
                    for dst, pair, a, b_ in ((e_rr, 1, re, k_re), (e_ii, 1, im, k_im), (e_ri, 1, re, k_im), (e_ir, 1, im, k_re),
                                             (n_rr, 2, re, o_re), (n_ii, 2, im, o_im), (n_ri, 2, re, o_im), (n_ir, 2, im, o_re)):
                        dve.tensor_tensor(dst[:], ps[pair][:, a], b_[par][:], ALU.mult).then_inc(wprod_done, 1)

                def add(n, m, r):
                    cb = r % 2
                    dve.wait_ge(out_mm, n + 1 + FIRST)
                    for t in range(2):
                        dst = X[:, U * m + 2 * (r // 2) + t, cb * CB:(cb + 1) * CB]
                        dve.scalar_tensor_tensor(dst, ps[0][:, t * CB:(t + 1) * CB], half_gate[:], dst, ALU.mult, ALU.add).then_inc(x_done, 1)

                dve.tensor_scalar(half_gate[:], tg[:, 1:2], 0.5, None, ALU.mult).then_inc(gate_done, 1)
                stats(0)
                offset(0)
                products(0, 0)
                select(0)
                dve.wait_ge(gate_done, 1)

                def units(m, more):
                    for r in range(U):
                        n = U * m + r
                        nxt = more or r < U - 1
                        if r % 2 == 0 and (more or r == 0):
                            stats(2 * m + r // 2 + 1)
                            offset(2 * m + r // 2 + 1)
                        if nxt:
                            products(n + 1, (r + 1) % 2)
                        weight_products(n, r % 2)
                        if nxt:
                            select(n + 1)
                        add(n, m, r)

                with dve.Fori(0, N // U - 1) as m:
                    units(m, True)
                units(N // U - 1, False)


def phase_dora_linear(nc, io, res):
    settle = settler(res["passed"])
    X, ident, tg, mhalf, E, w_in, stored = (res[k] for k in ("X", "ident", "tg", "mhalf", "w1", "w1_in", "stored"))
    out_d = io["out"].rearrange("b (h p) n -> b h p n", p=P)
    with ExitStack() as ctx:
        def sb(name, shape, dt=F32):
            return ctx.enter_context(nc.sbuf_tensor("d_" + name, shape, dt))

        def sb2(name, shape, dt=F32):
            return [sb(f"{name}{h}", shape, dt) for h in range(2)]

        def sem(name):
            return ctx.enter_context(nc.semaphore("d_" + name))

        def sem2(name):
            return [sem(f"{name}{h}") for h in range(2)]

        sq = sb("sq", [P, D])
        w_hi, w_lo = sb("w_hi", [P, KD, D], HALF), sb("w_lo", [P, KD, D], HALF)
        la, lb = sb("la", [P, D]), sb("lb", [P, D])
        mag, norm2, rnorm, gain = sb("mag", [P, KD]), sb("norm2", [P, KD]), sb("rnorm", [P, KD]), sb("gain", [P, KD])
        gain_row = sb("gain_row", [P, D])
        st, mv, ve, rstd, nmr = sb2("st", [P, 12]), sb2("mv", [P, 2]), sb2("ve", [P, 1]), sb2("rstd", [P, 1]), sb2("nmr", [P, 1])
        xn, x_hi, x_lo, prod = sb2("xn", [P, D]), sb2("x_hi", [P, D], HALF), sb2("x_lo", [P, D], HALF), sb2("prod", [P, D])
        psT = [ctx.enter_context(nc.psum_tensor(f"d_psT{h}", [P, D], F32)) for h in range(2)]
        psO = [ctx.enter_context(nc.psum_tensor(f"d_psO{h}", [P, D], F32)) for h in range(2)]

        small_in = sem("small_in")
        lora_mm, E_done, norm_done, rnorm_done, scaled = (sem(n) for n in ("lora_mm", "E_done", "norm_done", "rnorm_done", "scaled"))
        wT_mm, whi_done, wlo_done, gain_done, row_mm, row_done = (sem(n) for n in ("wT_mm", "whi_done", "wlo_done", "gain_done", "row_mm", "row_done"))
        stats_done, mv_done, ve_done, rstd_done, nmr_done, xn_done, hi_done = (
            sem(n) for n in ("stats_done", "mv_done", "ve_done", "rstd_done", "nmr_done", "xn_done", "hi_done"))
        T_mm, lo_done, out_mm, prod_done, x_done = (sem2(n) for n in ("T_mm", "lo_done", "out_mm", "prod_done", "x_done"))

        def following(b, h, steps):
            return b + (h + steps) // 2, (h + steps) % 2

        with nc.Block() as block:
            @block.sync
            def _(sp):
                for dst, name in ((la, "lora1_a"), (lb, "lora1_b"), (mag, "mag")):
                    sp.dma_start(dst[:], io[name]).then_inc(small_in, 16)
                with sp.Fori(0, B) as b:
                    for h in range(2):
                        sp.wait_ge(x_done[h], 2 * b + 2)
                        sp.dma_start(out_d[b, h], X[:, 2 * b + h, :]).then_inc(stored, 16)
                sp.wait_ge(stored, 16 * TILES)

            @block.gpsimd
            def _(pool):
                def rstd_of(b, h):
                    pool.wait_ge(mv_done, 2 * b + h + 1)
                    settle(pool)
                    pool.tensor_scalar(ve[h][:], mv[h][:, 1:2], EPS, None, ALU.add).then_inc(ve_done, 1)
                    pool.wait_ge(ve_done, 2 * b + h + 1)
                    pool.tensor_tensor(rstd[h][:], ve[h][:], mhalf[:], ALU.pow).then_inc(rstd_done, 1)

                for h in range(2):
                    rstd_of(0, h)
                for o in range(KD):
                    pool.wait_ge(norm_done, o + 1)
                    pool.tensor_tensor(rnorm[:, o:o + 1], norm2[:, o:o + 1], mhalf[:], ALU.pow).then_inc(rnorm_done, 1)
                with pool.Fori(1, B) as b:
                    for h in range(2):
                        rstd_of(b, h)

            @block.scalar
            def _(act):
                def normed(b, h):
                    act.wait_ge(T_mm[h], b + FIRST)
                    act.wait_ge(nmr_done, 2 * b + h + 1)
                    settle(act)
                    act.activation(xn[h][:], X[:, 2 * b + h, :], ACT.Identity, scale=rstd[h][:], bias=nmr[h][:]).then_inc(xn_done, 1)

                def high(b, h):
                    act.wait_ge(out_mm[h], 2 * b + FIRST)
                    act.wait_ge(T_mm[h], b + 1 + FIRST)
                    act.activation(x_hi[h][:], psT[h][:], ACT.Copy, scale=LN_SCALE).then_inc(hi_done, 1)

                for h in range(2):
                    normed(0, h)
                for o in range(KD + 1):
                    if o < KD:
                        act.wait_ge(E_done, o + 1)
                        if o:
                            act.wait_ge(norm_done, o)
                        act.activation(sq[:], E[:, o, :], ACT.Square, accum_out=norm2[:, o:o + 1]).then_inc(norm_done, 1)
                    if o >= 1:
                        act.wait_ge(wT_mm, o)
                        act.activation(w_hi[:, :, (o - 1) * P:o * P], psT[(o - 1) % 2][:].rearrange("p (k t) -> p k t", k=KD),
                                       ACT.Copy, scale=W_SCALE).then_inc(whi_done, 1)

                def batch(b, more):
                    for h in range(2):
                        if more or h == 0:
                            high(*following(b, h, 1))
                        if more:
                            normed(*following(b, h, 2))

                high(0, 0)
                with act.Fori(0, B - 1) as b:
                    batch(b, True)
                batch(B - 1, False)

            @block.tensor
            def _(pe):
                for used in (*T_mm, *out_mm):
                    pe.sem_inc(used, FIRST)
                pe.wait_ge(small_in, 48)
                for o in range(KD + 1):
                    if o < KD:
                        if o >= 2:
                            pe.wait_ge(E_done, o - 1)
                        for n in range(2):
                            mm = pe.matmul(psO[o % 2][:, n * BANK:(n + 1) * BANK], lb[:, o * P:(o + 1) * P], la[:, n * BANK:(n + 1) * BANK], start=True, stop=True)
                        mm.then_inc(lora_mm, 1)
                    if o >= 1:
                        pe.wait_ge(scaled, o)
                        if o >= 3:
                            pe.wait_ge(wlo_done, o - 2)
                        for k in range(KD):
                            mm = pe.transpose(psT[(o - 1) % 2][:, k * P:(k + 1) * P], E[:, o - 1, k * P:(k + 1) * P], ident[:])
                        mm.then_inc(wT_mm, 1)
                pe.wait_ge(E_done, KD)
                pe.wait_ge(gain_done, 1)
                for o in range(KD):
                    mm = pe.matmul(psO[1][:, o * P:(o + 1) * P], gain[:, o:o + 1].to_broadcast([P, P]), ident[:], start=True, stop=True)
                mm.then_inc(row_mm, 1)

                def turn(b, h):
                    pe.wait_ge(xn_done, 2 * b + h + 1)
                    pe.wait_ge(lo_done[h], b + FIRST)
                    for k in range(KD):
                        mm = pe.transpose(psT[h][:, k * P:(k + 1) * P], xn[h][:, k * P:(k + 1) * P], ident[:])
                    mm.then_inc(T_mm[h], 1)

                def linear(b, h):
                    pe.wait_ge(lo_done[h], b + 1 + FIRST)
                    pe.wait_ge(prod_done[h], 2 * b + FIRST)
                    for n in range(2):
                        cols = slice(n * BANK, (n + 1) * BANK)
                        q = 0
                        for k in range(KD):
                            ks = slice(k * P, (k + 1) * P)
                            for a, w in ((x_hi, w_hi), (x_hi, w_lo), (x_lo, w_hi)):
                                mm = pe.matmul(psO[h][:, cols], a[h][:, ks], w[:, k, cols], start=(q == 0), stop=(q == 3 * KD - 1))
                                q += 1
                        mm.then_inc(out_mm[h], 1)

                def batch(b, more):
                    for h in range(2):
                        if more or h == 0:
                            turn(*following(b, h, 1))
                        linear(b, h)

                pe.wait_ge(wlo_done, KD)
                turn(0, 0)
                pe.wait_ge(row_done, 1)
                with pe.Fori(0, B - 1) as b:
                    batch(b, True)
                batch(B - 1, False)

            @block.vector
            def _(dve):
                for used in (*lo_done, *prod_done):
                    dve.sem_inc(used, FIRST)

                def stats(b, h):
                    settle(dve)
                    for n in range(2):
                        dve.bn_stats(st[h][:, 6 * n:6 * n + 6], X[:, 2 * b + h, n * BANK:(n + 1) * BANK]).then_inc(stats_done, 1)
                    dve.wait_ge(stats_done, 4 * b + 2 * h + 2)
                    settle(dve)
                    dve.bn_aggr(mv[h][:], st[h][:]).then_inc(mv_done, 1)
                    dve.wait_ge(rstd_done, 2 * b + h + 1)
                    dve.scalar_tensor_tensor(nmr[h][:], mv[h][:, 0:1], -1.0, rstd[h][:], ALU.mult, ALU.mult).then_inc(nmr_done, 1)

                def low(b, h):
                    dve.wait_ge(hi_done, 2 * b + h + 1)
                    dve.scalar_tensor_tensor(x_lo[h][:], psT[h][:], LN_SCALE, x_hi[h][:], ALU.mult, ALU.subtract).then_inc(lo_done[h], 1)

                def add(b, h):
                    for n in range(2):
                        cols = slice(n * BANK, (n + 1) * BANK)
                        dve.wait_ge(out_mm[h], 2 * b + n + 1 + FIRST)
                        dve.tensor_tensor(prod[h][:, cols], psO[h][:, cols], gain_row[:, cols], ALU.mult).then_inc(prod_done[h], 1)
                    for n in range(2):
                        cols = slice(n * BANK, (n + 1) * BANK)
                        dve.wait_ge(prod_done[h], 2 * b + n + 1 + FIRST)
                        dve.tensor_tensor(X[:, 2 * b + h, cols], X[:, 2 * b + h, cols], prod[h][:, cols], ALU.add).then_inc(x_done[h], 1)

                for h in range(2):
                    stats(0, h)
                dve.wait_ge(small_in, 48)
                dve.tensor_scalar(gain[:], mag[:], tg[:, 3:4], 1.0 / (W_SCALE * LN_SCALE), ALU.mult, ALU.mult).then_inc(gain_done, 1)
                dve.wait_ge(w_in, 16)
                for o in range(KD + 2):
                    if o < KD:
                        dve.wait_ge(lora_mm, o + 1)
                        dve.tensor_tensor(E[:, o, :], E[:, o, :], psO[o % 2][:], ALU.add).then_inc(E_done, 1)
                    if 1 <= o <= KD:
                        dve.wait_ge(rnorm_done, o)
                        dve.tensor_scalar(E[:, o - 1, :], E[:, o - 1, :], rnorm[:, o - 1:o], None, ALU.mult).then_inc(scaled, 1)
                    if o >= 2:
                        dve.wait_ge(whi_done, o - 1)
                        cols = slice((o - 2) * P, (o - 1) * P)
                        dve.scalar_tensor_tensor(w_lo[:, :, cols], psT[(o - 2) % 2][:].rearrange("p (k t) -> p k t", k=KD), W_SCALE,
                                                 w_hi[:, :, cols], ALU.mult, ALU.subtract).then_inc(wlo_done, 1)
                dve.wait_ge(row_mm, 1)
                dve.tensor_copy(gain_row[:], psO[1][:]).then_inc(row_done, 1)

                def batch(b, more):
                    for h in range(2):
                        if more or h == 0:
                            low(*following(b, h, 1))
                        if more:
                            stats(*following(b, h, 2))
                        add(b, h)

                low(0, 0)
                dve.wait_ge(row_done, 1)
                with dve.Fori(0, B - 1) as b:
                    batch(b, True)
                batch(B - 1, False)


def build(nc, io):
    with ExitStack() as ctx:
        def sb(name, shape, dt=F32):
            return ctx.enter_context(nc.sbuf_tensor(name, shape, dt))
        res = {"X": sb("X", [P, TILES, D]), "ident": sb("ident", [P, P]), "blk": sb("blk", [P, P]),
               "tg": sb("tg", [P, 4]), "gates": sb("gates", [P, 4]), "mhalf": sb("mhalf", [P, 1])}
        res["passed"] = ctx.enter_context(nc.semaphore("passed"))
        res["stored"] = ctx.enter_context(nc.semaphore("stored"))
        res["x_in"] = [ctx.enter_context(nc.semaphore(f"x_in{h}")) for h in range(2)]
        for name, n in (("w_scale", 3), ("ab_scale", 2), ("lora_gain", 3), ("hid_gain", 1), ("ffn_gain", 1)):
            res[name] = sb(name, [P, n])
        phase_prepare(nc, io, res)
        with ExitStack() as inner:
            res["xT_hi"] = inner.enter_context(nc.sbuf_tensor("xT_hi", [P, KD, B * L], HALF))
            res["xT_lo"] = inner.enter_context(nc.sbuf_tensor("xT_lo", [P, KD, B * L], HALF))
            phase_linear_attention(nc, io, res)
            phase_nf4_ffn(nc, io, res)
        res["w1"], res["w1_in"] = sb("w1", [P, KD, D]), ctx.enter_context(nc.semaphore("w1_in"))
        phase_autocorrelation(nc, io, res)
        phase_dora_linear(nc, io, res)


def layouts(inputs):
    a = {k: np.asarray(v) for k, v in inputs.items()}
    padf = DFF_PAD - DFF
    kk = KD // 2
    units = pack_units()
    codes = np.zeros((PAIRS, UNITS, P, BANK), np.int32)
    absmax = np.zeros((PAIRS, UNITS, 2, BANK), np.float32)
    gate_up, absmax_of = [], []
    for m in ("g", "u"):
        c = np.pad(a[f"L0_ffn_{m}_codes"], ((0, padf), (0, 0)))
        s = np.pad(a[f"L0_ffn_{m}_absmax"], ((0, padf), (0, 0)))
        absmax_of.append(s)
        gate_up.append((c.reshape(PAIRS, 2, P, 2, kk, P), s.reshape(PAIRS, 2, P, 2, kk, 2)))
    dc = np.pad(a["L0_ffn_d_codes"], ((0, 0), (0, padf))).reshape(2, BANK, PAIRS, 2, P)
    ds = np.pad(a["L0_ffn_d_absmax"], ((0, 0), (0, padf // QBLK))).reshape(2, BANK, PAIRS, 2, 2)
    for u, (m, c, hf) in enumerate(units):
        if m < 2:
            cc, ss = gate_up[m]
            codes[:, u] = cc[:, c, :, hf].transpose(0, 3, 2, 1).reshape(PAIRS, P, BANK)
            absmax[:, u] = ss[:, c, :, hf].transpose(0, 3, 2, 1).reshape(PAIRS, 2, BANK)
        else:
            codes[:, u] = dc[hf, :, :, c].transpose(1, 2, 0)
            absmax[:, u] = ds[hf, :, :, c].transpose(1, 2, 0)
    lora_a = np.zeros((96, 3, D), np.float32)
    lora_b = np.zeros((PAIRS, 96, 3, PAIR), np.float32)
    bound_a, bound_b = np.zeros((P, 3, KD, R0), np.float32), np.zeros((P, 3, DFF_PAD // P, R0), np.float32)
    for m, name in enumerate(("g", "u", "d")):
        la, lb = a[f"L0_ffn_{name}_lora_a"], a[f"L0_ffn_{name}_lora_b"]
        wide, long = (la.T, lb) if m < 2 else (lb, la.T)
        long = np.pad(long, ((0, 0), (0, padf)))
        bound_a[:, m] = wide.T.reshape(KD, P, R0).transpose(1, 0, 2)
        bound_b[:, m] = long.T.reshape(-1, P, R0).transpose(1, 0, 2)
        long = long.reshape(R0, PAIRS, PAIR).transpose(1, 0, 2)
        for g in range(3):
            lora_a[32 * g:32 * g + R0, m] = wide
            lora_b[:, 32 * g:32 * g + R0, m] = long
    bound_q = np.stack([s.reshape(P, -1) for s in (*absmax_of, np.pad(a["L0_ffn_d_absmax"], ((0, 0), (0, padf // QBLK))))], 1)
    fwd, inv = spectra()
    lora1_a, lora1_b = np.zeros((P, D), np.float32), np.zeros((P, D), np.float32)
    lora1_a[:R1], lora1_b[:R1] = a["L1_ffn_lora_A"], a["L1_ffn_lora_B"].T
    arrays = {
        "bound_q": bound_q, "bound_a": bound_a, "bound_b": bound_b,
        "lora1_a": lora1_a, "lora1_b": lora1_b, "mag": a["L1_ffn_magnitude"].reshape(KD, P).T,
        "w1": a["L1_ffn_W"].reshape(KD, P, D).transpose(1, 0, 2),
        "fwd": fwd, "inv": inv,
        "x": a["x"], "ctx": a["ctx_4096"],
        "ctxT": a["ctx_4096"].reshape(B, 2, P, KD, P).transpose(0, 1, 4, 3, 2).reshape(B, 2, P, D), "g_xattn": a["g_xattn"], "g_ffn": a["g_ffn"],
        "ident": np.eye(P, dtype=np.float32), "blk": np.kron(np.eye(P // ROWS0), np.ones((ROWS0, ROWS0))).astype(np.float32),
        "codes": codes, "absmax": absmax, "lora_a": lora_a, "lora_b": lora_b,
    }
    return {k: np.ascontiguousarray(v) for k, v in arrays.items()}


def kernel(**inputs):
    import concourse.bacc as bacc
    from concourse.bass_utils import run_bass_kernel_spmd

    nc = bacc.Bacc("TRN2", target_bir_lowering=False, num_devices=1, dynamic_dma_scratch_size=2048)
    arrays, io = {}, {}
    for name, arr in layouts(inputs).items():
        arrays[f"in_{name}"] = arr
        io[name] = nc.dram_tensor(f"in_{name}", arr.shape, mybir.dt.from_np(arr.dtype), kind="ExternalInput").ap()
    io["out"] = nc.dram_tensor("out_0", (B, L, D), F32, kind="ExternalOutput").ap()
    build(nc, io)
    r = run_bass_kernel_spmd(nc, [arrays], core_ids=[0])
    return r.results[0]["out_0"]
```

```python
from contextlib import ExitStack

import numpy as np

import concourse.bass as bass
from concourse import mybir

F32 = mybir.dt.float32
I32 = mybir.dt.int32
HALF = mybir.dt.float16
ALU = mybir.AluOpType
ACT = mybir.ActivationFunctionType
AX = mybir.AxisListType

P = 128
B, L, D = 8, 256, 1024
TILES = B * L // P
KD = D // P
BANK = 512
EPS = 1e-5
DFF, R0 = 2752, 16
PAIR = 2 * P
PAIRS = -(-DFF // PAIR)
DFF_PAD = PAIRS * PAIR
QBLK = 64
HEADS0 = 8
ROWS0 = L // HEADS0
TOPK = int(2 * np.log(L))
R1 = 32
HALVES = 2
UNITS = 12
TB = B * L // BANK
BIG = 3.0e38
W_SCALE = 2.0 ** 12
LN_SCALE = 2.0 ** 6
DFT_SCALE, TOP_SCALE = 2.0 ** 8, 2.0 ** 14
WMAX, ABMAX, HMAX = 2.0 ** 13, 2.0 ** 13, 2.0 ** 15

NF4 = [-1.0, -0.6961928009986877, -0.5250730514526367, -0.39491748809814453, -0.28444138169288635,
       -0.18477343022823334, -0.09105003625154495, 0.0, 0.07958029955625534, 0.16093020141124725,
       0.2461123019456863, 0.33791524171829224, 0.44070982933044434, 0.5626170039176941,
       0.7229568362236023, 1.0]


def nf4_lines():
    out = []
    for j in (4, 5, 6, 7, 0, 1, 2, 3):
        s = NF4[2 * j + 1] - NF4[2 * j]
        o = NF4[2 * j] - 2 * j * s
        out.append((s, o) if j >= 4 else (-s, -o))
    return out


def pack_units():
    units = [(m, c, hf) for c in range(2) for m in (0, 1) for hf in range(2)]
    return units + [(2, c, hf) for c in range(2) for hf in range(2)]


LAST = DFF % P
assert LAST == P // 2 and PAIRS * 2 * P - DFF == P - LAST


FIRST = 1


def settler(passed):
    def settle(engine):
        engine.sem_inc(passed, 1)
    return settle


def ffn_scales(nc, ctx, io, res, ps, const_set, tanh_done):
    ident, tg = res["ident"], res["tg"]
    NQ, NA, NB = io["bound_q"].shape[-1], KD, DFF_PAD // P
    TINY = 1e-30

    def sb(name, shape, dt=F32):
        return ctx.enter_context(nc.sbuf_tensor("p_" + name, shape, dt))

    def sem(name):
        return ctx.enter_context(nc.semaphore("p_" + name))

    q, a, b = sb("q", [P, 3, NQ]), sb("a", [P, 3, NA, R0]), sb("b", [P, 3, NB, R0])
    a_rows, b_cols = sb("a_rows", [P, 3, NA]), sb("b_cols", [P, 3, NB])
    own, every, norms = sb("own", [P, 12]), sb("every", [P, 12]), sb("norms", [P, 12])
    top, diag = sb("top", [9, 1]), sb("diag", [9, 9])
    ones, half = res["ones"], res["half"]
    M, N, rM, rN, ab, rab, abp, ratio, nn = (sb(n, [P, k]) for n, k in (
        ("M", 3), ("N", 3), ("rM", 3), ("rN", 3), ("ab", 2), ("rab", 2), ("abp", 1), ("ratio", 3), ("nn", 1)))
    ps_top, ps_all = ps[0:9, 0:P], ps[:, BANK:BANK + 12]
    bound_in = sem("bound_in")
    squared, step, top_mm, all_mm, norms_done = (sem(n) for n in ("squared", "step", "top_mm", "all_mm", "norms_done"))
    OWN, DIAG, EVERY = 6, 8, 9

    def sp_part(sp):
        for dst, name in ((q, "bound_q"), (a, "bound_a"), (b, "bound_b")):
            sp.dma_start(dst[:], io[name]).then_inc(bound_in, 16)

    def pool_part(pool, i):
        if i == TILES:
            pool.wait_ge(step, EVERY)
            pool.tensor_tensor(norms[:], every[:], half[:].to_broadcast([P, 12]), ALU.pow).then_inc(norms_done, 1)

    def act_part(act, i):
        if i == TILES - 2:
            act.wait_ge(bound_in, 48)
            for t in (q, a, b):
                act.activation(t[:], t[:], ACT.Square).then_inc(squared, 1)

    def pe_part(pe, i):
        if i == TILES:
            pe.wait_ge(step, OWN)
            pe.matmul(ps_top, own[:, 0:9], ident[:], start=True, stop=True).then_inc(top_mm, 1)
            pe.wait_ge(const_set, 3)
            pe.matmul(ps_all[:, 9:12], ones[:], own[:, 9:12], start=True, stop=True)
            pe.wait_ge(step, DIAG)
            pe.matmul(ps_all[:, 0:9], ones[0:9, :], diag[:], start=True, stop=True).then_inc(all_mm, 1)

    def dve_part(dve, i):
        if i == TILES - 1:
            dve.wait_ge(squared, 3)
            dve.reduce_max(own[:, 0:3], q[:], AX.X).then_inc(step, 1)
            dve.reduce_sum(a_rows[:], a[:], AX.X).then_inc(step, 1)
            dve.reduce_sum(b_cols[:], b[:], AX.X).then_inc(step, 1)
            dve.wait_ge(step, 3)
            dve.reduce_max(own[:, 3:6], a_rows[:], AX.X).then_inc(step, 1)
            dve.reduce_max(own[:, 6:9], b_cols[:], AX.X).then_inc(step, 1)
            dve.reduce_sum(own[:, 9:12], a_rows[:], AX.X).then_inc(step, 1)
        if i == TILES:
            dve.wait_ge(top_mm, 1)
            dve.reduce_max(top[:], ps_top, AX.X).then_inc(step, 1)
            dve.wait_ge(step, 7)
            dve.tensor_scalar(diag[:], ident[0:9, 0:9], top[:], None, ALU.mult).then_inc(step, 1)
            dve.wait_ge(all_mm, 1)
            dve.tensor_copy(every[:], ps_all).then_inc(step, 1)
        if i == TILES + 1:
            dve.wait_ge(norms_done, 1)
            max_q, max_a, max_b, norm_a = (norms[:, 3 * k:3 * k + 3] for k in range(4))
            dve.tensor_tensor(M[:], max_a, max_b, ALU.mult).then_inc(step, 1)
            dve.tensor_tensor(N[:], norm_a, max_b, ALU.mult).then_inc(step, 1)
            dve.reduce_max(ab[:], norms[:, 3:9].rearrange("p (s m) -> p s m", s=2), AX.X).then_inc(step, 1)
            dve.wait_ge(step, 12)
            dve.scalar_tensor_tensor(own[:, 0:3], max_q, TINY, M[:], ALU.max, ALU.add).then_inc(step, 1)
            dve.tensor_scalar(ratio[:], max_q, D ** 0.5, TINY, ALU.mult, ALU.max).then_inc(step, 1)
            dve.tensor_scalar(ab[:], ab[:], TINY, None, ALU.max).then_inc(step, 1)
            dve.wait_ge(step, 15)
            dve.tensor_tensor(N[:], ratio[:], N[:], ALU.add).then_inc(step, 1)
            dve.tensor_tensor(M[:, 0:2], own[:, 0:1].to_broadcast([P, 2]), own[:, 1:2].to_broadcast([P, 2]), ALU.max).then_inc(step, 1)
            dve.tensor_copy(M[:, 2:3], own[:, 2:3]).then_inc(step, 1)
            dve.wait_ge(step, 18)
            dve.reciprocal(rM[:], M[:]).then_inc(step, 1)
            dve.reciprocal(rab[:], ab[:]).then_inc(step, 1)
            dve.tensor_tensor(abp[:], ab[:, 0:1], ab[:, 1:2], ALU.mult).then_inc(step, 1)
            dve.wait_ge(step, 21)
            dve.reciprocal(rN[:], N[:]).then_inc(step, 1)
            dve.tensor_tensor(nn[:], N[:, 0:1], N[:, 1:2], ALU.mult).then_inc(step, 1)
            dve.tensor_scalar(res["w_scale"][:], rM[:], WMAX, None, ALU.mult).then_inc(step, 1)
            dve.tensor_scalar(res["ab_scale"][:], rab[:], ABMAX, None, ALU.mult).then_inc(step, 1)
            dve.wait_ge(step, 25)
            dve.tensor_scalar(res["lora_gain"][:], res["w_scale"][:], abp[:], ABMAX ** -2, ALU.mult, ALU.mult).then_inc(step, 1)
            dve.tensor_tensor(ratio[:], M[:], rN[:], ALU.mult).then_inc(step, 1)
            dve.scalar_tensor_tensor(nn[:], M[:, 2:3], D / (WMAX * HMAX), nn[:], ALU.mult, ALU.mult).then_inc(step, 1)
            dve.wait_ge(step, 28)
            dve.scalar_tensor_tensor(res["hid_gain"][:], ratio[:, 0:1], HMAX / (D * WMAX ** 2 * LN_SCALE ** 2), ratio[:, 1:2], ALU.mult, ALU.mult).then_inc(step, 1)
            dve.wait_ge(tanh_done, 1)
            dve.tensor_tensor(res["ffn_gain"][:], nn[:], tg[:, 2:3], ALU.mult).then_inc(step, 1)
            dve.wait_ge(step, 30)

    return sp_part, pool_part, act_part, pe_part, dve_part


def exists(i):
    return not isinstance(i, int) or 0 <= i < TILES


def after(engine, semaphore, count):
    if not isinstance(count, int) or count > 0:
        engine.wait_ge(semaphore, count)


def phase_linear_attention(nc, io, res):
    settle = settler(res["passed"])
    X, xT_hi, xT_lo, ident, blk, tg, mhalf, gates = (res[k] for k in ("X", "xT_hi", "xT_lo", "ident", "blk", "tg", "mhalf", "gates"))
    x_d = io["x"].rearrange("b (h p) n -> b h p n", p=P)
    c_d = io["ctx"].rearrange("b (h p) n -> b h p n", p=P)
    with ExitStack() as ctx:
        def sb(name, shape, dt=F32):
            return [ctx.enter_context(nc.sbuf_tensor(f"{name}{h}", shape, dt)) for h in range(2)]

        def sem(name):
            return ctx.enter_context(nc.semaphore(name))

        c_in, cT, eq, ek, ekT, xn = (sb(n, [P, D]) for n in ("c_in", "cT", "eq", "ek", "ekT", "xn"))
        kvm, rS = sb("kvm", [P, P]), sb("rS", [P, D // ROWS0])
        rSx = ctx.enter_context(nc.sbuf_tensor("rSx", [P, D], F32))
        st, mv, ve, rstd, nmr = sb("st", [P, 12]), sb("mv", [P, 2]), sb("ve", [P, 1]), sb("rstd", [P, 1]), sb("nmr", [P, 1])
        st2, mv2, ve2, rstd2, nmr2 = sb("st2", [P, 12]), sb("mv2", [P, 2]), sb("ve2", [P, 1]), sb("rstd2", [P, 1]), sb("nmr2", [P, 1])
        cm, ncm, ksum, rks = sb("cm", [P, 1]), sb("ncm", [P, 1]), sb("ksum", [P, 1]), sb("rks", [P, 1])
        psE, psB, psO, psX = (ctx.enter_context(nc.psum_tensor(n, [P, D], F32)) for n in ("psE", "psB", "psO", "psX"))

        x_in, ctx_in, cT_in = ([sem(f"{n}{h}") for h in range(2)] for n in ("x_in", "ctx_in", "cT_in"))
        stats_done, mv_done, ve_done, rstd_done, nmr_done = (sem(n) for n in ("stats_done", "mv_done", "ve_done", "rstd_done", "nmr_done"))
        cmax_done, ncm_done, eq_done, ek_done, rks_done = (sem(n) for n in ("cmax_done", "ncm_done", "eq_done", "ek_done", "rks_done"))
        ekT_mm, ekT_done, kv_mm, kvm_done = (sem(n) for n in ("ekT_mm", "ekT_done", "kv_mm", "kvm_done"))
        sums_mm, rS_done, rSx_done, rS_mm, eqn_done, out_mm, x_done = (sem(n) for n in ("sums_mm", "rS_done", "rSx_done", "rS_mm", "eqn_done", "out_mm", "x_done"))
        stats2_done, mv2_done, ve2_done, rstd2_done, nmr2_done = (sem(n) for n in ("stats2_done", "mv2_done", "ve2_done", "rstd2_done", "nmr2_done"))
        xn_done, xT_mm, hi_done, lo_done = (sem(n) for n in ("xn_done", "xT_mm", "hi_done", "lo_done"))

        const_in, gates_in, const_set, tanh_done = (sem(n) for n in ("const_in", "gates_in", "const_set", "tanh_done"))
        scales_sp, scales_pool, scales_act, scales_pe, scales_dve = ffn_scales(nc, ctx, io, res, psB, const_set, tanh_done)

        def run(engine, step, scales):
            for i in range(4):
                step(i, i % 2)
            with engine.Fori(2, B - 1) as b:
                for h in range(2):
                    step(b * 2 + h, h)
            for i in range(TILES - 2, TILES + 3):
                step(i, i % 2)
                scales(engine, i)

        with nc.Block() as block:
            @block.sync
            def _(sp):
                def load(b, h):
                    sp.dma_start(c_in[h][:], c_d[b, h]).then_inc(ctx_in[h], 16)

                def load_T(b, h):
                    sp.dma_start(cT[h][:], io["ctxT"][b, h]).then_inc(cT_in[h], 16)

                for h in range(2):
                    sp.dma_start(X[:, h, :], x_d[0, h]).then_inc(x_in[h], 16)
                    load(0, h)
                    if h == 0:
                        sp.dma_start(ident[:], io["ident"]).then_inc(const_in, 16)
                        sp.dma_start(blk[:], io["blk"]).then_inc(const_in, 16)
                    load_T(0, h)
                for n, g in enumerate(("g_xattn", "g_ffn")):
                    sp.dma_start(gates[:, 2 * n:2 * n + 2], io[g].partition_broadcast(P)).then_inc(gates_in, 16)
                with sp.Fori(1, B) as b:
                    for h in range(2):
                        sp.wait_ge(ek_done, b * 2 + h - 1)
                        sp.dma_start(X[:, b * 2 + h, :], x_d[b, h]).then_inc(x_in[h], 16)
                        load(b, h)
                        sp.wait_ge(kv_mm, b * 2 + h - 1)
                        load_T(b, h)
                scales_sp(sp)

            @block.gpsimd
            def _(pool):
                def rsqrt(i, h, mv_, ve_, rs_, mvd, ved, rsd):
                    pool.wait_ge(mvd, i + 1)
                    settle(pool)
                    pool.tensor_scalar(ve_[h][:], mv_[h][:, 1:2], EPS, None, ALU.add).then_inc(ved, 1)
                    pool.wait_ge(ved, i + 1)
                    pool.tensor_tensor(rs_[h][:], ve_[h][:], mhalf[:], ALU.pow).then_inc(rsd, 1)

                def step(i, h):
                    if exists(i - 1):
                        rsqrt(i - 1, 1 - h, mv2, ve2, rstd2, mv2_done, ve2_done, rstd2_done)
                    if exists(i + 2):
                        rsqrt(i + 2, h, mv, ve, rstd, mv_done, ve_done, rstd_done)

                pool.memset(mhalf[:], -0.5).then_inc(const_set, 1)
                pool.memset(res["half"][:], 0.5).then_inc(const_set, 1)
                pool.memset(res["ones"][:], 1.0).then_inc(const_set, 1)
                pool.wait_ge(const_set, 3)
                for h in range(2):
                    rsqrt(h, h, mv, ve, rstd, mv_done, ve_done, rstd_done)
                run(pool, step, scales_pool)

            @block.scalar
            def _(act):
                def exponentials(i, h):
                    act.wait_ge(nmr_done, i + 1)
                    after(act, out_mm, i - 1)
                    settle(act)
                    act.activation(eq[h][:], X[:, i, :], ACT.Exp, scale=rstd[h][:], bias=nmr[h][:]).then_inc(eq_done, 1)
                    after(act, ekT_mm, i - 1)
                    after(act, rks_done, i - 1)
                    act.wait_ge(ncm_done, i + 1)
                    act.activation(ek[h][:], c_in[h][:], ACT.Exp, bias=ncm[h][:], accum_out=ksum[h][:]).then_inc(ek_done, 1)

                def step(i, h):
                    if exists(i):
                        after(act, kv_mm, i - 1)
                        act.wait_ge(ekT_mm, i + 1)
                        act.activation(ekT[h][:], psE[:], ACT.Copy).then_inc(ekT_done, 1)
                        after(act, rS_mm, i)
                        act.wait_ge(rS_done, i + 1)
                        act.activation(rSx[:].rearrange("p (n r) -> p n r", r=ROWS0), rS[h][:].unsqueeze(2).to_broadcast([P, D // ROWS0, ROWS0]),
                                       ACT.Copy).then_inc(rSx_done, 1)
                    if exists(i + 1):
                        exponentials(i + 1, 1 - h)
                    if exists(i - 1):
                        after(act, xT_mm, i - 2)
                        act.wait_ge(nmr2_done, i)
                        settle(act)
                        act.activation(xn[1 - h][:], X[:, i - 1, :], ACT.Identity, scale=rstd2[1 - h][:], bias=nmr2[1 - h][:]).then_inc(xn_done, 1)
                    if exists(i - 2):
                        act.wait_ge(xT_mm, i - 1)
                        settle(act)
                        act.activation(xT_hi[:, :, bass.ds((i - 2) * P, P)], psX[:].rearrange("p (k t) -> p k t", k=KD),
                                       ACT.Copy, scale=LN_SCALE).then_inc(hi_done, 1)

                exponentials(0, 0)
                act.wait_ge(gates_in, 32)
                act.activation(tg[:], gates[:], ACT.Tanh).then_inc(tanh_done, 1)
                run(act, step, scales_act)

            @block.tensor
            def _(pe):
                def step(i, h):
                    if exists(i):
                        after(pe, kvm_done, i)
                        pe.wait_ge(ek_done, i + 1)
                        for k in range(KD):
                            mm = pe.transpose(psE[:, k * P:(k + 1) * P], ek[h][:, k * P:(k + 1) * P], ident[:])
                        mm.then_inc(ekT_mm, 1)
                        after(pe, eqn_done, i)
                        pe.wait_ge(eq_done, i + 1)
                        for k in range(KD):
                            mm = pe.matmul(psB[:, k * P:(k + 1) * P], eq[h][:, k * P:(k + 1) * P], blk[:], start=True, stop=True)
                        mm.then_inc(sums_mm, 1)
                    if exists(i - 1):
                        pe.wait_ge(eqn_done, i)
                        pe.wait_ge(kvm_done, i)
                        after(pe, x_done, i - 1)
                        for n in range(2):
                            mm = pe.matmul(psO[:, n * BANK:(n + 1) * BANK], kvm[1 - h][:], eq[1 - h][:, n * BANK:(n + 1) * BANK], start=True, stop=True)
                        mm.then_inc(out_mm, 1)
                    if exists(i):
                        pe.wait_ge(ekT_done, i + 1)
                        pe.wait_ge(cT_in[h], (i // 2) * 16 + 16 if isinstance(i, int) else (i - h) * 8 + 16)
                        for k in range(KD):
                            mm = pe.matmul(psE[:, 0:P], ekT[h][:, k * P:(k + 1) * P], cT[h][:, k * P:(k + 1) * P], start=(k == 0), stop=(k == KD - 1))
                        mm.then_inc(kv_mm, 1)
                        pe.wait_ge(rSx_done, i + 1)
                        for k in range(KD):
                            mm = pe.transpose(psB[:, k * P:(k + 1) * P], rSx[:, k * P:(k + 1) * P], ident[:])
                        mm.then_inc(rS_mm, 1)
                    if exists(i - 2):
                        pe.wait_ge(xn_done, i - 1)
                        after(pe, lo_done, i - 2)
                        for k in range(KD):
                            mm = pe.transpose(psX[:, k * P:(k + 1) * P], xn[h][:, k * P:(k + 1) * P], ident[:])
                        mm.then_inc(xT_mm, 1)

                pe.wait_ge(const_in, 32)
                run(pe, step, scales_pe)

            @block.vector
            def _(dve):
                def stats(i, h, st_, mv_, sd, md):
                    settle(dve)
                    for n in range(2):
                        dve.bn_stats(st_[h][:, 6 * n:6 * n + 6], X[:, i, n * BANK:(n + 1) * BANK]).then_inc(sd, 1)
                    dve.wait_ge(sd, i * 2 + 2)
                    settle(dve)
                    dve.bn_aggr(mv_[h][:], st_[h][:]).then_inc(md, 1)

                def offset(i, h, mv_, rs_, nm_, rsd, nmd):
                    dve.wait_ge(rsd, i + 1)
                    dve.scalar_tensor_tensor(nm_[h][:], mv_[h][:, 0:1], -1.0, rs_[h][:], ALU.mult, ALU.mult).then_inc(nmd, 1)

                def prepare(i, h):
                    loads = (i // 2) * 16 + 16 if isinstance(i, int) else (i - h) * 8 + 16
                    dve.wait_ge(x_in[h], loads)
                    stats(i, h, st, mv, stats_done, mv_done)
                    dve.wait_ge(ctx_in[h], loads)
                    dve.reduce_max(cm[h][:], c_in[h][:], AX.X).then_inc(cmax_done, 1)
                    offset(i, h, mv, rstd, nmr, rstd_done, nmr_done)
                    dve.wait_ge(cmax_done, i + 1)
                    dve.tensor_scalar(ncm[h][:], cm[h][:], -1.0, None, ALU.mult).then_inc(ncm_done, 1)

                def step(i, h):
                    if exists(i - 3):
                        dve.wait_ge(hi_done, i - 2)
                        cols = bass.ds((i - 3) * P, P)
                        dve.scalar_tensor_tensor(xT_lo[:, :, cols], psX[:].rearrange("p (k t) -> p k t", k=KD), LN_SCALE,
                                                 xT_hi[:, :, cols], ALU.mult, ALU.subtract).then_inc(lo_done, 1)
                    if exists(i):
                        dve.wait_ge(ek_done, i + 1)
                        dve.reciprocal(rks[h][:], ksum[h][:]).then_inc(rks_done, 1)
                        dve.wait_ge(sums_mm, i + 1)
                        dve.reciprocal(rS[h][:], psB[:, 0:D:ROWS0]).then_inc(rS_done, 1)
                    if exists(i - 1):
                        dve.wait_ge(out_mm, i)
                        dve.scalar_tensor_tensor(X[:, i - 1, :], psO[:], tg[:, 0:1], X[:, i - 1, :], ALU.mult, ALU.add).then_inc(x_done, 1)
                        dve.wait_ge(x_done, i)
                        stats(i - 1, 1 - h, st2, mv2, stats2_done, mv2_done)
                    if exists(i):
                        dve.wait_ge(rks_done, i + 1)
                        dve.wait_ge(kv_mm, i + 1)
                        dve.scalar_tensor_tensor(kvm[h][:], psE[:, 0:P], rks[h][:], blk[:], ALU.mult, ALU.mult).then_inc(kvm_done, 1)
                    if exists(i - 1):
                        offset(i - 1, 1 - h, mv2, rstd2, nmr2, rstd2_done, nmr2_done)
                    if exists(i):
                        dve.wait_ge(rS_mm, i + 1)
                        dve.tensor_tensor(eq[h][:], psB[:], eq[h][:], ALU.mult).then_inc(eqn_done, 1)
                    if exists(i + 2):
                        prepare(i + 2, h)

                for h in range(2):
                    prepare(h, h)
                dve.wait_ge(const_in, 32)
                dve.wait_ge(tanh_done, 1)
                run(dve, step, scales_dve)


def phase_nf4_ffn(nc, io, res):
    X, xT_hi, xT_lo = (res[k] for k in ("X", "xT_hi", "xT_lo"))
    w_scale, ab_scale, lora_gain, hid_gain, ffn_gain = (res[k] for k in ("w_scale", "ab_scale", "lora_gain", "hid_gain", "ffn_gain"))
    units = pack_units()
    lines_of = nf4_lines()
    NL = len(lines_of)
    OPS = 7
    RING = 3
    ACC_FIRST = 8
    HID_FIRST = 2
    with ExitStack() as ctx:
        def sb(name, shape, dt=F32):
            return ctx.enter_context(nc.sbuf_tensor(name, shape, dt))

        def sem(name):
            return ctx.enter_context(nc.semaphore(name))

        codes = [sb(f"codes{s}", [P, BANK], I32) for s in range(RING)]
        absm = [sb(f"absm{s}", [P, BANK]) for s in range(RING)]
        line_all = sb("lines", [P, NL, BANK])
        line = [line_all[:, j, :] for j in range(NL)]
        wt = [sb(f"wt{s}", [P, BANK]) for s in range(2)]
        gu_hi = [sb(f"gu_hi{c}", [P, 2, KD, P], HALF) for c in range(2)]
        gu_lo = [sb(f"gu_lo{c}", [P, 2, KD, P], HALF) for c in range(2)]
        dn_hi = [sb(f"dn_hi{c}", [P, D], HALF) for c in range(2)]
        dn_lo = [sb(f"dn_lo{c}", [P, D], HALF) for c in range(2)]
        hid_hi = [sb(f"hid_hi{c}", [P, B * L], HALF) for c in range(2)]
        hid_lo = [sb(f"hid_lo{c}", [P, B * L], HALF) for c in range(2)]
        rel = [sb(f"rel{s}", [P, BANK]) for s in range(2)]
        LROWS = 96
        lora_a = sb("lora_a", [LROWS, 3, D], HALF)
        lora_bf = sb("lora_bf", [LROWS, 3, PAIR])
        lora_b = sb("lora_b", [LROWS, 3, PAIR], HALF)
        la_f = [t[0:LROWS].bitcast(F32) for t in (hid_hi[0], hid_hi[1], hid_lo[0])]

        ps_lora = [ctx.enter_context(nc.psum_tensor(f"ps_lora{s}", [P, BANK], F32)) for s in range(2)]
        ps_ring = [ctx.enter_context(nc.psum_tensor(f"ps_ring{s}", [P, BANK], F32)) for s in range(6)]

        codes_in = [sem(f"codes_in{s}") for s in range(RING)]
        absm_in = [sem(f"absm_in{s}") for s in range(RING)]
        la_in, la_hi, la_done = sem("la_in"), sem("la_hi"), sem("la_done")
        lb_in, lb_hi, lb_done = sem("lb_in"), sem("lb_hi"), sem("lb_done")
        line_done, line_used = sem("line_done"), sem("line_used")
        scaled, wt_done, whi_done, wlo_done = sem("scaled"), sem("wt_done"), sem("whi_done"), sem("wlo_done")
        lora_mm = sem("lora_mm")
        up_mm, rel_done, mul_done, hidhi_done, hidlo_done = (sem(n) for n in ("up_mm", "rel_done", "mul_done", "hidhi_done", "hidlo_done"))
        down_mm, acc_done = sem("down_mm"), sem("acc_done")

        def dest(u, part):
            m, c, hf = units[u]
            if m == 2:
                return (dn_hi if part == 0 else dn_lo)[c][:, hf * BANK:(hf + 1) * BANK]
            kk = KD // 2
            return (gu_hi if part == 0 else gu_lo)[c][:, m, hf * kk:(hf + 1) * kk, :].rearrange("p k f -> p (k f)")

        AHEAD = 5

        def shared(j, c):
            return isinstance(j, int) and j == PAIRS - 1 and c == 1

        def unit_no(j, u):
            return j * UNITS + u

        with nc.Block() as block:
            @block.sync
            def _(sp):
                def load(j, u, first=False):
                    g = unit_no(j, u)
                    s = u % RING
                    if not first:
                        sp.wait_ge(scaled, g - RING + 1)
                    sp.dma_start(codes[s][:], io["codes"][j, u]).then_inc(codes_in[s], 16)
                    for half in range(2):
                        sp.dma_start(absm[s][half * QBLK:(half + 1) * QBLK, :],
                                     io["absmax"][j, u, half].partition_broadcast(QBLK)).then_inc(absm_in[s], 16)

                def load_lora(j, first=False):
                    if not first:
                        sp.wait_ge(lb_done, j)
                    sp.dma_start(lora_bf[:], io["lora_b"][j]).then_inc(lb_in, 16)

                load(0, 0, first=True)
                for m in range(3):
                    sp.dma_start(la_f[m], io["lora_a"][:, m]).then_inc(la_in, 16)
                load_lora(0, first=True)
                for u in range(1, UNITS):
                    load(0, u, first=u < RING)
                with sp.Fori(1, PAIRS) as j:
                    load_lora(j)
                    for u in range(UNITS):
                        load(j, u)

                sp.wait_ge(up_mm, 2 * TB * PAIRS)
                c_d = io["ctx"].rearrange("b (t p) n -> b p t n", p=P)
                sp.dma_start(res["ctx_in0"], c_d[0]).then_inc(res["ctx_in"][0], 16)
                for name in ("fwd", "fwd_hi", "fwd_lo", "inv"):
                    sp.dma_start(res[name], io[name]).then_inc(res["const_in"], 16)
                sp.dma_start(res["ctx_in1"], c_d[1]).then_inc(res["ctx_in"][1], 16)

            @block.scalar
            def _(act):
                def lora_parts(j):
                    act.wait_ge(lb_in, j * 16 + 16)
                    if not isinstance(j, int):
                        act.wait_ge(lora_mm, j * UNITS)
                    act.activation(lora_b[:], lora_bf[:], ACT.Copy, scale=ab_scale[0:LROWS, 1:2]).then_inc(lb_hi, 1)

                def lines(j, u, first=False):
                    g = unit_no(j, u)
                    act.wait_ge(codes_in[u % RING], (j * (UNITS // RING) + u // RING) * 16 + 16)
                    for k, (slope, off) in enumerate(lines_of):
                        if not first:
                            act.wait_ge(line_used, (g - 1) * OPS + (OPS if k in (0, 4) else k if k < 4 else k - 1))
                        act.activation(
                            line[k], codes[u % RING][:], ACT.Copy, bias=off, scale=slope).then_inc(line_done, 1)

                def w_hi(j, u):
                    g = unit_no(j, u)
                    act.wait_ge(wt_done, g + 1)
                    act.activation(dest(u, 0), wt[u % 2][:], ACT.Copy).then_inc(whi_done, 1)

                def relu(j, c, t):
                    n = j * 2 * TB + c * TB + t
                    act.wait_ge(up_mm, n + 1)
                    act.wait_ge(hidlo_done, n - 1 + HID_FIRST)
                    if shared(j, c):
                        act.activation(rel[t % 2][P - LAST:P], ps_ring[2 + 2 * (t % 2)][0:LAST], ACT.Relu).then_inc(rel_done, 1)
                    else:
                        act.activation(rel[t % 2][:], ps_ring[2 + 2 * (t % 2)][:], ACT.Relu).then_inc(rel_done, 1)

                def h_hi(j, c, t):
                    n = j * 2 * TB + c * TB + t
                    act.wait_ge(mul_done, n + 1)
                    act.activation(hid_hi[c][:, t * BANK:(t + 1) * BANK], rel[t % 2][:], ACT.Copy).then_inc(hidhi_done, 1)

                lines(0, 0, first=True)
                act.wait_ge(la_in, 48)
                for m in range(3):
                    act.activation(lora_a[:, m], la_f[m], ACT.Copy, scale=ab_scale[0:LROWS, 0:1]).then_inc(la_hi, 1)
                lora_parts(0)
                for u in range(1, AHEAD):
                    lines(0, u)
                    w_hi(0, u - 1)

                def unit(j, u):
                    lines(j, u)
                    w_hi(j, u - 1)

                def pair(j, more):
                    unit(j, AHEAD)
                    for t in range(TB):
                        relu(j, 0, t)
                        unit(j, AHEAD + 1 + t)
                        h_hi(j, 0, t)
                    relu(j, 1, 0)
                    unit(j, 10)
                    h_hi(j, 1, 0)
                    if more:
                        lora_parts(j + 1)
                    unit(j, 11)
                    relu(j, 1, 1)
                    if more:
                        lines(j + 1, 0)
                    w_hi(j, 11)
                    h_hi(j, 1, 1)
                    if more:
                        unit(j + 1, 1)
                    relu(j, 1, 2)
                    if more:
                        unit(j + 1, 2)
                    h_hi(j, 1, 2)
                    relu(j, 1, 3)
                    h_hi(j, 1, 3)
                    if more:
                        unit(j + 1, 3)
                        unit(j + 1, 4)

                with act.Fori(0, PAIRS - 1) as j:
                    pair(j, True)
                pair(PAIRS - 1, False)

            @block.gpsimd
            def _(pool):
                def w_lo(j, u):
                    pool.wait_ge(whi_done, unit_no(j, u) + 1)
                    pool.tensor_tensor(dest(u, 1), wt[u % 2][:], dest(u, 0), ALU.subtract).then_inc(wlo_done, 1)

                def h_lo(j, c, t):
                    pool.wait_ge(hidhi_done, j * 2 * TB + c * TB + t + 1)
                    pool.tensor_tensor(hid_lo[c][:, t * BANK:(t + 1) * BANK], rel[t % 2][:], hid_hi[c][:, t * BANK:(t + 1) * BANK],
                                       ALU.subtract).then_inc(hidlo_done, 1)

                def pair(j, more):
                    for t in range(TB):
                        w_lo(j, AHEAD + t)
                        h_lo(j, 0, t)
                    w_lo(j, 9)
                    h_lo(j, 1, 0)
                    w_lo(j, 10)
                    w_lo(j, 11)
                    h_lo(j, 1, 1)
                    if more:
                        w_lo(j + 1, 0)
                        w_lo(j + 1, 1)
                    for t in (2, 3):
                        h_lo(j, 1, t)
                    if more:
                        for u in (2, 3, 4):
                            w_lo(j + 1, u)

                pool.sem_inc(hidlo_done, HID_FIRST)
                for u in range(AHEAD):
                    w_lo(0, u)
                with pool.Fori(0, PAIRS - 1) as j:
                    pair(j, True)
                pair(PAIRS - 1, False)

            @block.vector
            def _(dve):
                dve.sem_inc(acc_done, ACC_FIRST)

                def lora_parts(j):
                    dve.wait_ge(lb_hi, j + 1)
                    dve.scalar_tensor_tensor(lora_b[64:96], lora_bf[64:96], ab_scale[64:96, 1:2], lora_b[64:96], ALU.mult, ALU.subtract).then_inc(lb_done, 1)

                def combine(j, u, sign):
                    g = unit_no(j, u)
                    base, n = 4 * sign, g * OPS + 3 * sign
                    for k in range(1, 4):
                        dve.wait_ge(line_done, g * NL + base + k + 1)
                        if k == 1:
                            dve.scalar_tensor_tensor(line[base], line[base], 0.0, line[base + 1], ALU.max, ALU.max).then_inc(line_used, 1)
                        else:
                            dve.wait_ge(line_used, n + k - 1)
                            dve.tensor_tensor(line[base], line[base], line[base + k], ALU.max).then_inc(line_used, 1)

                def finish(j, u):
                    g = unit_no(j, u)
                    m = units[u][0]
                    dve.wait_ge(line_used, g * OPS + 6)
                    if not (isinstance(g, int) and g < 2):
                        dve.wait_ge(wlo_done, g - 1)
                    dve.tensor_tensor(wt[u % 2][:], line[0], line[4], ALU.subtract).then_inc(line_used, 1)
                    dve.wait_ge(line_used, g * OPS + OPS)
                    dve.wait_ge(absm_in[u % RING], (j * (UNITS // RING) + u // RING) * 32 + 32)
                    dve.scalar_tensor_tensor(wt[u % 2][:], wt[u % 2][:], w_scale[:, m:m + 1], absm[u % RING][:], ALU.mult, ALU.mult).then_inc(scaled, 1)
                    dve.wait_ge(scaled, g + 1)
                    dve.wait_ge(lora_mm, g + 1)
                    dve.scalar_tensor_tensor(wt[u % 2][:], ps_lora[u % 2][:], lora_gain[:, m:m + 1], wt[u % 2][:], ALU.mult, ALU.add).then_inc(wt_done, 1)

                def weights(j, u):
                    combine(j, u, 0)
                    combine(j, u, 1)
                    finish(j, u)

                def mul(j, c, t):
                    n = j * 2 * TB + c * TB + t
                    dve.wait_ge(rel_done, n + 1)
                    if shared(j, c):
                        rows = slice(P - LAST, P)
                        dve.scalar_tensor_tensor(rel[t % 2][rows], ps_ring[2 + 2 * (t % 2)][rows], hid_gain[rows], rel[t % 2][rows], ALU.mult, ALU.mult).then_inc(mul_done, 1)
                    else:
                        dve.scalar_tensor_tensor(rel[t % 2][:], ps_ring[3 + 2 * (t % 2)][:], hid_gain[:], rel[t % 2][:], ALU.mult, ALU.mult).then_inc(mul_done, 1)

                def accumulate(j, n):
                    i, hf = n // HALVES, n % HALVES
                    dve.wait_ge(down_mm, j * 2 * TILES + n + 1)
                    dst = X[:, i, hf * BANK:(hf + 1) * BANK]
                    dve.scalar_tensor_tensor(dst, ps_ring[n % 6][:], ffn_gain[:], dst, ALU.mult, ALU.add).then_inc(acc_done, 1)

                combine(0, 0, 0)
                combine(0, 0, 1)
                for m in range(3):
                    dve.wait_ge(la_hi, m + 1)
                    dve.scalar_tensor_tensor(lora_a[32:64, m], la_f[m][32:64], ab_scale[32:64, 0:1], lora_a[32:64, m], ALU.mult, ALU.subtract).then_inc(la_done, 1)
                lora_parts(0)
                finish(0, 0)
                for u in range(1, AHEAD):
                    weights(0, u)

                def outputs(j, first, count):
                    for n in range(first, first + count):
                        accumulate(j, n)

                def pair(j, more):
                    weights(j, AHEAD)
                    for t in range(TB):
                        mul(j, 0, t)
                        weights(j, AHEAD + 1 + t)
                    mul(j, 1, 0)
                    weights(j, 10)
                    if more:
                        lora_parts(j + 1)
                    weights(j, 11)
                    mul(j, 1, 1)
                    if more:
                        weights(j + 1, 0)
                        weights(j + 1, 1)
                    mul(j, 1, 2)
                    if more:
                        weights(j + 1, 2)
                    mul(j, 1, 3)
                    dve.wait_ge(acc_done, j * 2 * TILES + ACC_FIRST)
                    for s in range(4):
                        if more and s < 2:
                            outputs(j, 8 * s, 3)
                            combine(j + 1, 3 + s, 0)
                            outputs(j, 8 * s + 3, 3)
                            combine(j + 1, 3 + s, 1)
                            outputs(j, 8 * s + 6, 2)
                            finish(j + 1, 3 + s)
                        else:
                            outputs(j, 8 * s, 8)

                with dve.Fori(0, PAIRS - 1) as j:
                    pair(j, True)
                pair(PAIRS - 1, False)

            @block.tensor
            def _(pe):
                def lora(j, u):
                    g = unit_no(j, u)
                    m, c, hf = units[u]
                    if u == 0:
                        pe.wait_ge(lb_done, j + 1)
                    if not (isinstance(g, int) and g < 2):
                        pe.wait_ge(wt_done, g - 1)
                    o = ps_lora[u % 2]
                    if m == 2:
                        mm = pe.matmul(o[:], lora_b[:, m, c * P:(c + 1) * P], lora_a[:, m, hf * BANK:(hf + 1) * BANK], start=True, stop=True)
                    else:
                        for k in range(KD // 2):
                            kk = hf * (KD // 2) + k
                            mm = pe.matmul(o[:, k * P:(k + 1) * P], lora_a[:, m, kk * P:(kk + 1) * P], lora_b[:, m, c * P:(c + 1) * P], start=True, stop=True)
                    mm.then_inc(lora_mm, 1)

                def up(j, c, t):
                    n = j * 2 * TB + c * TB + t
                    if c == 0 and t < 2:
                        pe.wait_ge(acc_done, j * 2 * TILES - 4 + 2 * t + ACC_FIRST)
                    else:
                        pe.wait_ge(mul_done, n - 1)
                    ts = slice(t * BANK, (t + 1) * BANK)
                    for m in range(1 if shared(j, c) else 2):
                        if t == 0:
                            pe.wait_ge(wlo_done, j * UNITS + 4 * c + 2 * m + 2)
                        o = ps_ring[2 + 2 * (t % 2) + m]
                        q = 0
                        if c == 0 and t == 0 and m == 1:
                            lora(j, AHEAD)
                        for k in range(KD):
                            for w, xx in ((gu_hi, xT_hi), (gu_hi, xT_lo), (gu_lo, xT_hi)):
                                mm = pe.matmul(o[:], w[c][:, m, k, :], xx[:, k, ts], start=(q == 0), stop=(q == 3 * KD - 1))
                                q += 1
                    mm.then_inc(up_mm, 1)

                def down(j, n):
                    i, hf = n // HALVES, n % HALVES
                    if n == 0:
                        pe.wait_ge(wlo_done, j * UNITS + UNITS)
                    if n % (2 * TILES // TB) == 0:
                        pe.wait_ge(hidlo_done, j * 2 * TB + TB + n // (2 * TILES // TB) + 1 + HID_FIRST)
                    if n < 2:
                        pe.wait_ge(acc_done, j * 2 * TILES - 2 + n + 1 + ACC_FIRST)
                    elif n < 6:
                        pe.wait_ge(mul_done, j * 2 * TB + 2 * TB - 2 + n // 2)
                    else:
                        pe.wait_ge(acc_done, j * 2 * TILES + n - 5 + ACC_FIRST)
                    q = 0
                    for c in range(2):
                        for hh, w in ((hid_hi, dn_hi), (hid_hi, dn_lo), (hid_lo, dn_hi)):
                            mm = pe.matmul(ps_ring[n % 6][:], hh[c][:, i * P:(i + 1) * P], w[c][:, hf * BANK:(hf + 1) * BANK],
                                           start=(q == 0), stop=(q == 5))
                            q += 1
                    mm.then_inc(down_mm, 1)

                pe.wait_ge(la_done, 3)
                for u in range(AHEAD):
                    lora(0, u)

                def pair(j, more):
                    for t in range(TB):
                        up(j, 0, t)
                        lora(j, AHEAD + 1 + t)
                    up(j, 1, 0)
                    lora(j, 10)
                    lora(j, 11)
                    up(j, 1, 1)
                    if more:
                        lora(j + 1, 0)
                    up(j, 1, 2)
                    if more:
                        lora(j + 1, 1)
                    up(j, 1, 3)
                    if more:
                        lora(j + 1, 2)
                    for n in range(2 * TILES):
                        down(j, n)
                        if more and n in (7, 15):
                            lora(j + 1, 3 + n // 8)

                with pe.Fori(0, PAIRS - 1) as j:
                    pair(j, True)
                pair(PAIRS - 1, False)


def spectra():
    t, f = np.arange(L)[:, None], np.arange(P)[None, :]
    even, odd = 2 * np.pi * t * f / L, 2 * np.pi * t * (f + 0.5) / L
    nyquist = np.where(t % 2 == 0, 1.0, -1.0)
    im = -np.sin(even)
    im[:, :1] = nyquist
    odd_re, odd_im = np.cos(odd), -np.sin(odd)
    last = (t == L - 1)
    fwd = np.stack([np.stack([np.cos(even), im]), np.stack([odd_re, odd_im]),
                    np.stack([odd_re - last * odd_re.sum(0), odd_im - last * odd_im.sum(0)]),
                    np.stack([np.cos(even) + L * last * (f == 0), im])])
    weight = np.where(f == 0, 1.0, 2.0) / L
    im_inv = -np.sin(even) * weight
    im_inv[:, :1] = (nyquist - 1.0) / L
    inv = np.stack([np.cos(even) * weight, im_inv, odd_re * 2 / L, odd_im * 2 / L])
    fwd = fwd.reshape(4, 2, 2, P, P).transpose(3, 2, 0, 1, 4)
    scaled = fwd[:, :, 0:2] * DFT_SCALE
    high = scaled.astype(np.float16)
    return (fwd[:, :, 2:].astype(np.float32), high, (scaled - high).astype(np.float16), inv.transpose(2, 0, 1).astype(np.float32))


def phase_autocorrelation(nc, io, res):
    settle = settler(res["passed"])
    X, ident, tg, mhalf = (res[k] for k in ("X", "ident", "tg", "mhalf"))
    CB = BANK
    CH = CB // P
    U = 4
    N = B * 2
    c_d = io["ctx"].rearrange("b (t p) n -> b p t n", p=P)
    with ExitStack() as ctx:
        def sb(name, shape, dt=F32):
            return ctx.enter_context(nc.sbuf_tensor(name, shape, dt))

        def sem(name):
            return ctx.enter_context(nc.semaphore("a_" + name))

        fwd, fwd_hi, fwd_lo, inv, const_in, ctx_in = (res[k] for k in ("fwd", "fwd_hi", "fwd_lo", "inv", "const_in", "ctx_in"))
        c_in = [res[f"ctx_in{s}"] for s in range(2)]
        half_gate = sb("half_gate", [P, 1])
        xn = sb("a_xn", [P, 2, D])
        q_hi = [sb(f"q_hi{s}", [P, 2, D], HALF) for s in range(2)]
        q_lo = [sb(f"q_lo{s}", [P, 2, D], HALF) for s in range(2)]
        k_re, k_im, o_re, o_im = ([sb(f"{n}{s}", [P, CB]) for s in range(2)] for n in ("k_re", "k_im", "o_re", "o_im"))
        t_rr, t_ii, t_ir, t_ri = (sb(n, [P, CB]) for n in ("t_rr", "t_ii", "t_ir", "t_ri"))
        e_rr, e_ii, e_ri, e_ir = (sb(n, [P, CB]) for n in ("e_rr", "e_ii", "e_ri", "e_ir"))
        n_rr, n_ii, n_ri, n_ir = (sb(n, [P, CB]) for n in ("n_rr", "n_ii", "n_ri", "n_ir"))
        top8, next3 = sb("top8", [P, CH, 8]), sb("next3", [P, CH, 8])
        nmax, wsum, rws = sb("nmax", [P, CH]), sb("wsum", [P, CH]), sb("rws", [P, CH])
        cut, cut2, ex, wn = (sb(n, [P, CH, L]) for n in ("cut", "cut2", "ex", "wn"))
        wT_hi, wT_lo = res["wT_hi"], res["wT_lo"]
        st, mv, ve, rstd, nmr = sb("a_st", [P, 2, 12]), sb("a_mv", [P, 2, 2]), sb("a_ve", [P, 2]), sb("a_rstd", [P, 2]), sb("a_nmr", [P, 2])

        ps = [ctx.enter_context(nc.psum_tensor(f"a_ps{s}", [P, 2 * BANK], F32)) for s in range(4)]
        re, im = slice(0, CB), slice(CB, 2 * CB)

        gate_done = sem("gate_done")
        stats_done, mv_done, ve_done, rstd_done, nmr_done, xn_done = (sem(n) for n in ("stats_done", "mv_done", "ve_done", "rstd_done", "nmr_done", "xn_done"))
        qhi_done, qlo_done, wTlo_done = sem("qhi_done"), sem("qlo_done"), sem("wTlo_done")
        k_mm, u_mm, q_mm, k_done, u_done = (sem(n) for n in ("k_mm", "u_mm", "q_mm", "k_done", "u_done"))
        prod_done, prod_comb, prod_row, corr_mm = (sem(n) for n in ("prod_done", "prod_comb", "prod_row", "corr_mm"))
        top_done, cut_done, nmax_done, next_done, fill_done, cut2_done = (sem(n) for n in ("top_done", "cut_done", "nmax_done", "next_done", "fill_done", "cut2_done"))
        ex_done, w_done, rws_done, wn_done = (sem(n) for n in ("ex_done", "w_done", "rws_done", "wn_done"))
        wT_mm, wT_done, ws_mm, wprod_done, wprod_comb, out_mm, x_done = (sem(n) for n in ("wT_mm", "wT_done", "ws_mm", "wprod_done", "wprod_comb", "out_mm", "x_done"))
        wprod_row = sem("wprod_row")

        with nc.Block() as block:
            @block.sync
            def _(sp):
                for name in ("lora1_a", "lora1_b", "mag", "w1"):
                    sp.dma_start(res[name][:], io[name]).then_inc(res["w1_in"], 16)
                with sp.Fori(1, B // 2) as m:
                    for s in range(2):
                        sp.wait_ge(out_mm, 4 * m - 2 + 2 * s + FIRST)
                        sp.dma_start(c_in[s], c_d[2 * m + s]).then_inc(ctx_in[s], 16)

            @block.gpsimd
            def _(pool):
                def rstd_of(batch):
                    pool.wait_ge(mv_done, 2 * batch + 2)
                    settle(pool)
                    pool.tensor_scalar(ve[:], mv[:, :, 1], EPS, None, ALU.add).then_inc(ve_done, 1)
                    pool.wait_ge(ve_done, batch + 1)
                    pool.tensor_tensor(rstd[:], ve[:], mhalf[:].to_broadcast([P, 2]), ALU.pow).then_inc(rstd_done, 1)

                def corr_comb(n):
                    for k, (a, b_, op) in enumerate(((t_rr, t_ii, ALU.add), (t_ir, t_ri, ALU.subtract))):
                        pool.wait_ge(prod_done, 4 * n + 2 * k + 2)
                        pool.tensor_tensor(a[:], a[:], b_[:], op).then_inc(prod_comb, 1)

                def out_comb(n):
                    for k, (a, b_, op) in enumerate(((e_rr, e_ii, ALU.add), (e_ri, e_ir, ALU.subtract), (n_rr, n_ii, ALU.add), (n_ri, n_ir, ALU.subtract))):
                        pool.wait_ge(wprod_done, 8 * n + 2 * k + 2 + FIRST)
                        pool.tensor_tensor(a[:], a[:], b_[:], op).then_inc(wprod_comb, 1)

                rstd_of(0)
                corr_comb(0)
                rstd_of(1)

                def units(m, more):
                    for r in range(U):
                        n = U * m + r
                        if more or r < U - 1:
                            corr_comb(n + 1)
                        out_comb(n)
                        if r % 2 == 1 and more:
                            rstd_of(2 * m + r // 2 + 2)

                with pool.Fori(0, N // U - 1) as m:
                    units(m, True)
                units(N // U - 1, False)

            @block.scalar
            def _(act):
                def q_norm(batch):
                    act.wait_ge(nmr_done, batch + 1)
                    if not (isinstance(batch, int) and batch == 0):
                        act.wait_ge(qlo_done, 2 * batch)
                    settle(act)
                    for t in range(2):
                        act.activation(xn[:, t, :], X[:, 2 * batch + t, :], ACT.Identity, scale=rstd[:, t:t + 1], bias=nmr[:, t:t + 1]).then_inc(xn_done, 1)

                def q_high(batch, s):
                    for t in range(2):
                        act.wait_ge(xn_done, 2 * batch + t + 1)
                        act.activation(q_hi[s][:, t, :], xn[:, t, :], ACT.Copy, scale=LN_SCALE).then_inc(qhi_done, 1)

                def spectra_out(n, par):
                    for mm, done, pair, dst in ((k_mm, k_done, 1, (k_re, k_im)), (u_mm, u_done, 2, (o_re, o_im))):
                        act.wait_ge(mm, n + 1)
                        for half, d in zip((re, im), dst):
                            act.activation(d[par][:], ps[pair][:, half], ACT.Copy).then_inc(done, 1)

                def weights(n):
                    act.wait_ge(nmax_done, n + 1)
                    for c in range(CH):
                        act.activation(ex[:, c, :], ps[3][:, c * L:(c + 1) * L], ACT.Exp, scale=1.0 / (LN_SCALE * DFT_SCALE), bias=nmax[:, c:c + 1]).then_inc(ex_done, 1)
                    act.wait_ge(rws_done, n + 1)
                    for c in range(CH):
                        act.activation(wn[:, c, :], cut2[:, c, :], ACT.Copy, scale=rws[:, c:c + 1]).then_inc(wn_done, 1)

                def weights_T(n):
                    act.wait_ge(wT_mm, n + 1)
                    act.activation(wT_hi[:].rearrange("p h c -> p (h c)"), ps[3][:], ACT.Copy, scale=TOP_SCALE).then_inc(wT_done, 1)

                def corr_row(n):
                    act.wait_ge(prod_comb, 2 * n + 2)
                    act.activation(t_ir[0:1, :], t_ii[0:1, :], ACT.Copy).then_inc(prod_row, 1)

                def out_row(n):
                    act.wait_ge(wprod_comb, 4 * n + 2)
                    act.activation(e_ri[0:1, :], e_ii[0:1, :], ACT.Copy).then_inc(wprod_row, 1)

                q_norm(0)
                q_high(0, 0)
                spectra_out(0, 0)
                corr_row(0)
                weights(0)

                def units(m, more):
                    for r in range(U):
                        n = U * m + r
                        nxt = more or r < U - 1
                        if nxt:
                            spectra_out(n + 1, (r + 1) % 2)
                        weights_T(n)
                        if r % 2 == 0 and (more or r == 0):
                            q_norm(2 * m + r // 2 + 1)
                        if nxt:
                            corr_row(n + 1)
                        out_row(n)
                        if nxt:
                            weights(n + 1)
                        if r % 2 == 0 and (more or r == 0):
                            q_high(2 * m + r // 2 + 1, (r // 2 + 1) % 2)

                with act.Fori(0, N // U - 1) as m:
                    units(m, True)
                units(N // U - 1, False)

            @block.tensor
            def _(pe):
                pe.sem_inc(out_mm, FIRST)

                def dft(pair, half, kind, src):
                    for t in range(2):
                        mm = pe.matmul(ps[pair][:, half], fwd[:, t, kind - 2, 0 if half is re else 1, :], src(t), start=(t == 0), stop=(t == 1))
                    return mm

                def dft_parts(pair, half, kind, high, low):
                    part = 0 if half is re else 1
                    for t in range(2):
                        for k, (w, src) in enumerate(((fwd_hi, high), (fwd_hi, low), (fwd_lo, high))):
                            mm = pe.matmul(ps[pair][:, half], w[:, t, kind, part, :], src(t), start=(t == 0 and k == 0), stop=(t == 1 and k == 2))
                    return mm

                def spectra_in(n, batch, r, first=False):
                    s, cb = (r // 2) % 2, r % 2
                    cs = slice(cb * CB, (cb + 1) * CB)
                    if cb == 0:
                        pe.wait_ge(ctx_in[s], 16 * (batch // 2 + 1) if isinstance(batch, int) else 16 * first)
                    if not (isinstance(n, int) and n == 0):
                        pe.wait_ge(k_done, 2 * n)
                        pe.wait_ge(u_done, 2 * n)
                        pe.wait_ge(wprod_done, 8 * n - 8 + FIRST)
                    for half in (re, im):
                        mm = dft(1, half, 3, lambda t: c_in[s][:, t, cs])
                    mm.then_inc(k_mm, 1)
                    for half in (re, im):
                        mm = dft(2, half, 2, lambda t: c_in[s][:, t, cs])
                    mm.then_inc(u_mm, 1)

                def q_spectrum(n, batch, r):
                    s, cb = (r // 2) % 2, r % 2
                    cs = slice(cb * CB, (cb + 1) * CB)
                    if cb == 0:
                        pe.wait_ge(qlo_done, 2 * batch + 2)
                    if not (isinstance(n, int) and n < 2):
                        pe.wait_ge(x_done, 2 * n - 2 + FIRST)
                    for half in (re, im):
                        mm = dft_parts(0, half, 0, lambda t: q_hi[s][:, t, cs], lambda t: q_lo[s][:, t, cs])
                    mm.then_inc(q_mm, 1)

                def corr(n):
                    pe.wait_ge(prod_comb, 2 * n + 2)
                    pe.wait_ge(prod_row, n + 1)
                    if not (isinstance(n, int) and n == 0):
                        pe.wait_ge(wTlo_done, n)
                    for c in range(CH):
                        for k, src in enumerate((t_rr, t_ir)):
                            mm = pe.matmul(ps[3][:, c * L:(c + 1) * L], src[:, c * P:(c + 1) * P], inv[:, k, :], start=(k == 0), stop=(k == 1))
                    mm.then_inc(corr_mm, 1)

                def weight_turn(n):
                    pe.wait_ge(wn_done, CH * n + CH)
                    for h in range(2):
                        for c in range(CH):
                            mm = pe.transpose(ps[3][:, h * CB + c * P:h * CB + (c + 1) * P], wn[:, c, h * P:(h + 1) * P], ident[:])
                    mm.then_inc(wT_mm, 1)

                def weight_dfts(n, nxt):
                    pe.wait_ge(wTlo_done, n + 1)
                    pe.wait_ge(k_done, 2 * n + (4 if nxt else 2))
                    for half in (re, im):
                        mm = dft_parts(1, half, 0, lambda t: wT_hi[:, t, :], lambda t: wT_lo[:, t, :])
                    mm.then_inc(ws_mm, 1)
                    pe.wait_ge(u_done, 2 * n + (4 if nxt else 2))
                    for half in (re, im):
                        mm = dft_parts(2, half, 1, lambda t: wT_hi[:, t, :], lambda t: wT_lo[:, t, :])
                    mm.then_inc(ws_mm, 1)

                def output(n, nxt):
                    pe.wait_ge(prod_done, 4 * n + (8 if nxt else 4))
                    pe.wait_ge(wprod_row, n + 1)
                    for first in (0, 2):
                        pe.wait_ge(wprod_comb, 4 * n + first + 2)
                        for t in range(2):
                            for k in (first, first + 1):
                                mm = pe.matmul(ps[0][:, t * CB:(t + 1) * CB], inv[:, k, t * P:(t + 1) * P], (e_rr, e_ri, n_rr, n_ri)[k][:],
                                               start=(k == 0), stop=(k == 3))
                    mm.then_inc(out_mm, 1)

                pe.wait_ge(const_in, 64)
                spectra_in(0, 0, 0)
                q_spectrum(0, 0, 0)
                corr(0)

                def units(m, more):
                    for r in range(U):
                        n = U * m + r
                        nxt = more or r < U - 1
                        if nxt:
                            r1 = (r + 1) % U
                            batch = 2 * m + (r + 1) // 2
                            spectra_in(n + 1, batch, r1, first=(m + 1 if r < U - 1 else m + 2))
                        weight_turn(n)
                        if nxt:
                            q_spectrum(n + 1, batch, r1)
                        weight_dfts(n, nxt)
                        if nxt:
                            corr(n + 1)
                        output(n, nxt)

                with pe.Fori(0, N // U - 1) as m:
                    units(m, True)
                units(N // U - 1, False)

            @block.vector
            def _(dve):
                for used in (wprod_done, x_done):
                    dve.sem_inc(used, FIRST)
                def stats(batch):
                    for t in range(2):
                        if not (isinstance(batch, int) and batch == 0):
                            dve.wait_ge(nmr_done, batch)
                        settle(dve)
                        for h in range(2):
                            dve.bn_stats(st[:, t, 6 * h:6 * h + 6], X[:, 2 * batch + t, h * BANK:(h + 1) * BANK]).then_inc(stats_done, 1)
                    for t in range(2):
                        dve.wait_ge(stats_done, 4 * batch + 2 * t + 2)
                        if t == 0 and not (isinstance(batch, int) and batch == 0):
                            dve.wait_ge(xn_done, 2 * batch)
                        settle(dve)
                        dve.bn_aggr(mv[:, t, :], st[:, t, :]).then_inc(mv_done, 1)

                def offset(batch):
                    dve.wait_ge(rstd_done, batch + 1)
                    dve.wait_ge(mv_done, 2 * batch + 2)
                    dve.scalar_tensor_tensor(nmr[:], mv[:, :, 0], -1.0, rstd[:], ALU.mult, ALU.mult).then_inc(nmr_done, 1)

                def q_low(batch, s):
                    for t in range(2):
                        dve.wait_ge(qhi_done, 2 * batch + t + 1)
                        dve.scalar_tensor_tensor(q_lo[s][:, t, :], xn[:, t, :], LN_SCALE, q_hi[s][:, t, :], ALU.mult, ALU.subtract).then_inc(qlo_done, 1)

                def weights_low(n):
                    dve.wait_ge(wT_done, n + 1)
                    dve.scalar_tensor_tensor(wT_lo[:].rearrange("p h c -> p (h c)"), ps[3][:], TOP_SCALE, wT_hi[:].rearrange("p h c -> p (h c)"),
                                             ALU.mult, ALU.subtract).then_inc(wTlo_done, 1)

                def products(n, par):
                    dve.wait_ge(q_mm, n + 1)
                    dve.wait_ge(k_done, 2 * n + 2)
                    if not (isinstance(n, int) and n == 0):
                        dve.wait_ge(corr_mm, n)
                    for dst, a, b_ in ((t_rr, re, k_re), (t_ii, im, k_im), (t_ir, im, k_re), (t_ri, re, k_im)):
                        dve.tensor_tensor(dst[:], ps[0][:, a], b_[par][:], ALU.mult).then_inc(prod_done, 1)

                def select(n):
                    dve.wait_ge(corr_mm, n + 1)
                    settle(dve)
                    row = [ps[3][:, c * L:(c + 1) * L] for c in range(CH)]
                    for c in range(CH):
                        dve.max(top8[:, c, :], row[c]).then_inc(top_done, 1)
                    for c in range(CH):
                        dve.wait_ge(top_done, CH * n + c + 1)
                        if c == 0:
                            dve.wait_ge(next_done, CH * n)
                        settle(dve)
                        dve.match_replace(cut[:, c, :], top8[:, c, :], row[c], -BIG).then_inc(cut_done, 1)
                    dve.wait_ge(top_done, CH * n + CH)
                    dve.tensor_scalar(nmax[:], top8[:, :, 0], -1.0 / (LN_SCALE * DFT_SCALE), None, ALU.mult).then_inc(nmax_done, 1)
                    for c in range(CH):
                        dve.wait_ge(cut_done, CH * n + c + 1)
                        settle(dve)
                        dve.max(next3[:, c, :], cut[:, c, :]).then_inc(next_done, 1)
                    dve.wait_ge(next_done, CH * n + CH)
                    dve.memset(next3[:, :, TOPK - 8:8], -BIG).then_inc(fill_done, 1)
                    dve.wait_ge(fill_done, n + 1)
                    dve.wait_ge(wn_done, CH * n)
                    settle(dve)
                    for c in range(CH):
                        dve.match_replace(cut2[:, c, :], next3[:, c, :], cut[:, c, :], -BIG).then_inc(cut2_done, 1)
                    for c in range(CH):
                        dve.wait_ge(cut2_done, CH * n + c + 1)
                        dve.wait_ge(ex_done, CH * n + c + 1)
                        dve.scalar_tensor_tensor(cut2[:, c, :], cut2[:, c, :], -0.5 * BIG, ex[:, c, :], ALU.is_le, ALU.mult,
                                                 accum_out=wsum[:, c:c + 1]).then_inc(w_done, 1)
                    dve.wait_ge(w_done, CH * n + CH)
                    dve.reciprocal(rws[:], wsum[:]).then_inc(rws_done, 1)

                def weight_products(n, par):
                    dve.wait_ge(ws_mm, 2 * n + 1)
                    if not (isinstance(n, int) and n == 0):
                        dve.wait_ge(out_mm, n + FIRST)
                    for dst, pair, a, b_ in ((e_rr, 1, re, k_re), (e_ii, 1, im, k_im), (e_ri, 1, re, k_im), (e_ir, 1, im, k_re),
                                             (n_rr, 2, re, o_re), (n_ii, 2, im, o_im), (n_ri, 2, re, o_im), (n_ir, 2, im, o_re)):
                        if dst is n_rr:
                            dve.wait_ge(ws_mm, 2 * n + 2)
                        dve.tensor_tensor(dst[:], ps[pair][:, a], b_[par][:], ALU.mult).then_inc(wprod_done, 1)

                def add(n, m, r):
                    cb = r % 2
                    dve.wait_ge(out_mm, n + 1 + FIRST)
                    for t in range(2):
                        dst = X[:, U * m + 2 * (r // 2) + t, cb * CB:(cb + 1) * CB]
                        dve.scalar_tensor_tensor(dst, ps[0][:, t * CB:(t + 1) * CB], half_gate[:], dst, ALU.mult, ALU.add).then_inc(x_done, 1)

                dve.tensor_scalar(half_gate[:], tg[:, 1:2], 0.5 / (TOP_SCALE * DFT_SCALE), None, ALU.mult).then_inc(gate_done, 1)
                stats(0)
                offset(0)
                q_low(0, 0)
                products(0, 0)
                select(0)
                stats(1)
                offset(1)
                dve.wait_ge(gate_done, 1)

                def units(m, more):
                    for r in range(U):
                        n = U * m + r
                        nxt = more or r < U - 1
                        weights_low(n)
                        if nxt:
                            products(n + 1, (r + 1) % 2)
                        weight_products(n, r % 2)
                        if nxt:
                            select(n + 1)
                        add(n, m, r)
                        if r % 2 == 0 and (more or r == 0):
                            q_low(2 * m + r // 2 + 1, (r // 2 + 1) % 2)
                        elif r % 2 == 1 and more:
                            stats(2 * m + r // 2 + 2)
                            offset(2 * m + r // 2 + 2)

                with dve.Fori(0, N // U - 1) as m:
                    units(m, True)
                units(N // U - 1, False)


def phase_dora_linear(nc, io, res):
    settle = settler(res["passed"])
    X, ident, tg, mhalf, E, stored = (res[k] for k in ("X", "ident", "tg", "mhalf", "w1", "stored"))
    la, lb, mag, w_in = (res[k] for k in ("lora1_a", "lora1_b", "mag", "w1_in"))
    out_d = io["out"].rearrange("b (h p) n -> b h p n", p=P)
    with ExitStack() as ctx:
        def sb(name, shape, dt=F32):
            return ctx.enter_context(nc.sbuf_tensor("d_" + name, shape, dt))

        def sb2(name, shape, dt=F32):
            return [sb(f"{name}{h}", shape, dt) for h in range(2)]

        def sem(name):
            return ctx.enter_context(nc.semaphore("d_" + name))

        def sem2(name):
            return [sem(f"{name}{h}") for h in range(2)]

        sq = sb("sq", [P, D])
        w_hi, w_lo = sb("w_hi", [P, KD, D], HALF), sb("w_lo", [P, KD, D], HALF)
        norm2, rnorm, gain = sb("norm2", [P, KD]), sb("rnorm", [P, KD]), sb("gain", [P, KD])
        gain_row = sb("gain_row", [P, D])
        st, mv, ve, rstd, nmr = sb2("st", [P, 12]), sb2("mv", [P, 2]), sb2("ve", [P, 1]), sb2("rstd", [P, 1]), sb2("nmr", [P, 1])
        xn, x_hi, x_lo, prod = sb2("xn", [P, D]), sb2("x_hi", [P, D], HALF), sb2("x_lo", [P, D], HALF), sb2("prod", [P, D])
        psT = [ctx.enter_context(nc.psum_tensor(f"d_psT{h}", [P, D], F32)) for h in range(2)]
        psO = [ctx.enter_context(nc.psum_tensor(f"d_psO{h}", [P, D], F32)) for h in range(2)]

        lora_mm, E_done, norm_done, rnorm_done, scaled = (sem(n) for n in ("lora_mm", "E_done", "norm_done", "rnorm_done", "scaled"))
        wT_mm, whi_done, wlo_done, gain_done, row_mm, row_done = (sem(n) for n in ("wT_mm", "whi_done", "wlo_done", "gain_done", "row_mm", "row_done"))
        stats_done, mv_done, ve_done, rstd_done, nmr_done, xn_done, hi_done = (
            sem(n) for n in ("stats_done", "mv_done", "ve_done", "rstd_done", "nmr_done", "xn_done", "hi_done"))
        T_mm, lo_done, out_mm, prod_done, x_done = (sem2(n) for n in ("T_mm", "lo_done", "out_mm", "prod_done", "x_done"))

        def following(b, h, steps):
            return b + (h + steps) // 2, (h + steps) % 2

        with nc.Block() as block:
            @block.sync
            def _(sp):
                with sp.Fori(0, B) as b:
                    for h in range(2):
                        sp.wait_ge(x_done[h], 2 * b + 2)
                        sp.dma_start(out_d[b, h], X[:, 2 * b + h, :]).then_inc(stored, 16)
                sp.wait_ge(stored, 16 * TILES)

            @block.gpsimd
            def _(pool):
                def rstd_of(b, h):
                    pool.wait_ge(mv_done, 2 * b + h + 1)
                    settle(pool)
                    pool.tensor_scalar(ve[h][:], mv[h][:, 1:2], EPS, None, ALU.add).then_inc(ve_done, 1)
                    pool.wait_ge(ve_done, 2 * b + h + 1)
                    pool.tensor_tensor(rstd[h][:], ve[h][:], mhalf[:], ALU.pow).then_inc(rstd_done, 1)

                for h in range(2):
                    rstd_of(0, h)
                for o in range(KD):
                    pool.wait_ge(norm_done, o + 1)
                    pool.tensor_tensor(rnorm[:, o:o + 1], norm2[:, o:o + 1], mhalf[:], ALU.pow).then_inc(rnorm_done, 1)
                with pool.Fori(1, B) as b:
                    for h in range(2):
                        rstd_of(b, h)

            @block.scalar
            def _(act):
                def normed(b, h):
                    act.wait_ge(T_mm[h], b + FIRST)
                    act.wait_ge(nmr_done, 2 * b + h + 1)
                    settle(act)
                    act.activation(xn[h][:], X[:, 2 * b + h, :], ACT.Identity, scale=rstd[h][:], bias=nmr[h][:]).then_inc(xn_done, 1)

                def high(b, h):
                    act.wait_ge(out_mm[h], 2 * b + FIRST)
                    act.wait_ge(T_mm[h], b + 1 + FIRST)
                    act.activation(x_hi[h][:], psT[h][:], ACT.Copy, scale=LN_SCALE).then_inc(hi_done, 1)

                for h in range(2):
                    normed(0, h)
                for o in range(KD + 3):
                    if o >= 3:
                        act.wait_ge(wT_mm, o - 2)
                        act.activation(w_hi[:, :, (o - 3) * P:(o - 2) * P], psT[(o - 3) % 2][:].rearrange("p (k t) -> p k t", k=KD),
                                       ACT.Copy, scale=W_SCALE).then_inc(whi_done, 1)
                    if o < KD:
                        act.wait_ge(E_done, o + 1)
                        if o:
                            act.wait_ge(norm_done, o)
                        act.activation(sq[:], E[:, o, :], ACT.Square, accum_out=norm2[:, o:o + 1]).then_inc(norm_done, 1)

                def batch(b, more):
                    for h in range(2):
                        if more or h == 0:
                            high(*following(b, h, 1))
                        if more:
                            normed(*following(b, h, 2))

                high(0, 0)
                with act.Fori(0, B - 1) as b:
                    batch(b, True)
                batch(B - 1, False)

            @block.tensor
            def _(pe):
                for used in (*T_mm, *out_mm):
                    pe.sem_inc(used, FIRST)
                pe.wait_ge(w_in, 64)
                for o in range(KD + 2):
                    if o < KD:
                        if o >= 2:
                            pe.wait_ge(E_done, o - 1)
                        for n in range(2):
                            mm = pe.matmul(psO[o % 2][:, n * BANK:(n + 1) * BANK], lb[:, o * P:(o + 1) * P], la[:, n * BANK:(n + 1) * BANK], start=True, stop=True)
                        mm.then_inc(lora_mm, 1)
                    if o >= 2:
                        pe.wait_ge(scaled, o - 1)
                        if o >= 4:
                            pe.wait_ge(wlo_done, o - 3)
                        for k in range(KD):
                            mm = pe.transpose(psT[o % 2][:, k * P:(k + 1) * P], E[:, o - 2, k * P:(k + 1) * P], ident[:])
                        mm.then_inc(wT_mm, 1)
                pe.wait_ge(E_done, KD)
                pe.wait_ge(gain_done, 1)
                for o in range(KD):
                    mm = pe.matmul(psO[1][:, o * P:(o + 1) * P], gain[:, o:o + 1].to_broadcast([P, P]), ident[:], start=True, stop=True)
                mm.then_inc(row_mm, 1)

                def turn(b, h):
                    pe.wait_ge(xn_done, 2 * b + h + 1)
                    pe.wait_ge(lo_done[h], b + FIRST)
                    for k in range(KD):
                        mm = pe.transpose(psT[h][:, k * P:(k + 1) * P], xn[h][:, k * P:(k + 1) * P], ident[:])
                    mm.then_inc(T_mm[h], 1)

                def linear(b, h):
                    pe.wait_ge(lo_done[h], b + 1 + FIRST)
                    pe.wait_ge(prod_done[h], 2 * b + FIRST)
                    for n in range(2):
                        cols = slice(n * BANK, (n + 1) * BANK)
                        q = 0
                        for k in range(KD):
                            ks = slice(k * P, (k + 1) * P)
                            for a, w in ((x_hi, w_hi), (x_hi, w_lo), (x_lo, w_hi)):
                                mm = pe.matmul(psO[h][:, cols], a[h][:, ks], w[:, k, cols], start=(q == 0), stop=(q == 3 * KD - 1))
                                q += 1
                        mm.then_inc(out_mm[h], 1)

                def batch(b, more):
                    for h in range(2):
                        if more or h == 0:
                            turn(*following(b, h, 1))
                        linear(b, h)

                pe.wait_ge(wlo_done, KD)
                turn(0, 0)
                pe.wait_ge(row_done, 1)
                with pe.Fori(0, B - 1) as b:
                    batch(b, True)
                batch(B - 1, False)

            @block.vector
            def _(dve):
                for used in (*lo_done, *prod_done):
                    dve.sem_inc(used, FIRST)

                def stats(b, h):
                    settle(dve)
                    for n in range(2):
                        dve.bn_stats(st[h][:, 6 * n:6 * n + 6], X[:, 2 * b + h, n * BANK:(n + 1) * BANK]).then_inc(stats_done, 1)
                    dve.wait_ge(stats_done, 4 * b + 2 * h + 2)
                    settle(dve)
                    dve.bn_aggr(mv[h][:], st[h][:]).then_inc(mv_done, 1)
                    dve.wait_ge(rstd_done, 2 * b + h + 1)
                    dve.scalar_tensor_tensor(nmr[h][:], mv[h][:, 0:1], -1.0, rstd[h][:], ALU.mult, ALU.mult).then_inc(nmr_done, 1)

                def low(b, h):
                    dve.wait_ge(hi_done, 2 * b + h + 1)
                    dve.scalar_tensor_tensor(x_lo[h][:], psT[h][:], LN_SCALE, x_hi[h][:], ALU.mult, ALU.subtract).then_inc(lo_done[h], 1)

                def add(b, h):
                    for n in range(2):
                        cols = slice(n * BANK, (n + 1) * BANK)
                        dve.wait_ge(out_mm[h], 2 * b + n + 1 + FIRST)
                        dve.tensor_tensor(prod[h][:, cols], psO[h][:, cols], gain_row[:, cols], ALU.mult).then_inc(prod_done[h], 1)
                    for n in range(2):
                        cols = slice(n * BANK, (n + 1) * BANK)
                        dve.wait_ge(prod_done[h], 2 * b + n + 1 + FIRST)
                        dve.tensor_tensor(X[:, 2 * b + h, cols], X[:, 2 * b + h, cols], prod[h][:, cols], ALU.add).then_inc(x_done[h], 1)

                for h in range(2):
                    stats(0, h)
                dve.wait_ge(w_in, 64)
                dve.tensor_scalar(gain[:], mag[:], tg[:, 3:4], 1.0 / (W_SCALE * LN_SCALE), ALU.mult, ALU.mult).then_inc(gain_done, 1)
                for o in range(KD + 4):
                    if o >= 4:
                        dve.wait_ge(whi_done, o - 3)
                        cols = slice((o - 4) * P, (o - 3) * P)
                        dve.scalar_tensor_tensor(w_lo[:, :, cols], psT[(o - 4) % 2][:].rearrange("p (k t) -> p k t", k=KD), W_SCALE,
                                                 w_hi[:, :, cols], ALU.mult, ALU.subtract).then_inc(wlo_done, 1)
                    if o < KD:
                        dve.wait_ge(lora_mm, o + 1)
                        dve.tensor_tensor(E[:, o, :], E[:, o, :], psO[o % 2][:], ALU.add).then_inc(E_done, 1)
                    if 1 <= o <= KD:
                        dve.wait_ge(rnorm_done, o)
                        dve.tensor_scalar(E[:, o - 1, :], E[:, o - 1, :], rnorm[:, o - 1:o], None, ALU.mult).then_inc(scaled, 1)
                dve.wait_ge(row_mm, 1)
                dve.tensor_copy(gain_row[:], psO[1][:]).then_inc(row_done, 1)

                def batch(b, more):
                    for h in range(2):
                        if more or h == 0:
                            low(*following(b, h, 1))
                        if more:
                            stats(*following(b, h, 2))
                        add(b, h)

                low(0, 0)
                dve.wait_ge(row_done, 1)
                with dve.Fori(0, B - 1) as b:
                    batch(b, True)
                batch(B - 1, False)


def build(nc, io):
    with ExitStack() as ctx:
        def sb(name, shape, dt=F32):
            return ctx.enter_context(nc.sbuf_tensor(name, shape, dt))
        res = {"X": sb("X", [P, TILES, D]), "ident": sb("ident", [P, P]), "blk": sb("blk", [P, P]),
               "tg": sb("tg", [P, 4]), "gates": sb("gates", [P, 4]), "mhalf": sb("mhalf", [P, 1]), "half": sb("half", [P, 1]), "ones": sb("ones", [P, P])}
        res["passed"] = ctx.enter_context(nc.semaphore("passed"))
        res["stored"] = ctx.enter_context(nc.semaphore("stored"))
        for name, n in (("w_scale", 3), ("ab_scale", 2), ("lora_gain", 3), ("hid_gain", 1), ("ffn_gain", 1)):
            res[name] = sb(name, [P, n])
        res["xT_hi"] = sb("xT_hi", [P, KD, B * L], HALF)
        place, start = res["xT_hi"][:].rearrange("p k t -> p (k t)"), 0
        for name, shape, dt in (("ctx_in0", [2, D], F32), ("ctx_in1", [2, D], F32), ("fwd", [2, 2, 2, P], F32), ("inv", [4, L], F32),
                                ("fwd_hi", [2, 2, 2, P], HALF), ("fwd_lo", [2, 2, 2, P], HALF), ("wT_hi", [2, BANK], HALF), ("wT_lo", [2, BANK], HALF)):
            size = int(np.prod(shape)) * (2 if dt is F32 else 1)
            part = place[:, start:start + size]
            part = part.bitcast(F32) if dt is F32 else part
            dims = "abcd"[:len(shape)]
            res[name] = part.rearrange(f"p ({' '.join(dims)}) -> p {' '.join(dims)}", **dict(zip(dims[1:], shape[1:])))
            start += size
        res["const_in"] = ctx.enter_context(nc.semaphore("a_const_in"))
        res["ctx_in"] = [ctx.enter_context(nc.semaphore(f"a_ctx_in{s}")) for s in range(2)]
        with ExitStack() as inner:
            res["xT_lo"] = inner.enter_context(nc.sbuf_tensor("xT_lo", [P, KD, B * L], HALF))
            phase_linear_attention(nc, io, res)
            phase_nf4_ffn(nc, io, res)
        for name, shape in (("lora1_a", [P, D]), ("lora1_b", [P, D]), ("mag", [P, KD]), ("w1", [P, KD, D])):
            res[name] = sb(name, shape)
        res["w1_in"] = ctx.enter_context(nc.semaphore("w1_in"))
        phase_autocorrelation(nc, io, res)
        phase_dora_linear(nc, io, res)


def layouts(inputs):
    a = {k: np.asarray(v) for k, v in inputs.items()}
    padf = DFF_PAD - DFF
    kk = KD // 2
    units = pack_units()
    codes = np.zeros((PAIRS, UNITS, P, BANK), np.int32)
    absmax = np.zeros((PAIRS, UNITS, 2, BANK), np.float32)
    gate_up, absmax_of = [], []
    for m in ("g", "u"):
        c = np.pad(a[f"L0_ffn_{m}_codes"], ((0, padf), (0, 0)))
        s = np.pad(a[f"L0_ffn_{m}_absmax"], ((0, padf), (0, 0)))
        absmax_of.append(s.copy())
        if m == "g":
            c[DFF:], s[DFF:] = a["L0_ffn_u_codes"][DFF - LAST:], a["L0_ffn_u_absmax"][DFF - LAST:]
        gate_up.append((c.reshape(PAIRS, 2, P, 2, kk, P), s.reshape(PAIRS, 2, P, 2, kk, 2)))
    def rows_last(t, last):
        return np.concatenate([t[:, :-last], np.zeros_like(t[:, :last]), t[:, -last:]], 1)

    dc = rows_last(a["L0_ffn_d_codes"], LAST).reshape(2, BANK, PAIRS, 2, P)
    ds = rows_last(a["L0_ffn_d_absmax"], LAST // QBLK).reshape(2, BANK, PAIRS, 2, 2)
    for u, (m, c, hf) in enumerate(units):
        if m < 2:
            cc, ss = gate_up[m]
            codes[:, u] = cc[:, c, :, hf].transpose(0, 3, 2, 1).reshape(PAIRS, P, BANK)
            absmax[:, u] = ss[:, c, :, hf].transpose(0, 3, 2, 1).reshape(PAIRS, 2, BANK)
        else:
            codes[:, u] = dc[hf, :, :, c].transpose(1, 2, 0)
            absmax[:, u] = ds[hf, :, :, c].transpose(1, 2, 0)
    lora_a = np.zeros((96, 3, D), np.float32)
    lora_b = np.zeros((PAIRS, 96, 3, PAIR), np.float32)
    bound_a, bound_b = np.zeros((P, 3, KD, R0), np.float32), np.zeros((P, 3, DFF_PAD // P, R0), np.float32)
    for m, name in enumerate(("g", "u", "d")):
        la, lb = a[f"L0_ffn_{name}_lora_a"], a[f"L0_ffn_{name}_lora_b"]
        wide, long = (la.T, lb) if m < 2 else (lb, la.T)
        long = rows_last(long, LAST) if m == 2 else np.pad(long, ((0, 0), (0, padf)))
        bound_a[:, m] = wide.T.reshape(KD, P, R0).transpose(1, 0, 2)
        bound_b[:, m] = long.T.reshape(-1, P, R0).transpose(1, 0, 2)
        long = long.reshape(R0, PAIRS, PAIR).transpose(1, 0, 2)
        for g in range(3):
            lora_a[32 * g:32 * g + R0, m] = wide
            lora_b[:, 32 * g:32 * g + R0, m] = long
            if m == 1:
                lora_a[32 * g + R0:32 * g + 2 * R0, 0] = wide
                lora_b[-1, 32 * g + R0:32 * g + 2 * R0, 0, PAIR - LAST:] = a["L0_ffn_u_lora_b"][:, DFF - LAST:]
    bound_q = np.stack([s.reshape(P, -1) for s in (*absmax_of, np.pad(a["L0_ffn_d_absmax"], ((0, 0), (0, padf // QBLK))))], 1)
    fwd, fwd_hi, fwd_lo, inv = spectra()
    lora1_a, lora1_b = np.zeros((P, D), np.float32), np.zeros((P, D), np.float32)
    lora1_a[:R1], lora1_b[:R1] = a["L1_ffn_lora_A"], a["L1_ffn_lora_B"].T
    arrays = {
        "bound_q": bound_q, "bound_a": bound_a, "bound_b": bound_b,
        "lora1_a": lora1_a, "lora1_b": lora1_b, "mag": a["L1_ffn_magnitude"].reshape(KD, P).T,
        "w1": a["L1_ffn_W"].reshape(KD, P, D).transpose(1, 0, 2),
        "fwd": fwd, "fwd_hi": fwd_hi, "fwd_lo": fwd_lo, "inv": inv,
        "x": a["x"], "ctx": a["ctx_4096"],
        "ctxT": a["ctx_4096"].reshape(B, 2, P, KD, P).transpose(0, 1, 4, 3, 2).reshape(B, 2, P, D), "g_xattn": a["g_xattn"], "g_ffn": a["g_ffn"],
        "ident": np.eye(P, dtype=np.float32), "blk": np.kron(np.eye(P // ROWS0), np.ones((ROWS0, ROWS0))).astype(np.float32),
        "codes": codes, "absmax": absmax, "lora_a": lora_a, "lora_b": lora_b,
    }
    return {k: np.ascontiguousarray(v) for k, v in arrays.items()}


def kernel(**inputs):
    import concourse.bacc as bacc
    from concourse.bass_utils import run_bass_kernel_spmd

    nc = bacc.Bacc("TRN2", target_bir_lowering=False, num_devices=1, dynamic_dma_scratch_size=2048)
    arrays, io = {}, {}
    for name, arr in layouts(inputs).items():
        arrays[f"in_{name}"] = arr
        io[name] = nc.dram_tensor(f"in_{name}", arr.shape, mybir.dt.from_np(arr.dtype), kind="ExternalInput").ap()
    io["out"] = nc.dram_tensor("out_0", (B, L, D), F32, kind="ExternalOutput").ap()
    build(nc, io)
    r = run_bass_kernel_spmd(nc, [arrays], core_ids=[0])
    return r.results[0]["out_0"]
```
